# Optimizing a Trainium2 kernel written in Bass

```python
import numpy as np
import jax
import jax.numpy as jnp

def _softmax(x, axis=-1):
    return jax.nn.softmax(x, axis=axis)

def _gelu(x):
    return jax.nn.gelu(x, approximate=True)

def _silu(x):
    return jax.nn.silu(x)

def _sigmoid(x):
    return jax.nn.sigmoid(x)

def _layernorm(x, axis=-1, eps=1e-05):
    m = jnp.mean(x, axis=axis, keepdims=True)
    v = jnp.var(x, axis=axis, keepdims=True)
    return (x - m) / jnp.sqrt(v + eps)

def _scatter_add(tgt, idx, src, axis=0):
    return tgt.at[idx].add(src)

def _segment_sum(src, seg, n):
    return jax.ops.segment_sum(src, seg, n)
kernel_name = 'mk_perceiver_d4_seqx_r8_a6d029'

def setup_inputs(seed: int=0):
    np.random.seed(seed)
    _w = jnp.asarray

    def _rec_inputs():
        import jax
        import jax.numpy as jnp
        _rk = jax.random.key(seed)
        x = 0.0002417 + 0.9998 * jax.random.normal(jax.random.fold_in(_rk, 1), (32, 32, 128), jnp.float32)
        _lenS = 32 - jax.random.randint(jax.random.fold_in(_rk, 7), (32,), 0, max(1, 32 // 4) + 1, jnp.int32)
        _lenS2 = 257 - jax.random.randint(jax.random.fold_in(_rk, 8), (32,), 0, max(1, 257 // 4) + 1, jnp.int32)
        _ctx_1024P = jax.random.normal(jax.random.fold_in(_rk, 11), (32, 16, 128), jnp.float32)
        _ctx_1024c = jax.random.dirichlet(jax.random.fold_in(_rk, 511), 0.3 * jnp.ones((16,), jnp.float32), (32, 257))
        _ctx_1024t = jnp.einsum('bsk,bkd->bsd', _ctx_1024c, _ctx_1024P)
        _ctx_1024t = _ctx_1024t * jax.lax.rsqrt(jnp.mean(jnp.square(_ctx_1024t)) + 1e-12) * 0.953939
        ctx_1024 = 7.22013e-05 + 1.00017 * (_ctx_1024t + 0.3 * jax.random.normal(jax.random.fold_in(_rk, 611), (32, 257, 128), jnp.float32))
        fside_Bx16xSxS2_0 = -6.00028e-06 + 0.100001 * jax.random.normal(jax.random.fold_in(_rk, 13), (32, 16, 32, 257), jnp.float32)
        _validS = jnp.arange(32)[None, :] < _lenS[:, None]
        _validS2 = jnp.arange(257)[None, :] < _lenS2[:, None]
        _causal = jnp.tril(jnp.ones((32, 32), dtype=bool))
        mask_BxS2_bk1 = jnp.broadcast_to(_validS2[:, :], (32, 257))
        return (x, ctx_1024, fside_Bx16xSxS2_0, mask_BxS2_bk1)
    x, ctx_1024, fside_Bx16xSxS2_0, mask_BxS2_bk1 = _rec_inputs()

    def _L0_xattn_setup():
        import jax, jax.numpy as jnp
        import numpy as np
        D_MODEL = 128
        B, S = (4, 256)
        key = jax.random.key(seed)
        ks = jax.random.split(key, 10)
        s = 1.0 / np.sqrt(D_MODEL)
        return {'k': jax.random.normal(ks[0], (B, S, D_MODEL), jnp.float32), 'v': jax.random.normal(ks[1], (B, S, D_MODEL), jnp.float32), 'q': jax.random.normal(ks[2], (B, S, D_MODEL), jnp.float32), 'Wk': jax.random.normal(ks[3], (D_MODEL, D_MODEL), jnp.float32) * s, 'Wv': jax.random.normal(ks[4], (D_MODEL, D_MODEL), jnp.float32) * s, 'bv': jnp.zeros((D_MODEL,), jnp.float32), 'Wq': jax.random.normal(ks[5], (D_MODEL, D_MODEL), jnp.float32) * s, 'bq': jnp.zeros((D_MODEL,), jnp.float32), 'Wo': jax.random.normal(ks[6], (D_MODEL, D_MODEL), jnp.float32) * s, 'bo': jnp.zeros((D_MODEL,), jnp.float32)}
    _L0_xattn_all = _L0_xattn_setup()
    _L0_xattn_in = {k: v for k, v in _L0_xattn_all.items() if k in ('Wk', 'Wv', 'bv', 'Wq', 'bq', 'Wo', 'bo')}
    del _L0_xattn_all

    def _L0_attn_setup():
        import jax, jax.numpy as jnp
        import numpy as np
        NUM_HEADS = 16
        B, S, H = (2, 1024, 128)
        key = jax.random.key(seed)
        ks = jax.random.split(key, 6)
        scale = 1.0 / np.sqrt(H)
        return {'hidden_states': jax.random.normal(ks[0], (B, S, H), dtype=jnp.float32), 'Wq': jax.random.normal(ks[1], (H, H), dtype=jnp.float32) * scale, 'Wk': jax.random.normal(ks[2], (H, H), dtype=jnp.float32) * scale, 'Wv': jax.random.normal(ks[3], (H, H), dtype=jnp.float32) * scale, 'Wg': jax.random.normal(ks[4], (H, H), dtype=jnp.float32) * scale, 'Wo': jax.random.normal(ks[5], (H, H), dtype=jnp.float32) * scale, 'gamma': jnp.ones((H,), dtype=jnp.float32), 'beta': jnp.zeros((H,), dtype=jnp.float32)}
    _L0_attn_all = _L0_attn_setup()
    _L0_attn_in = {k: v for k, v in _L0_attn_all.items() if k in ('Wq', 'Wk', 'Wv', 'Wg', 'Wo', 'gamma', 'beta')}
    del _L0_attn_all

    def _L0_ffn_setup():
        import jax, jax.numpy as jnp
        import numpy as np
        D_MODEL, FF_DIM = (128, 256)
        N_SHARED, N_ROUTED, TOP_K = (1, 8, 2)
        BATCH, SEQ = (2, 256)
        key = jax.random.key(seed)
        ks = jax.random.split(key, 8)
        init = lambda k, shape: jax.random.normal(k, shape, jnp.float32) * 0.02
        x = jax.random.normal(ks[0], (BATCH, SEQ, D_MODEL), jnp.float32)
        Wg = init(ks[1], (D_MODEL, N_ROUTED))
        Ws1 = init(ks[2], (D_MODEL, FF_DIM))
        Ws3 = init(ks[3], (D_MODEL, FF_DIM))
        Ws2 = init(ks[4], (FF_DIM, D_MODEL))
        We1 = init(ks[5], (N_ROUTED, D_MODEL, FF_DIM))
        We3 = init(ks[6], (N_ROUTED, D_MODEL, FF_DIM))
        We2 = init(ks[7], (N_ROUTED, FF_DIM, D_MODEL))
        return {'x': x, 'Wg': Wg, 'Ws1': Ws1, 'Ws3': Ws3, 'Ws2': Ws2, 'We1': We1, 'We3': We3, 'We2': We2}
    _L0_ffn_all = _L0_ffn_setup()
    _L0_ffn_in = {k: v for k, v in _L0_ffn_all.items() if k in ('Wg', 'Ws1', 'Ws3', 'Ws2', 'We1', 'We3', 'We2')}
    del _L0_ffn_all

    def _L1_xattn_setup():
        import jax, jax.numpy as jnp
        import numpy as np
        B, N, M = (4, 128, 512)
        DQ, DC = (128, 128)
        H, DH = (16, 64)
        INNER = H * DH
        SCALE = DH ** (-0.5)
        key = jax.random.key(seed)
        ks = jax.random.split(key, 6)
        x = jax.random.normal(ks[0], (B, N, DQ), dtype=jnp.float32)
        context = jax.random.normal(ks[1], (B, M, DC), dtype=jnp.float32)
        mask = jax.random.bernoulli(ks[2], 0.9, (B, M))
        Wq = jax.random.normal(ks[3], (DQ, INNER), dtype=jnp.float32) / np.sqrt(DQ)
        Wkv = jax.random.normal(ks[4], (DC, 2 * INNER), dtype=jnp.float32) / np.sqrt(DC)
        Wo = jax.random.normal(ks[5], (INNER, DQ), dtype=jnp.float32) / np.sqrt(INNER)
        bo = jnp.zeros((DQ,), dtype=jnp.float32)
        return {'x': x, 'context': context, 'mask': mask, 'Wq': Wq, 'Wkv': Wkv, 'Wo': Wo, 'bo': bo}
    _L1_xattn_all = _L1_xattn_setup()
    _L1_xattn_in = {k: v for k, v in _L1_xattn_all.items() if k in ('Wq', 'Wkv', 'Wo', 'bo')}
    del _L1_xattn_all

    def _L1_attn_setup():
        import jax, jax.numpy as jnp
        import numpy as np
        B, S, DIN, DIM = (1, 512, 128, 128)
        NH, NKV = (16, 4)
        HD = DIM // NH
        GS = NH // NKV
        key = jax.random.key(seed)
        ks = jax.random.split(key, 5)

        def w(k, shape, fan_in):
            return jax.random.normal(k, shape, jnp.float32) * fan_in ** (-0.5)
        return {'x': jax.random.normal(ks[0], (B, S, DIN), jnp.float32), 'wq': w(ks[1], (DIM, DIN), DIN), 'wk': w(ks[2], (NKV * HD, DIN), DIN), 'wv': w(ks[3], (NKV * HD, DIN), DIN), 'wo': w(ks[4], (DIM, DIM), DIM)}
    _L1_attn_all = _L1_attn_setup()
    _L1_attn_in = {k: v for k, v in _L1_attn_all.items() if k in ('wq', 'wk', 'wv', 'wo')}
    del _L1_attn_all

    def _L1_ffn_setup():
        import jax, jax.numpy as jnp
        import numpy as np
        D_MODEL = 128
        E = 4
        MIN_E = 1
        TH_LO = 0.5
        TH_HI = 2.0
        key = jax.random.key(seed)
        ks = jax.random.split(key, 12)
        B, N, D, H = (4, 256, D_MODEL, 2 * D_MODEL)
        s = 0.02
        return {'x': jax.random.normal(ks[0], (B, N, D), dtype=jnp.float32), 'gate_w': jax.random.normal(ks[1], (D, E), dtype=jnp.float32) * s, 'gate_b': jnp.zeros((E,), dtype=jnp.float32), 'dp_w1': jax.random.normal(ks[2], (D, D // 2), dtype=jnp.float32) * s, 'dp_b1': jnp.zeros((D // 2,), dtype=jnp.float32), 'dp_w2': jax.random.normal(ks[3], (D // 2, 1), dtype=jnp.float32) * s, 'dp_b2': jnp.zeros((1,), dtype=jnp.float32), 'ew1': jax.random.normal(ks[4], (E, D, H), dtype=jnp.float32) * s, 'eb1': jnp.zeros((E, H), dtype=jnp.float32), 'ew2': jax.random.normal(ks[5], (E, H, D), dtype=jnp.float32) * s, 'eb2': jnp.zeros((E, D), dtype=jnp.float32)}
    _L1_ffn_all = _L1_ffn_setup()
    _L1_ffn_in = {k: v for k, v in _L1_ffn_all.items() if k in ('gate_w', 'gate_b', 'dp_w1', 'dp_b1', 'dp_w2', 'dp_b2', 'ew1', 'eb1', 'ew2', 'eb2')}
    del _L1_ffn_all

    def _L2_xattn_setup():
        import jax, jax.numpy as jnp
        import numpy as np
        import math
        H = 16
        D = 128
        FF = 512
        DK = D // H
        EPS = 1e-05

        def layer_norm(x, g, b):
            mu = jnp.mean(x, axis=-1, keepdims=True)
            var = jnp.var(x, axis=-1, keepdims=True)
            return (x - mu) * jax.lax.rsqrt(var + EPS) * g + b
        key = jax.random.key(seed)
        ks = jax.random.split(key, 16)
        B, S = (2, 256)
        s = 1.0 / math.sqrt(D)
        return {'x_q': jax.random.normal(ks[0], (B, S, D), jnp.float32), 'x_kv': jax.random.normal(ks[1], (B, S, D), jnp.float32), 'bias': jax.random.normal(ks[2], (B, H, S, S), jnp.float32) * 0.1, 'Wq': jax.random.normal(ks[3], (D, D), jnp.float32) * s, 'Wk': jax.random.normal(ks[4], (D, D), jnp.float32) * s, 'Wv': jax.random.normal(ks[5], (D, D), jnp.float32) * s, 'Wo': jax.random.normal(ks[6], (D, D), jnp.float32) * s, 'W1': jax.random.normal(ks[7], (FF, D), jnp.float32) * s, 'b1': jnp.zeros((FF,), jnp.float32), 'W2': jax.random.normal(ks[8], (D, FF), jnp.float32) * (1.0 / math.sqrt(FF)), 'b2': jnp.zeros((D,), jnp.float32), 'g1': jnp.ones((D,), jnp.float32), 'be1': jnp.zeros((D,), jnp.float32), 'g2': jnp.ones((D,), jnp.float32), 'be2': jnp.zeros((D,), jnp.float32)}
    _L2_xattn_all = _L2_xattn_setup()
    _L2_xattn_in = {k: v for k, v in _L2_xattn_all.items() if k in ('Wq', 'Wk', 'Wv', 'Wo', 'W1', 'b1', 'W2', 'b2', 'g1', 'be1', 'g2', 'be2')}
    del _L2_xattn_all

    def _L2_attn_setup():
        import math
        import jax, jax.numpy as jnp
        import numpy as np
        D_HIDDEN = 128
        NB_HEADS = 16
        NUM_BUCKETS = 32
        MAX_DISTANCE = 128
        B, L = (2, 128)

        def _relative_position_bucket(relative_position, num_buckets=NUM_BUCKETS, max_distance=MAX_DISTANCE):
            n = -relative_position
            num_buckets = num_buckets // 2
            ret = (n < 0).astype(jnp.int32) * num_buckets
            n = jnp.abs(n)
            max_exact = num_buckets // 2
            is_small = n < max_exact
            val_if_large = max_exact + (jnp.log(jnp.maximum(n, 1).astype(jnp.float32) / max_exact) / math.log(max_distance / max_exact) * (num_buckets - max_exact)).astype(jnp.int32)
            val_if_large = jnp.minimum(val_if_large, num_buckets - 1)
            return ret + jnp.where(is_small, n, val_if_large)

        def layer_normalize(p):
            mean = jnp.mean(p, axis=-1, keepdims=True)
            st_dev = jnp.sqrt(jnp.mean((p - mean) ** 2, axis=-1, keepdims=True))
            return (p - mean) / st_dev

        def _encoder_block(x, Wq, bq, Wk, bk, Wv, bv, Wo, bo, rel_bias, W1, b1, W2, b2):
            d_batch, q_len, d = x.shape
            d_head = d // NB_HEADS
            q = x @ Wq.T + bq
            k = x @ Wk.T + bk
            v = x @ Wv.T + bv
            qm = q.reshape(d_batch * NB_HEADS, q_len, d_head)
            km = k.reshape(d_batch * NB_HEADS, q_len, d_head)
            vm = v.reshape(d_batch * NB_HEADS, q_len, d_head)
            att = jnp.einsum('nqd,nkd->nqk', qm, km)
            att = jax.nn.softmax(att, axis=-1)
            rel_pos = jnp.arange(q_len)[:, None] - jnp.arange(q_len)[None, :]
            buckets = _relative_position_bucket(rel_pos)
            single = rel_bias[buckets]
            batch_pos = jnp.transpose(jnp.tile(single, (1, 1, d_batch)), (2, 0, 1))
            att_out = jnp.einsum('nqk,nkd->nqd', att + batch_pos, vm)
            att_out = att_out.reshape(d_batch, q_len, d) @ Wo.T + bo
            att_block = layer_normalize(att_out + x)
            ff = (att_block @ W1.T + b1) @ W2.T + b2
            return layer_normalize(ff + att_block)
        key = jax.random.key(seed)
        ks = jax.random.split(key, 16)
        s = 1.0 / math.sqrt(D_HIDDEN)
        return {'x': jax.random.normal(ks[0], (B, L, D_HIDDEN), jnp.float32), 'Wq': jax.random.normal(ks[1], (D_HIDDEN, D_HIDDEN), jnp.float32) * s, 'bq': jax.random.normal(ks[2], (D_HIDDEN,), jnp.float32) * s, 'Wk': jax.random.normal(ks[3], (D_HIDDEN, D_HIDDEN), jnp.float32) * s, 'bk': jax.random.normal(ks[4], (D_HIDDEN,), jnp.float32) * s, 'Wv': jax.random.normal(ks[5], (D_HIDDEN, D_HIDDEN), jnp.float32) * s, 'bv': jax.random.normal(ks[6], (D_HIDDEN,), jnp.float32) * s, 'Wo': jax.random.normal(ks[7], (D_HIDDEN, D_HIDDEN), jnp.float32) * s, 'bo': jax.random.normal(ks[8], (D_HIDDEN,), jnp.float32) * s, 'rel_bias': jax.random.normal(ks[9], (NUM_BUCKETS, NB_HEADS), jnp.float32) * 0.02, 'W1': jax.random.normal(ks[10], (D_HIDDEN, D_HIDDEN), jnp.float32) * s, 'b1': jax.random.normal(ks[11], (D_HIDDEN,), jnp.float32) * s, 'W2': jax.random.normal(ks[12], (D_HIDDEN, D_HIDDEN), jnp.float32) * s, 'b2': jax.random.normal(ks[13], (D_HIDDEN,), jnp.float32) * s}
    _L2_attn_all = _L2_attn_setup()
    _L2_attn_in = {k: v for k, v in _L2_attn_all.items() if k in ('Wq', 'bq', 'Wk', 'bk', 'Wv', 'bv', 'Wo', 'bo', 'rel_bias', 'W1', 'b1', 'W2', 'b2')}
    del _L2_attn_all

    def _L2_ffn_setup():
        import jax, jax.numpy as jnp
        import numpy as np
        B, S, H, F, E, R, TOPK = (4, 256, 128, 512, 4, 4, 2)

        def _more_forward(x, Wg, bg, W1, b1, W2, b2):
            b, s, h = x.shape
            cur = x
            for r in range(R):
                flat = cur.reshape(-1, h)
                logits = flat @ Wg[r] + bg[r]
                vals, idx = jax.lax.top_k(logits, TOPK)
                w = jax.nn.softmax(vals, axis=-1)
                cw = jnp.sum(jax.nn.one_hot(idx, E, dtype=flat.dtype) * w[..., None], axis=1)
                hmid = jax.nn.gelu(jnp.einsum('nh,ehf->enf', flat, W1) + b1[:, None, :])
                y = jnp.einsum('enf,efh->enh', hmid, W2) + b2[:, None, :]
                out = jnp.einsum('ne,enh->nh', cw, y)
                cur = cur + out.reshape(b, s, h)
            return cur
        key = jax.random.key(seed)
        ks = jax.random.split(key, 8)
        scale = 0.02
        return {'x': jax.random.normal(ks[0], (B, S, H), dtype=jnp.float32), 'Wg': jax.random.normal(ks[1], (R, H, E), dtype=jnp.float32) * scale, 'bg': jnp.zeros((R, E), dtype=jnp.float32), 'W1': jax.random.normal(ks[2], (E, H, F), dtype=jnp.float32) * scale, 'b1': jnp.zeros((E, F), dtype=jnp.float32), 'W2': jax.random.normal(ks[3], (E, F, H), dtype=jnp.float32) * scale, 'b2': jnp.zeros((E, H), dtype=jnp.float32)}
    _L2_ffn_all = _L2_ffn_setup()
    _L2_ffn_in = {k: v for k, v in _L2_ffn_all.items() if k in ('Wg', 'bg', 'W1', 'b1', 'W2', 'b2')}
    del _L2_ffn_all

    def _L3_xattn_setup():
        import jax, jax.numpy as jnp
        import numpy as np
        D_MODEL = 128
        H = 16
        D_K = D_MODEL // H
        key = jax.random.key(seed)
        ks = jax.random.split(key, 11)
        B, S = (4, 256)
        scale = 1.0 / np.sqrt(D_MODEL)
        return {'Q': jax.random.normal(ks[0], (B, S, D_MODEL), jnp.float32), 'K': jax.random.normal(ks[1], (B, S, D_MODEL), jnp.float32), 'V': jax.random.normal(ks[2], (B, S, D_MODEL), jnp.float32), 'Wq': jax.random.normal(ks[3], (D_MODEL, D_MODEL), jnp.float32) * scale, 'bq': jnp.zeros((D_MODEL,), jnp.float32), 'Wk': jax.random.normal(ks[4], (D_MODEL, D_MODEL), jnp.float32) * scale, 'bk': jnp.zeros((D_MODEL,), jnp.float32), 'Wv': jax.random.normal(ks[5], (D_MODEL, D_MODEL), jnp.float32) * scale, 'bv': jnp.zeros((D_MODEL,), jnp.float32), 'Wo': jax.random.normal(ks[6], (D_MODEL, D_MODEL), jnp.float32) * scale, 'bo': jnp.zeros((D_MODEL,), jnp.float32)}
    _L3_xattn_all = _L3_xattn_setup()
    _L3_xattn_in = {k: v for k, v in _L3_xattn_all.items() if k in ('Wq', 'bq', 'Wk', 'bk', 'Wv', 'bv', 'Wo', 'bo')}
    del _L3_xattn_all

    def _L3_attn_setup():
        import jax, jax.numpy as jnp
        import numpy as np
        HEADS = 16
        BIAS_STRENGTH = 0.1
        LN_EPS = 1e-05

        def _layernorm(x, gamma, beta):
            mu = jnp.mean(x, axis=-1, keepdims=True)
            var = jnp.mean((x - mu) ** 2, axis=-1, keepdims=True)
            return (x - mu) * jax.lax.rsqrt(var + LN_EPS) * gamma + beta

        def _spatial_bias(spatial_centers, N, dtype):
            diff = spatial_centers[:, None, :] - spatial_centers[None, :, :]
            dist = jnp.sqrt(jnp.sum(diff * diff, axis=-1))
            max_dist = jnp.max(dist)
            core = jnp.where(max_dist > 1e-06, -dist / max_dist, 0.0) * BIAS_STRENGTH
            P = spatial_centers.shape[0]
            bias = jnp.zeros((N, N), dtype=dtype)
            return bias.at[1:P + 1, 1:P + 1].set(core.astype(dtype))
        key = jax.random.key(seed)
        ks = jax.random.split(key, 4)
        B, N, D, P = (2, 256, 128, 128)
        return {'x': jax.random.normal(ks[0], (B, N, D), dtype=jnp.float32), 'W_qkv': jax.random.normal(ks[1], (3 * D, D), dtype=jnp.float32) * D ** (-0.5), 'W_proj': jax.random.normal(ks[2], (D, D), dtype=jnp.float32) * D ** (-0.5), 'b_proj': jnp.zeros((D,), dtype=jnp.float32), 'ln_gamma': jnp.ones((D,), dtype=jnp.float32), 'ln_beta': jnp.zeros((D,), dtype=jnp.float32), 'spatial_centers': jax.random.uniform(ks[3], (P, 2), dtype=jnp.float32)}
    _L3_attn_all = _L3_attn_setup()
    _L3_attn_in = {k: v for k, v in _L3_attn_all.items() if k in ('W_qkv', 'W_proj', 'b_proj', 'ln_gamma', 'ln_beta', 'spatial_centers')}
    del _L3_attn_all

    def _L3_ffn_setup():
        import jax, jax.numpy as jnp
        import numpy as np
        D_MODEL, D_FF, RANK = (128, 512, 32)
        B, S = (4, 512)
        key = jax.random.key(seed)
        ks = jax.random.split(key, 7)
        return {'x': jax.random.normal(ks[0], (B, S, D_MODEL), dtype=jnp.float32), 'U1': jax.random.normal(ks[1], (D_MODEL, RANK), dtype=jnp.float32) * 0.02, 'V1': jax.random.normal(ks[2], (RANK, D_FF), dtype=jnp.float32) * 0.02, 'b1': jnp.zeros((D_FF,), dtype=jnp.float32), 'U2': jax.random.normal(ks[3], (D_FF, RANK), dtype=jnp.float32) * 0.02, 'V2': jax.random.normal(ks[4], (RANK, D_MODEL), dtype=jnp.float32) * 0.02, 'b2': jnp.zeros((D_MODEL,), dtype=jnp.float32)}
    _L3_ffn_all = _L3_ffn_setup()
    _L3_ffn_in = {k: v for k, v in _L3_ffn_all.items() if k in ('U1', 'V1', 'b1', 'U2', 'V2', 'b2')}
    del _L3_ffn_all
    return {'x': x, 'ctx_1024': ctx_1024, 'fside_Bx16xSxS2_0': fside_Bx16xSxS2_0, 'mask_BxS2_bk1': mask_BxS2_bk1, 'L0_xattn_Wk': _L0_xattn_in['Wk'], 'L0_xattn_Wv': _L0_xattn_in['Wv'], 'L0_xattn_bv': _L0_xattn_in['bv'], 'L0_xattn_Wq': _L0_xattn_in['Wq'], 'L0_xattn_bq': _L0_xattn_in['bq'], 'L0_xattn_Wo': _L0_xattn_in['Wo'], 'L0_xattn_bo': _L0_xattn_in['bo'], 'L0_attn_Wq': _L0_attn_in['Wq'], 'L0_attn_Wk': _L0_attn_in['Wk'], 'L0_attn_Wv': _L0_attn_in['Wv'], 'L0_attn_Wg': _L0_attn_in['Wg'], 'L0_attn_Wo': _L0_attn_in['Wo'], 'L0_attn_gamma': _L0_attn_in['gamma'], 'L0_attn_beta': _L0_attn_in['beta'], 'L0_ffn_Wg': _L0_ffn_in['Wg'], 'L0_ffn_Ws1': _L0_ffn_in['Ws1'], 'L0_ffn_Ws3': _L0_ffn_in['Ws3'], 'L0_ffn_Ws2': _L0_ffn_in['Ws2'], 'L0_ffn_We1': _L0_ffn_in['We1'], 'L0_ffn_We3': _L0_ffn_in['We3'], 'L0_ffn_We2': _L0_ffn_in['We2'], 'L1_xattn_Wq': _L1_xattn_in['Wq'], 'L1_xattn_Wkv': _L1_xattn_in['Wkv'], 'L1_xattn_Wo': _L1_xattn_in['Wo'], 'L1_xattn_bo': _L1_xattn_in['bo'], 'L1_attn_wq': _L1_attn_in['wq'], 'L1_attn_wk': _L1_attn_in['wk'], 'L1_attn_wv': _L1_attn_in['wv'], 'L1_attn_wo': _L1_attn_in['wo'], 'L1_ffn_gate_w': _L1_ffn_in['gate_w'], 'L1_ffn_gate_b': _L1_ffn_in['gate_b'], 'L1_ffn_dp_w1': _L1_ffn_in['dp_w1'], 'L1_ffn_dp_b1': _L1_ffn_in['dp_b1'], 'L1_ffn_dp_w2': _L1_ffn_in['dp_w2'], 'L1_ffn_dp_b2': _L1_ffn_in['dp_b2'], 'L1_ffn_ew1': _L1_ffn_in['ew1'], 'L1_ffn_eb1': _L1_ffn_in['eb1'], 'L1_ffn_ew2': _L1_ffn_in['ew2'], 'L1_ffn_eb2': _L1_ffn_in['eb2'], 'L2_xattn_Wq': _L2_xattn_in['Wq'], 'L2_xattn_Wk': _L2_xattn_in['Wk'], 'L2_xattn_Wv': _L2_xattn_in['Wv'], 'L2_xattn_Wo': _L2_xattn_in['Wo'], 'L2_xattn_W1': _L2_xattn_in['W1'], 'L2_xattn_b1': _L2_xattn_in['b1'], 'L2_xattn_W2': _L2_xattn_in['W2'], 'L2_xattn_b2': _L2_xattn_in['b2'], 'L2_xattn_g1': _L2_xattn_in['g1'], 'L2_xattn_be1': _L2_xattn_in['be1'], 'L2_xattn_g2': _L2_xattn_in['g2'], 'L2_xattn_be2': _L2_xattn_in['be2'], 'L2_attn_Wq': _L2_attn_in['Wq'], 'L2_attn_bq': _L2_attn_in['bq'], 'L2_attn_Wk': _L2_attn_in['Wk'], 'L2_attn_bk': _L2_attn_in['bk'], 'L2_attn_Wv': _L2_attn_in['Wv'], 'L2_attn_bv': _L2_attn_in['bv'], 'L2_attn_Wo': _L2_attn_in['Wo'], 'L2_attn_bo': _L2_attn_in['bo'], 'L2_attn_rel_bias': _L2_attn_in['rel_bias'], 'L2_attn_W1': _L2_attn_in['W1'], 'L2_attn_b1': _L2_attn_in['b1'], 'L2_attn_W2': _L2_attn_in['W2'], 'L2_attn_b2': _L2_attn_in['b2'], 'L2_ffn_Wg': _L2_ffn_in['Wg'], 'L2_ffn_bg': _L2_ffn_in['bg'], 'L2_ffn_W1': _L2_ffn_in['W1'], 'L2_ffn_b1': _L2_ffn_in['b1'], 'L2_ffn_W2': _L2_ffn_in['W2'], 'L2_ffn_b2': _L2_ffn_in['b2'], 'L3_xattn_Wq': _L3_xattn_in['Wq'], 'L3_xattn_bq': _L3_xattn_in['bq'], 'L3_xattn_Wk': _L3_xattn_in['Wk'], 'L3_xattn_bk': _L3_xattn_in['bk'], 'L3_xattn_Wv': _L3_xattn_in['Wv'], 'L3_xattn_bv': _L3_xattn_in['bv'], 'L3_xattn_Wo': _L3_xattn_in['Wo'], 'L3_xattn_bo': _L3_xattn_in['bo'], 'L3_attn_W_qkv': _L3_attn_in['W_qkv'], 'L3_attn_W_proj': _L3_attn_in['W_proj'], 'L3_attn_b_proj': _L3_attn_in['b_proj'], 'L3_attn_ln_gamma': _L3_attn_in['ln_gamma'], 'L3_attn_ln_beta': _L3_attn_in['ln_beta'], 'L3_attn_spatial_centers': _L3_attn_in['spatial_centers'], 'L3_ffn_U1': _L3_ffn_in['U1'], 'L3_ffn_V1': _L3_ffn_in['V1'], 'L3_ffn_b1': _L3_ffn_in['b1'], 'L3_ffn_U2': _L3_ffn_in['U2'], 'L3_ffn_V2': _L3_ffn_in['V2'], 'L3_ffn_b2': _L3_ffn_in['b2']}

def reference(x, ctx_1024, fside_Bx16xSxS2_0, mask_BxS2_bk1, L0_xattn_Wk, L0_xattn_Wv, L0_xattn_bv, L0_xattn_Wq, L0_xattn_bq, L0_xattn_Wo, L0_xattn_bo, L0_attn_Wq, L0_attn_Wk, L0_attn_Wv, L0_attn_Wg, L0_attn_Wo, L0_attn_gamma, L0_attn_beta, L0_ffn_Wg, L0_ffn_Ws1, L0_ffn_Ws3, L0_ffn_Ws2, L0_ffn_We1, L0_ffn_We3, L0_ffn_We2, L1_xattn_Wq, L1_xattn_Wkv, L1_xattn_Wo, L1_xattn_bo, L1_attn_wq, L1_attn_wk, L1_attn_wv, L1_attn_wo, L1_ffn_gate_w, L1_ffn_gate_b, L1_ffn_dp_w1, L1_ffn_dp_b1, L1_ffn_dp_w2, L1_ffn_dp_b2, L1_ffn_ew1, L1_ffn_eb1, L1_ffn_ew2, L1_ffn_eb2, L2_xattn_Wq, L2_xattn_Wk, L2_xattn_Wv, L2_xattn_Wo, L2_xattn_W1, L2_xattn_b1, L2_xattn_W2, L2_xattn_b2, L2_xattn_g1, L2_xattn_be1, L2_xattn_g2, L2_xattn_be2, L2_attn_Wq, L2_attn_bq, L2_attn_Wk, L2_attn_bk, L2_attn_Wv, L2_attn_bv, L2_attn_Wo, L2_attn_bo, L2_attn_rel_bias, L2_attn_W1, L2_attn_b1, L2_attn_W2, L2_attn_b2, L2_ffn_Wg, L2_ffn_bg, L2_ffn_W1, L2_ffn_b1, L2_ffn_W2, L2_ffn_b2, L3_xattn_Wq, L3_xattn_bq, L3_xattn_Wk, L3_xattn_bk, L3_xattn_Wv, L3_xattn_bv, L3_xattn_Wo, L3_xattn_bo, L3_attn_W_qkv, L3_attn_W_proj, L3_attn_b_proj, L3_attn_ln_gamma, L3_attn_ln_beta, L3_attn_spatial_centers, L3_ffn_U1, L3_ffn_V1, L3_ffn_b1, L3_ffn_U2, L3_ffn_V2, L3_ffn_b2):
    import jax
    import jax.numpy as jnp

    def _L0_xattn_ref(k, v, q, Wk, Wv, bv, Wq, bq, Wo, bo):
        import jax, jax.numpy as jnp
        import numpy as np
        D_MODEL = 128
        B, S = (4, 256)
        kp = jnp.einsum('bsd,ed->bse', k, Wk)
        vp = jnp.einsum('bsd,ed->bse', v, Wv) + bv
        qp = jnp.einsum('bsd,ed->bse', q, Wq) + bq
        scale = 1.0 / jnp.sqrt(jnp.float32(kp.shape[-1]))
        scores = jnp.einsum('bqd,bkd->bqk', qp, kp) * scale
        probs = jax.nn.softmax(scores, axis=-1)
        ctx = jnp.einsum('bqk,bkd->bqd', probs, vp)
        return jnp.einsum('bqd,ed->bqe', ctx, Wo) + bo

    def _L0_attn_ref(hidden_states, Wq, Wk, Wv, Wg, Wo, gamma, beta):
        import jax, jax.numpy as jnp
        import numpy as np
        NUM_HEADS = 16
        B, S, H = (2, 1024, 128)
        b, s, h = hidden_states.shape
        nh = NUM_HEADS
        dk = h // nh
        dv = h // nh
        q = (hidden_states @ Wq).reshape(b, s, nh, dk)
        k = (hidden_states @ Wk).reshape(b, s, nh, dk)
        v = (hidden_states @ Wv).reshape(b, s, nh, dv)
        g = hidden_states @ Wg
        q = jax.nn.elu(q) + 1.0
        k = jax.nn.elu(k) + 1.0
        qk = jnp.sum(q * k, axis=-1, keepdims=True)
        k_sum = jnp.sum(k, axis=1, keepdims=True)
        normalizer = jnp.sum(q * k_sum, axis=-1, keepdims=True)
        z = qk * v / (normalizer + 1e-06)
        z = z.reshape(b, s, nh * dv)
        mu = jnp.mean(z, axis=-1, keepdims=True)
        var = jnp.mean(jnp.square(z - mu), axis=-1, keepdims=True)
        z = (z - mu) * jax.lax.rsqrt(var + 1e-05) * gamma + beta
        z = z * jax.nn.silu(g)
        return z @ Wo

    def _L0_ffn_ref(x, Wg, Ws1, Ws3, Ws2, We1, We3, We2):
        import jax, jax.numpy as jnp
        import numpy as np
        D_MODEL, FF_DIM = (128, 256)
        N_SHARED, N_ROUTED, TOP_K = (1, 8, 2)
        BATCH, SEQ = (2, 256)
        B, S, d = x.shape
        E = Wg.shape[1]
        xf = x.reshape(-1, d)
        T = xf.shape[0]
        gates = jax.nn.sigmoid(xf @ Wg)
        vals, idx = jax.lax.top_k(gates, TOP_K)
        vals = vals / vals.sum(axis=-1, keepdims=True)
        w = jnp.zeros((T, E), x.dtype).at[jnp.arange(T)[:, None], idx].add(vals)
        shared = jax.nn.silu(xf @ Ws1) * (xf @ Ws3) @ Ws2
        h = jax.nn.silu(jnp.einsum('td,edf->tef', xf, We1)) * jnp.einsum('td,edf->tef', xf, We3)
        routed = jnp.einsum('tef,efd,te->td', h, We2, w)
        out = (shared + routed) / (N_SHARED + TOP_K)
        return out.reshape(B, S, d)

    def _L1_xattn_ref(x, context, mask, Wq, Wkv, Wo, bo):
        import jax, jax.numpy as jnp
        import numpy as np
        B, N, M = (4, 128, 512)
        DQ, DC = (128, 128)
        H, DH = (16, 64)
        INNER = H * DH
        SCALE = DH ** (-0.5)
        q = x @ Wq
        kv = context @ Wkv
        k, v = jnp.split(kv, 2, axis=-1)

        def heads(t):
            b, s, _ = t.shape
            return t.reshape(b, s, H, DH).transpose(0, 2, 1, 3)
        q, k, v = (heads(q), heads(k), heads(v))
        sim = jnp.einsum('bhid,bhjd->bhij', q, k) * SCALE
        max_neg = -jnp.finfo(sim.dtype).max
        sim = jnp.where(mask[:, None, None, :], sim, max_neg)
        sim = jnp.clip(sim, -5.0, 5.0)
        attn = jax.nn.softmax(sim, axis=-1)
        out = jnp.einsum('bhij,bhjd->bhid', attn, v)
        out = out.transpose(0, 2, 1, 3).reshape(x.shape[0], x.shape[1], INNER)
        return out @ Wo + bo

    def _L1_attn_ref(x, wq, wk, wv, wo):
        import jax, jax.numpy as jnp
        import numpy as np
        B, S, DIN, DIM = (1, 512, 128, 128)
        NH, NKV = (16, 4)
        HD = DIM // NH
        GS = NH // NKV
        b, s, _ = x.shape
        q = (x @ wq.T).reshape(b, s, NKV, GS, HD)
        k = (x @ wk.T).reshape(b, s, NKV, HD)
        v = (x @ wv.T).reshape(b, s, NKV, HD)
        scale = jnp.asarray(HD ** 0.5, x.dtype)
        att = jnp.einsum('bsgmd,btgd->bgmst', q, k) / scale
        causal = jnp.triu(jnp.ones((s, s), bool), 1)
        att = jnp.where(causal, -jnp.inf, att)
        att = jax.nn.softmax(att, axis=-1)
        ctx = jnp.einsum('bgmst,btgd->bsgmd', att, v).reshape(b, s, DIM)
        return ctx @ wo.T

    def _L1_ffn_ref(x, gate_w, gate_b, dp_w1, dp_b1, dp_w2, dp_b2, ew1, eb1, ew2, eb2):
        import jax, jax.numpy as jnp
        import numpy as np
        D_MODEL = 128
        E = 4
        MIN_E = 1
        TH_LO = 0.5
        TH_HI = 2.0
        B, N, D = x.shape
        xf = x.reshape(B * N, D)
        T = B * N
        h = jax.nn.relu(xf @ dp_w1 + dp_b1)
        entropy = jax.nn.softplus(h @ dp_w2 + dp_b2)[:, 0]
        norm = jnp.clip((entropy - TH_LO) / (TH_HI - TH_LO), 0.0, 1.0)
        k_tok = jnp.clip(jnp.round(MIN_E + norm * (E - MIN_E)).astype(jnp.int32), MIN_E, E)
        logits = xf @ gate_w + gate_b
        top_logits, top_idx = jax.lax.top_k(logits, E)
        pos = jnp.arange(E)
        sel = pos[None, :] < k_tok[:, None]
        masked = jnp.where(sel, top_logits, -jnp.inf)
        w_top = jax.nn.softmax(masked, axis=-1)
        dense_w = jnp.zeros((T, E), dtype=xf.dtype).at[jnp.arange(T)[:, None], top_idx].set(w_top)
        hid = jax.nn.relu(jnp.einsum('td,edh->teh', xf, ew1) + eb1[None, :, :])
        y = jnp.einsum('teh,ehd->ted', hid, ew2) + eb2[None, :, :]
        out = jnp.einsum('te,ted->td', dense_w, y)
        return out.reshape(B, N, D)

    def _L2_xattn_ref(x_q, x_kv, bias, Wq, Wk, Wv, Wo, W1, b1, W2, b2, g1, be1, g2, be2):
        import jax, jax.numpy as jnp
        import numpy as np
        import math
        H = 16
        D = 128
        FF = 512
        DK = D // H
        EPS = 1e-05

        def layer_norm(x, g, b):
            mu = jnp.mean(x, axis=-1, keepdims=True)
            var = jnp.var(x, axis=-1, keepdims=True)
            return (x - mu) * jax.lax.rsqrt(var + EPS) * g + b
        B, S, _ = x_q.shape

        def split(x):
            return x.reshape(B, -1, H, DK).transpose(0, 2, 1, 3)
        q = split(x_q @ Wq.T)
        k = split(x_kv @ Wk.T)
        v = split(x_kv @ Wv.T)
        scores = jnp.einsum('bhqd,bhkd->bhqk', q, k) / math.sqrt(DK) + bias
        p = jax.nn.softmax(scores, axis=-1)
        o = jnp.einsum('bhqk,bhkd->bhqd', p, v)
        o = o.transpose(0, 2, 1, 3).reshape(B, S, D)
        x = x_q + o @ Wo.T
        h = jax.nn.gelu(layer_norm(x, g1, be1) @ W1.T + b1, approximate=False)
        x = x + h @ W2.T + b2
        return layer_norm(x, g2, be2)

    def _L2_attn_ref(x, Wq, bq, Wk, bk, Wv, bv, Wo, bo, rel_bias, W1, b1, W2, b2):
        import math
        import jax, jax.numpy as jnp
        import numpy as np
        D_HIDDEN = 128
        NB_HEADS = 16
        NUM_BUCKETS = 32
        MAX_DISTANCE = 128
        B, L = (2, 128)

        def _relative_position_bucket(relative_position, num_buckets=NUM_BUCKETS, max_distance=MAX_DISTANCE):
            n = -relative_position
            num_buckets = num_buckets // 2
            ret = (n < 0).astype(jnp.int32) * num_buckets
            n = jnp.abs(n)
            max_exact = num_buckets // 2
            is_small = n < max_exact
            val_if_large = max_exact + (jnp.log(jnp.maximum(n, 1).astype(jnp.float32) / max_exact) / math.log(max_distance / max_exact) * (num_buckets - max_exact)).astype(jnp.int32)
            val_if_large = jnp.minimum(val_if_large, num_buckets - 1)
            return ret + jnp.where(is_small, n, val_if_large)

        def layer_normalize(p):
            mean = jnp.mean(p, axis=-1, keepdims=True)
            st_dev = jnp.sqrt(jnp.mean((p - mean) ** 2, axis=-1, keepdims=True))
            return (p - mean) / st_dev

        def _encoder_block(x, Wq, bq, Wk, bk, Wv, bv, Wo, bo, rel_bias, W1, b1, W2, b2):
            d_batch, q_len, d = x.shape
            d_head = d // NB_HEADS
            q = x @ Wq.T + bq
            k = x @ Wk.T + bk
            v = x @ Wv.T + bv
            qm = q.reshape(d_batch * NB_HEADS, q_len, d_head)
            km = k.reshape(d_batch * NB_HEADS, q_len, d_head)
            vm = v.reshape(d_batch * NB_HEADS, q_len, d_head)
            att = jnp.einsum('nqd,nkd->nqk', qm, km)
            att = jax.nn.softmax(att, axis=-1)
            rel_pos = jnp.arange(q_len)[:, None] - jnp.arange(q_len)[None, :]
            buckets = _relative_position_bucket(rel_pos)
            single = rel_bias[buckets]
            batch_pos = jnp.transpose(jnp.tile(single, (1, 1, d_batch)), (2, 0, 1))
            att_out = jnp.einsum('nqk,nkd->nqd', att + batch_pos, vm)
            att_out = att_out.reshape(d_batch, q_len, d) @ Wo.T + bo
            att_block = layer_normalize(att_out + x)
            ff = (att_block @ W1.T + b1) @ W2.T + b2
            return layer_normalize(ff + att_block)
        return _encoder_block(x, Wq, bq, Wk, bk, Wv, bv, Wo, bo, rel_bias, W1, b1, W2, b2)

    def _L2_ffn_ref(x, Wg, bg, W1, b1, W2, b2):
        import jax, jax.numpy as jnp
        import numpy as np
        B, S, H, F, E, R, TOPK = (4, 256, 128, 512, 4, 4, 2)

        def _more_forward(x, Wg, bg, W1, b1, W2, b2):
            b, s, h = x.shape
            cur = x
            for r in range(R):
                flat = cur.reshape(-1, h)
                logits = flat @ Wg[r] + bg[r]
                vals, idx = jax.lax.top_k(logits, TOPK)
                w = jax.nn.softmax(vals, axis=-1)
                cw = jnp.sum(jax.nn.one_hot(idx, E, dtype=flat.dtype) * w[..., None], axis=1)
                hmid = jax.nn.gelu(jnp.einsum('nh,ehf->enf', flat, W1) + b1[:, None, :])
                y = jnp.einsum('enf,efh->enh', hmid, W2) + b2[:, None, :]
                out = jnp.einsum('ne,enh->nh', cw, y)
                cur = cur + out.reshape(b, s, h)
            return cur
        return _more_forward(x, Wg, bg, W1, b1, W2, b2)

    def _L3_xattn_ref(Q, K, V, Wq, bq, Wk, bk, Wv, bv, Wo, bo):
        import jax, jax.numpy as jnp
        import numpy as np
        D_MODEL = 128
        H = 16
        D_K = D_MODEL // H
        B, S, _ = Q.shape

        def proj(x, W, b):
            return (x @ W.T + b).reshape(B, -1, H, D_K).transpose(0, 2, 1, 3)
        q = proj(Q, Wq, bq)
        k = proj(K, Wk, bk)
        v = proj(V, Wv, bv)
        scores = jnp.einsum('bhqd,bhkd->bhqk', q, k) / jnp.sqrt(jnp.float32(D_K))
        attn = jax.nn.softmax(scores, axis=-1)
        ctx = jnp.einsum('bhqk,bhkd->bhqd', attn, v)
        ctx = ctx.transpose(0, 2, 1, 3).reshape(B, S, H * D_K)
        return ctx @ Wo.T + bo

    def _L3_attn_ref(x, W_qkv, W_proj, b_proj, ln_gamma, ln_beta, spatial_centers):
        import jax, jax.numpy as jnp
        import numpy as np
        HEADS = 16
        BIAS_STRENGTH = 0.1
        LN_EPS = 1e-05

        def _layernorm(x, gamma, beta):
            mu = jnp.mean(x, axis=-1, keepdims=True)
            var = jnp.mean((x - mu) ** 2, axis=-1, keepdims=True)
            return (x - mu) * jax.lax.rsqrt(var + LN_EPS) * gamma + beta

        def _spatial_bias(spatial_centers, N, dtype):
            diff = spatial_centers[:, None, :] - spatial_centers[None, :, :]
            dist = jnp.sqrt(jnp.sum(diff * diff, axis=-1))
            max_dist = jnp.max(dist)
            core = jnp.where(max_dist > 1e-06, -dist / max_dist, 0.0) * BIAS_STRENGTH
            P = spatial_centers.shape[0]
            bias = jnp.zeros((N, N), dtype=dtype)
            return bias.at[1:P + 1, 1:P + 1].set(core.astype(dtype))
        B, N, D = x.shape
        H = HEADS
        hd = D // H
        scale = hd ** (-0.5)
        qkv = jnp.einsum('bnd,ed->bne', x, W_qkv)
        qkv = qkv.reshape(B, N, 3, H, hd).transpose(2, 0, 3, 1, 4)
        q, k, v = (qkv[0], qkv[1], qkv[2])
        attn = jnp.einsum('bhnd,bhmd->bhnm', q, k) * scale
        P = spatial_centers.shape[0]
        if N >= P + 1:
            attn = attn + _spatial_bias(spatial_centers, N, x.dtype)[None, None]
        attn = jax.nn.softmax(attn, axis=-1)
        out = jnp.einsum('bhnm,bhmd->bhnd', attn, v)
        out = out.transpose(0, 2, 1, 3).reshape(B, N, D)
        out = jnp.einsum('bnd,ed->bne', out, W_proj) + b_proj
        return out + _layernorm(x, ln_gamma, ln_beta)

    def _L3_ffn_ref(x, U1, V1, b1, U2, V2, b2):
        import jax, jax.numpy as jnp
        import numpy as np
        D_MODEL, D_FF, RANK = (128, 512, 32)
        B, S = (4, 512)
        P = jnp.einsum('bsd,dr->bsr', x, U1)
        H = jax.nn.gelu(jnp.einsum('bsr,rf->bsf', P, V1) + b1)
        Q = jnp.einsum('bsf,fr->bsr', H, U2)
        return jnp.einsum('bsr,rd->bsd', Q, V2) + b2
    x = x + _L0_xattn_ref(ctx_1024, ctx_1024, _layernorm(x, axis=-1), L0_xattn_Wk, L0_xattn_Wv, L0_xattn_bv, L0_xattn_Wq, L0_xattn_bq, L0_xattn_Wo, L0_xattn_bo)
    x = x + _L0_attn_ref(_layernorm(x, axis=-1), L0_attn_Wq, L0_attn_Wk, L0_attn_Wv, L0_attn_Wg, L0_attn_Wo, L0_attn_gamma, L0_attn_beta)
    x = x + _L0_ffn_ref(_layernorm(x, axis=-1), L0_ffn_Wg, L0_ffn_Ws1, L0_ffn_Ws3, L0_ffn_Ws2, L0_ffn_We1, L0_ffn_We3, L0_ffn_We2)
    x = x + _L1_xattn_ref(_layernorm(x, axis=-1), ctx_1024, mask_BxS2_bk1, L1_xattn_Wq, L1_xattn_Wkv, L1_xattn_Wo, L1_xattn_bo)
    x = x + _L1_attn_ref(_layernorm(x, axis=-1), L1_attn_wq, L1_attn_wk, L1_attn_wv, L1_attn_wo)
    x = x + _L1_ffn_ref(_layernorm(x, axis=-1), L1_ffn_gate_w, L1_ffn_gate_b, L1_ffn_dp_w1, L1_ffn_dp_b1, L1_ffn_dp_w2, L1_ffn_dp_b2, L1_ffn_ew1, L1_ffn_eb1, L1_ffn_ew2, L1_ffn_eb2)
    x = x + _L2_xattn_ref(_layernorm(x, axis=-1), ctx_1024, fside_Bx16xSxS2_0, L2_xattn_Wq, L2_xattn_Wk, L2_xattn_Wv, L2_xattn_Wo, L2_xattn_W1, L2_xattn_b1, L2_xattn_W2, L2_xattn_b2, L2_xattn_g1, L2_xattn_be1, L2_xattn_g2, L2_xattn_be2)
    x = x + _L2_attn_ref(_layernorm(x, axis=-1), L2_attn_Wq, L2_attn_bq, L2_attn_Wk, L2_attn_bk, L2_attn_Wv, L2_attn_bv, L2_attn_Wo, L2_attn_bo, L2_attn_rel_bias, L2_attn_W1, L2_attn_b1, L2_attn_W2, L2_attn_b2)
    x = x + _L2_ffn_ref(_layernorm(x, axis=-1), L2_ffn_Wg, L2_ffn_bg, L2_ffn_W1, L2_ffn_b1, L2_ffn_W2, L2_ffn_b2)
    x = x + _L3_xattn_ref(_layernorm(x, axis=-1), ctx_1024, ctx_1024, L3_xattn_Wq, L3_xattn_bq, L3_xattn_Wk, L3_xattn_bk, L3_xattn_Wv, L3_xattn_bv, L3_xattn_Wo, L3_xattn_bo)
    x = x + _L3_attn_ref(_layernorm(x, axis=-1), L3_attn_W_qkv, L3_attn_W_proj, L3_attn_b_proj, L3_attn_ln_gamma, L3_attn_ln_beta, L3_attn_spatial_centers)
    x = x + _L3_ffn_ref(_layernorm(x, axis=-1), L3_ffn_U1, L3_ffn_V1, L3_ffn_b1, L3_ffn_U2, L3_ffn_V2, L3_ffn_b2)
    return x

_drawn_inputs = setup_inputs


def setup_inputs(seed=0):
    import zlib

    import numpy as np

    out = dict(_drawn_inputs(seed))
    spreads = {'L0_xattn_bv': (0.0, 0.1),
     'L0_xattn_bq': (0.0, 0.1),
     'L0_xattn_bo': (0.0, 0.1),
     'L0_attn_gamma': (1.0, 0.2),
     'L0_attn_beta': (0.0, 0.1),
     'L1_xattn_bo': (0.0, 0.1),
     'L1_ffn_gate_b': (0.0, 0.1),
     'L1_ffn_dp_b1': (0.0, 0.1),
     'L1_ffn_eb1': (0.0, 0.558),
     'L1_ffn_eb2': (0.0, 0.1),
     'L2_xattn_b1': (0.0, 0.348),
     'L2_xattn_b2': (0.0, 0.371),
     'L2_xattn_g1': (1.0, 0.56),
     'L2_xattn_be1': (0.0, 0.362),
     'L2_xattn_g2': (1.0, 0.2),
     'L2_xattn_be2': (0.0, 0.312),
     'L2_ffn_bg': (0.0, 1.222),
     'L2_ffn_b1': (0.0, 0.627),
     'L2_ffn_b2': (0.0, 0.1),
     'L3_xattn_bq': (0.0, 0.8),
     'L3_xattn_bk': (0.0, 2.0),
     'L3_xattn_bv': (0.0, 0.394),
     'L3_xattn_bo': (0.0, 0.333),
     'L3_attn_b_proj': (0.0, 0.405),
     'L3_attn_ln_gamma': (1.0, 0.566),
     'L3_attn_ln_beta': (0.0, 0.423),
     'L3_ffn_b1': (0.0, 0.8),
     'L3_ffn_b2': (0.0, 0.435)}
    factors = {'fside_Bx16xSxS2_0': 23.846,
     'L0_ffn_Wg': 8.0,
     'L0_ffn_Ws1': 8.0,
     'L0_ffn_Ws3': 8.0,
     'L0_ffn_Ws2': 8.0,
     'L0_ffn_We1': 8.0,
     'L0_ffn_We3': 8.0,
     'L0_ffn_We2': 8.0,
     'L2_attn_bq': 2.782,
     'L2_attn_bv': 3.807,
     'L2_attn_b2': 2.801,
     'L3_ffn_U1': 8.0,
     'L3_ffn_V1': 8.0,
     'L3_ffn_U2': 8.0,
     'L3_ffn_V2': 8.0,
     'L1_ffn_ew1': 3.31,
     'L2_attn_bk': 3.484,
     'L2_attn_bo': 3.919,
     'L2_attn_b1': 3.878,
     'L2_ffn_Wg': 2.674}
    for name, (base, spread) in spreads.items():
        noise = np.random.default_rng([zlib.crc32(name.encode()), seed]).standard_normal(out[name].shape)
        drawn = base * np.exp(spread * noise) if base else spread * noise
        out[name] = jnp.asarray(drawn.astype(out[name].dtype))
    for name, factor in factors.items():
        out[name] = (out[name] * factor).astype(out[name].dtype)
    return out
```

```python
from contextlib import ExitStack

import concourse.bass as bass
from concourse import mybir

F32 = mybir.dt.float32
I32 = mybir.dt.int32
ALU = mybir.AluOpType
ACT = mybir.ActivationFunctionType
AX = mybir.AxisListType.X

P = 128
B = 32
S = 32
NT = B * S // P
TOK = B * S
KEYS = 257
KPAD = 260
H = 16
HG = 4
DK = 8
FQ = P + 1
DH1 = 64
UNIT = 256
WCOLS = 3 * UNIT + 2
LN_EPS = 1e-5
L0X_STEPS = B // 4


def weight_plan():
    groups = {
        "first": [("ident", 128), ("l0x_q", 128), ("l0x_k", 128), ("l0x_v", 128), ("l0x_o", 128),
                  ("cols", 64)],
        "l0": [("blockones", 128), ("l0a_qkvg", 512), ("l0a_o", 128), ("l0f_gate", 8), ("rank_low8", 64),
               ("rank_low4", 16), ("mask4", 4), ("mask16", 16), ("mask_last", 128)],
        "l1": [("l1a_q", 128), ("l1a_k", 128), ("l1a_v", 128), ("l1a_o", 128), ("causal", 32),
               ("l1f_gate", 4), ("l1f_dp1", 64), ("l1f_dp2", 1)],
        "l2": [("l2x_q", 128), ("l2x_k", 128), ("l2x_v", 128), ("l2x_o", 128), ("l2a_q", 512),
               ("l2a_k", 512), ("l2a_v", 512), ("l2a_o", 2048), ("l2a_w1", 128), ("l2a_w2", 128),
               ("mask_pair", 256), ("onehot", 1024), ("l2f_gate", 16)],
        "l3": [("l3x_q", 128), ("l3x_k", 128), ("l3x_v", 128), ("l3x_o", 128), ("l3a_q", 128),
               ("l3a_k", 128), ("l3a_v", 128), ("l3a_o", 128), ("l3f_u1", 128), ("l3f_v2", 128)],
    }
    at, spans = 0, {}
    for g, items in groups.items():
        a0 = at
        for name, n in items:
            spans[name] = (at, n)
            at += n
        spans["group_" + g] = (a0, at - a0)
    return spans, at


SPANS, WTOTAL = weight_plan()

ROWS = ["l0x_bo", "l0a_gamma", "l0a_beta", "l1x_bo", "l1f_b2_0", "l1f_b2_1", "l1f_b2_2", "l1f_b2_3",
        "l2x_b2", "l2x_g1", "l2x_be1", "l2x_g2", "l2x_be2", "l2a_bo", "l2a_b2",
        "l2f_b2_0", "l2f_b2_1", "l2f_b2_2", "l2f_b2_3", "l3x_bv", "l3x_bo", "l3a_bp", "l3a_lng",
        "l3a_lnb", "l3f_b2", "small"]
SMALL_L1GATE, SMALL_DPB2, SMALL_L2GATE = 0, 4, 8

COLS = {"l0x_bq": 0, "l0x_bv": 1, "l3x_bq": 2, "l3x_bk": 3, "l2a_b1": 4, "l1f_dpb1": 5,
        "l2a_bq": 8, "l2a_bk": 24, "l2a_bv": 40}

FF_UNITS = {"l0f": (0, 9), "l1f": (9, 4), "l2x": (13, 2), "l2f": (15, 8), "l3f": (23, 2)}
N_UNITS = 25


class Tally:

    def __init__(self, eng):
        self.eng, self.n = eng, {}
        self.i, self.per, self.start = None, {}, {}

    def value(self, name):
        v = self.n[name]
        return v + self.i * self.per[name] if self.i is not None and self.per.get(name) else v

    def up(self, name, k=1):
        self.n[name] = self.n.get(name, 0) + k
        return self.value(name)

    def loop(self, trips, per, body):
        self.start = dict(self.n)
        with self.eng.Fori(0, trips, 1) as i:
            self.i, self.per = i, per
            body(i)
            self.i, self.per = None, {}
        rise = {k: v - self.start.get(k, 0) for k, v in self.n.items() if v != self.start.get(k, 0)}
        assert rise == per, f"{self.eng.engine}: {rise}"
        for k, v in rise.items():
            self.n[k] = self.start.get(k, 0) + trips * v

    def skewed(self, steps, per, head, front, back):
        front(0, 0, True)
        front(1, 1, True)
        back(0, 0, True)
        front(2, 0, False)
        back(1, 1, True)

        def body(i):
            front(i * 2 + 3, 1, False)
            back(i * 2 + 2, 0, False)
            front(i * 2 + 4, 0, False)
            back(i * 2 + 3, 1, False)
        self.loop((steps - 4) // 2, per, body)
        front(steps - 1, 1, False)
        back(steps - 2, 0, False)
        back(steps - 1, 1, False)


def perceiver(nc, ctxT, ctxN, fside, mask, wpack, wrows, l1x_w, units, relb, x_in, out):
    ctx = ExitStack()
    with ctx:
        def sb(name, shape, dt=F32):
            return ctx.enter_context(nc.sbuf_tensor(name, shape, dt))

        W = sb("W", [P, WTOTAL])
        RB = sb("RB", [P, len(ROWS), P])
        X = sb("X", [P, NT, P])
        XN = sb("XN", [P, NT, P])
        XNT = sb("XNT", [P, TOK])
        Y = sb("Y", [P, NT, P])
        Z = sb("Z", [P, NT, P])
        ZT = sb("ZT", [P, TOK])
        OT = sb("OT", [P, TOK])
        ACC = sb("ACC", [P, NT, P])
        ACCB = sb("ACCB", [P, NT, P])
        CTX = sb("CTX", [P, 2, 2592])
        WB = sb("WB", [P, 2, WCOLS])
        ST = sb("ST", [P, NT, 6])
        MV = sb("MV", [P, NT, 2])
        SD = sb("SD", [P, 2, NT])
        SM = sb("SM", [P, 1200])
        AR = sb("AR", [P, 18432])
        MK = sb("MK", [P, 3, B], I32)
        PS = ctx.enter_context(nc.psum_tensor("PS", [P, 8, 512], F32))
        PSF = PS[:, :, :].rearrange("p b n -> p (b n)")

        def w(name):
            a, n = SPANS[name]
            return W[:, a:a + n]

        def row(name):
            return RB[:, ROWS.index(name), :]

        def rows_t(name, nt=NT):
            return row(name).unsqueeze(1).broadcast_to([P, nt, P])

        def col(name, n=1):
            a = SPANS["cols"][0] + COLS[name]
            return W[:, a:a + n]

        def ar(a, n):
            return AR[:, a:a + n]

        ident = w("ident")

        names = """act_ran dve_ran pool_ran
            x_landed w_first w_l0 w_l1 w_l2 w_l3 rows_landed l1x_w_landed mask_landed relb_landed
            ctx_landed0 ctx_landed1 unit_landed0 unit_landed1 out_landed
            var_ready std_ready norm_ready stream_ready turned turned_taken
            lin_ready lin_taken proj_ready bias_ready resid_done
            l0s_q_ready l0s_staged l0s_scores l0s_max l0s_exp l0s_probs l0s_pt l0s_pt_taken l0s_u l0s_u_taken
            l0a_mm l0a_act l0a_qk l0a_ksum
            gate_mm gate_hidden gate_entropy gate_shift gate_act expert_weights
            up_ready act_half h_ready down_ready down_used
            y_w_ready y_w_taken yq_ready yq_taken ys_ready yclip yexp yu_ready yu_taken yt_ready yt_taken
            yo_ready yo_taken
            xq_mm xq_ready xk_ready xk_taken xv_ready xv_taken xqb xs_ready xmax xexp xp_ready xpt_ready xpt_a xpt_d
            xu_ready xu_taken x_out
            qkv_taken c_in c_scores c_shift c_exp c_probs c_pt c_pt_taken c_pv c_masked
            pair_ready pair_taken""".split()
        sig = {n: ctx.enter_context(nc.semaphore(n)) for n in names}
        block = ctx.enter_context(nc.Block())

        l0_cT = [CTX[:, q, 0:4 * KPAD].rearrange("p (j k) -> p j k", j=4) for q in range(2)]
        l0_cn = [CTX[:, q, 1040:1040 + 8 * FQ].rearrange("p (j c f) -> p j c f", j=4, c=2) for q in range(2)]
        l0_cl = [CTX[0:1, q, 2072:2072 + 4 * FQ].rearrange("p (j f) -> p j f", j=4) for q in range(2)]
        l0_qp = ar(0, TOK)
        l0_qt = ar(TOK, TOK)
        l0_qs = [ar(2048 + 128 * q, 128) for q in range(2)]
        l0_p = [ar(2304 + KEYS * q, KEYS) for q in range(2)]
        l0_pt = [ar(2820 + 384 * q, 384).rearrange("p (c n) -> p c n", c=3) for q in range(2)]
        l0_ut = ar(3588, TOK)
        l0_ct = ar(4612, TOK)
        l0_neg = [SM[:, 0 + q:1 + q] for q in range(2)]
        l0_sum = [SM[:, 2 + q:3 + q] for q in range(2)]
        c_T = [CTX[:, q, 0:KPAD] for q in range(2)]
        c_N = [CTX[:, q, 260:260 + 2 * FQ].rearrange("p (c f) -> p c f", c=2) for q in range(2)]
        c_L = [CTX[0:1, q, 518:518 + FQ] for q in range(2)]
        c_F = [CTX[:, q, 700:700 + HG * KEYS].rearrange("p (g k) -> p g k", g=HG) for q in range(2)]
        y_w = ar(8192, 4096).rearrange("p (m h n) -> p m h n", m=4, h=8)
        y_A = ar(0, 2048).rearrange("p (h n) -> p h n", h=H)
        y_M = ar(2048, 2048).rearrange("p (h n) -> p h n", h=H)
        y_Q = [ar(4096 + 512 * q, 512) for q in range(2)]
        y_C = ar(5120, 1536).rearrange("p (c n) -> p c n", c=3)
        y_P = [ar(8192 + 1536 * q, 1536).rearrange("p (c n) -> p c n", c=3) for q in range(2)]
        y_U = ar(11264, 512).rearrange("p (g n) -> p g n", g=4)
        y_V = ar(11776, 512)
        y_hi = ar(12288, 3 * B).rearrange("p (c b) -> p c b", c=3)
        y_r = SM[:, 8:12]
        y_at = lambda h: 8 * (h % 2) + h // 2
        x_q = ar(0, TOK)
        x_qb = [ar(1024 + 512 * q, 512) for q in range(2)]
        x_k = [ar(2048 + 257 * q, 257) for q in range(2)]
        x_v = [ar(2564 + 256 * q, 256).rearrange("p (c n) -> p c n", c=2) for q in range(2)]
        x_vl = [ar(3076 + 128 * q, 128) for q in range(2)]
        x_p = [ar(3332 + 1028 * q, 1028).rearrange("p (g k) -> p g k", g=HG) for q in range(2)]
        x_s = ar(5388, 1028).rearrange("p (g k) -> p g k", g=HG)
        x_pt = [ar(6416 + 1024 * q, 1024).rearrange("p (c n) -> p c n", c=2) for q in range(2)]
        x_pl = [ar(8464 + 128 * q, 128) for q in range(2)]
        x_t = ar(8720, 128)
        x_neg = [SM[:, 16 + 4 * q:20 + 4 * q] for q in range(2)]
        x_sum = [SM[:, 24 + 4 * q:28 + 4 * q] for q in range(2)]
        x_rec = SM[:, 32:36]
        c_qb = ar(0, 4096)
        c_k = ar(4096, 1024)
        c_v = ar(5120, 1024)
        c_q = ar(6144, 1024)
        c_vt = ar(6144, 1024)
        c_p = ar(7168, 2048)
        c_p2 = ar(9216, 2048)
        c_pt = ar(11264, 2048)
        c_big = ar(13312, 4096)
        c_red = SM[:, 64:128]
        c_relb = ar(17408, 128).rearrange("p (m k) -> p m k", m=4)
        c_rel2 = ar(17536, 128).rearrange("p (k m) -> p k m", k=32)
        flat = lambda a: a[:, :, :].rearrange("p t n -> p (t n)")
        f_h = [ar(1024 * q, 1024).rearrange("p (c n) -> p c n", c=2) for q in range(2)]
        f_s = [ar(2048 + 512 * c, 512) for c in range(2)]
        f_pt = ar(3072, TOK)
        f_w = SM[:, 128:200].rearrange("p (t e) -> p t e", t=NT)

        g_l = SM[:, 200:264]
        g_e = SM[:, 264:328]
        g_m = SM[:, 328:336]
        g_k = SM[:, 336:344]
        g_rank = SM[:, 344:408]
        g_a = ar(4096, 512)
        g_b = ar(4608, 512)
        g_h = ar(5120, TOK)
        g_z = SM[:, 408:480].rearrange("p (j t) -> p j t", j=9)

        LAYERS_FF = {
            "l0f": (True, ACT.Silu, True), "l1f": (False, ACT.Relu, True),
            "l2x": (False, ACT.Gelu, False), "l2f": (False, ACT.Gelu_apprx_tanh, True),
            "l3f": (False, ACT.Gelu_apprx_tanh, False)}

        @block.sync
        def _(sp):
            seen = Tally(sp)
            sp.dma_start(X[:, :, :], x_in).then_inc(sig["x_landed"], 16)
            a, cols = SPANS["group_first"]
            sp.dma_start(W[:, a:a + cols], wpack[:, a:a + cols]).then_inc(sig["w_first"], 16)

            def load_units(layer, trips=1):
                u0, nu = FF_UNITS[layer]

                if seen.n.get("down_ready"):
                    sp.wait_ge(sig["down_ready"], seen.up("down_ready", 0))

                def load(u, q, free):
                    if free:
                        sp.wait_ge(sig["down_ready"], seen.up("down_ready", 2))
                    sp.dma_start(WB[:, q, :], units[bass.ds(u, 1), :, :].rearrange("u p n -> (u p) n"))\
                        .then_inc(sig[f"unit_landed{q}"], 16)
                if layer == "l0f":
                    load(0, 0, False)
                    load(1, 1, False)
                    seen.loop(3, {"down_ready": 4}, lambda i: (load(i * 2 + 2, 0, True), load(i * 2 + 3, 1, True)))
                    load(8, 0, True)
                    seen.up("down_ready", 4)
                elif layer == "l2f":
                    load(u0, 0, False)
                    load(u0 + 1, 1, False)
                    for r in range(4):
                        seen.loop(3, {"down_ready": 4}, lambda i: (load(i * 2 + (u0 + 2), 0, True),
                                                                load(i * 2 + (u0 + 3), 1, True)))
                        if r < 3:
                            load(u0, 0, True)
                            load(u0 + 1, 1, True)
                    seen.up("down_ready", 4)
                else:
                    load(u0, 0, False)
                    load(u0 + 1, 1, False)
                    if nu == 4:
                        load(u0 + 2, 0, True)
                        load(u0 + 3, 1, True)
                    seen.up("down_ready", 4)

            def l0_load(s, q, first):
                if not (first and (isinstance(s, int) and s < 2)):
                    sp.wait_ge(sig["l0s_u"], seen.up("l0s_u"))
                d = sig[f"ctx_landed{q}"]
                src = ctxT[bass.ds(s * 4, 4), :, :].rearrange("j p k -> p j k")
                sp.dma_start(l0_cT[q], src).then_inc(d, 16)
                for c in range(2):
                    src = ctxN[bass.ds(s * 4, 4), c * P:(c + 1) * P, :].rearrange("j p f -> p j f")
                    sp.dma_start(l0_cn[q][:, :, c, :], src).then_inc(d, 16)
                src = ctxN[bass.ds(s * 4, 4), 2 * P:KEYS, :].rearrange("j p f -> p j f")
                sp.dma_start(l0_cl[q], src).then_inc(d, 16)
            l0_load(0, 0, True)
            l0_load(1, 1, True)
            seen.loop(L0X_STEPS // 2 - 1, {"l0s_u": 2},
                   lambda i: (l0_load(i * 2 + 2, 0, False), l0_load(i * 2 + 3, 1, False)))
            seen.up("l0s_u", 2)
            load_units("l0f")

            def l1_load(b, q, free):
                if free:
                    sp.wait_ge(sig["yu_ready"], seen.up("yu_ready"))
                d = sig[f"ctx_landed{q}"]
                sp.dma_start(c_T[q], ctxT[bass.ds(b, 1), :, :].rearrange("j p k -> (j p) k")).then_inc(d, 16)
                src = ctxN[bass.ds(b, 1), 0:2 * P, :].rearrange("j (c p) f -> (j p) c f", c=2)
                sp.dma_start(c_N[q], src).then_inc(d, 16)
                sp.dma_start(c_L[q], ctxN[bass.ds(b, 1), 2 * P:KEYS, :].rearrange("j p f -> (j p) f"))\
                    .then_inc(d, 16)
            sp.wait_ge(sig["l0s_u"], seen.up("l0s_u", 0))
            l1_load(0, 0, False)
            l1_load(1, 1, False)
            seen.loop(B // 2 - 1, {"yu_ready": 2}, lambda i: (l1_load(i * 2 + 2, 0, True), l1_load(i * 2 + 3, 1, True)))
            seen.up("yu_ready", 2)
            load_units("l1f")

            def x_load(b, q, free, with_bias):
                if free:
                    sp.wait_ge(sig["xmax"], seen.up("xmax"))
                    sp.wait_ge(sig["xs_ready"], seen.up("xs_ready"))
                d = sig[f"ctx_landed{q}"]
                sp.dma_start(c_T[q], ctxT[bass.ds(b, 1), :, :].rearrange("j p k -> (j p) k")).then_inc(d, 16)
                if with_bias:
                    src = fside[bass.ds(b, 1), :, :].rearrange("j (g p) k -> (j p) g k", g=HG)
                    sp.dma_start(c_F[q], src).then_inc(d, 16)

            def x_loads(with_bias):
                x_load(0, 0, False, with_bias)
                x_load(1, 1, False, with_bias)
                seen.loop(B // 2 - 1, {"xmax": 2, "xs_ready": 2},
                       lambda i: (x_load(i * 2 + 2, 0, True, with_bias), x_load(i * 2 + 3, 1, True, with_bias)))
                seen.up("xmax", 2)
                seen.up("xs_ready", 2)
            sp.wait_ge(sig["yu_ready"], seen.up("yu_ready", 0))
            x_loads(True)
            load_units("l2x")
            load_units("l2f")
            sp.wait_ge(sig["xmax"], seen.up("xmax", 0))
            sp.wait_ge(sig["xs_ready"], seen.up("xs_ready", 0))
            x_loads(False)
            load_units("l3f")
            sp.wait_ge(sig["resid_done"], seen.up("resid_done", 12))
            sp.dma_start(out, X[:, :, :]).then_inc(sig["out_landed"], 16)
            sp.wait_ge(sig["out_landed"], 16)

        @block.tensor
        def _(pe):
            seen = Tally(pe)
            bank = lambda k: PS[:, k, :]

            def turn(src, ready="norm_ready"):
                if ready == "stream_ready":
                    pe.wait_ge(sig[ready], seen.up(ready))
                for t in range(NT):
                    if ready == "norm_ready":
                        pe.wait_ge(sig[ready], seen.up(ready))
                    m = pe.transpose(PS[:, t // 4, 128 * (t % 4):128 * (t % 4) + 128], src[:, t, :], ident)
                m.then_inc(sig["turned"], 1)
                pe.wait_ge(sig["turned_taken"], seen.up("turned_taken"))

            def wide(k, weight, src):
                for hh in range(2):
                    m = pe.matmul(bank(k + hh), weight, src[:, 512 * hh:512 * hh + 512], start=True, stop=True)
                return m

            def project(src, weight):
                for t in range(NT):
                    m = pe.matmul(PS[:, 6 + t // 4, 128 * (t % 4):128 * (t % 4) + 128],
                                  src[:, P * t:P * t + P], weight, start=True, stop=True)
                m.then_inc(sig["proj_ready"], 1)

            def ff(layer, src):
                gated = LAYERS_FF[layer][0]
                u0, nu = FF_UNITS[layer]
                def up(q, hh, first=False):
                    if hh == 0:
                        pe.wait_ge(sig[f"unit_landed{q}"], seen.up(f"unit_landed{q}", 16))
                    for c in range(2):
                        if not first:
                            pe.wait_ge(sig["h_ready"], seen.up("h_ready"))
                        m = pe.matmul(bank(2 * c), WB[:, q, 128 * c:128 * c + 128],
                                      src[:, 512 * hh:512 * hh + 512], start=True, stop=True)
                        if gated:
                            m = pe.matmul(bank(2 * c + 1), WB[:, q, UNIT + 128 * c:UNIT + 128 * c + 128],
                                          src[:, 512 * hh:512 * hh + 512], start=True, stop=True)
                        m.then_inc(sig["up_ready"], 1)

                def down(q, hh, first=False):
                    if not first:
                        pe.wait_ge(sig["down_used"], seen.up("down_used"))
                    for t in range(4):
                        for c in range(2):
                            m = pe.matmul(PS[:, 4 + hh, 128 * t:128 * t + 128],
                                          f_h[hh][:, c, 128 * t:128 * t + 128],
                                          WB[:, q, 2 * UNIT + 128 * c:2 * UNIT + 128 * c + 128],
                                          start=(c == 0), stop=(c == 1))
                    m.then_inc(sig["down_ready"], 1)

                up(0, 0, first=True)
                up(0, 1)
                down(0, 0, first=True)
                up(1, 0)
                down(0, 1, first=True)

                def body(i):
                    up(1, 1)
                    down(1, 0)
                    up(0, 0)
                    down(1, 1)
                    up(0, 1)
                    down(0, 0)
                    up(1, 0)
                    down(0, 1)
                trips = (nu - 2) // 2
                if trips > 0:
                    seen.loop(trips, {"unit_landed0": 16, "unit_landed1": 16, "h_ready": 8, "down_used": 4}, body)
                up(1, 1)
                down(1, 0)
                if nu % 2:
                    up(0, 0)
                    down(1, 1)
                    up(0, 1)
                    down(0, 0)
                    pe.wait_ge(sig["h_ready"], seen.up("h_ready", 2))
                    down(0, 1)
                else:
                    pe.wait_ge(sig["h_ready"], seen.up("h_ready", 2))
                    down(1, 1)
                pe.wait_ge(sig["down_used"], seen.up("down_used", 2))

            pe.wait_ge(sig["w_first"], 16)
            turn(XN)
            wide(2, w("l0x_q"), XNT).then_inc(sig["lin_ready"], 1)
            pe.wait_ge(sig["lin_taken"], seen.up("lin_taken"))
            wide(4, w("l0x_k"), l0_qt).then_inc(sig["lin_ready"], 1)

            def l0_front(s, q, first):
                pe.wait_ge(sig[f"ctx_landed{q}"], seen.up(f"ctx_landed{q}", 64))
                pe.wait_ge(sig["l0s_staged"], seen.up("l0s_staged"))
                if not (isinstance(s, int) and s == 0):
                    pe.wait_ge(sig["l0s_exp"], seen.up("l0s_exp"))
                for j in range(4):
                    m = pe.matmul(PS[32 * j:32 * j + 32, 0, 0:KEYS], l0_qs[q][:, 32 * j:32 * j + 32],
                                  l0_cT[q][:, j, 0:KEYS], start=True, stop=True)
                m.then_inc(sig["l0s_scores"], 1)

            def l0_back(s, q, first):
                pe.wait_ge(sig["l0s_probs"], seen.up("l0s_probs"))
                for c in range(2):
                    m = pe.transpose(PS[:, 1, 128 * c:128 * c + 128], l0_p[q][:, 128 * c:128 * c + 128], ident)
                m = pe.transpose(PS[0:1, 1, 256:384], l0_p[q][:, 256:257], ident)
                m.then_inc(sig["l0s_pt"], 1)
                pe.wait_ge(sig["l0s_pt_taken"], seen.up("l0s_pt_taken"))
                if not (isinstance(s, int) and s == 0):
                    pe.wait_ge(sig["l0s_u_taken"], seen.up("l0s_u_taken"))
                for j in range(4):
                    for c in range(2):
                        pe.matmul(PS[:, 2, 32 * j:32 * j + 32], l0_cn[q][:, j, c, 0:P],
                                  l0_pt[q][:, c, 32 * j:32 * j + 32], start=(c == 0), stop=False)
                    m = pe.matmul(PS[:, 2, 32 * j:32 * j + 32], l0_cl[q][0:1, j, 0:P],
                                  l0_pt[q][0:1, 2, 32 * j:32 * j + 32], start=False, stop=True)
                m.then_inc(sig["l0s_u"], 1)
            seen.skewed(L0X_STEPS, {"ctx_landed0": 64, "ctx_landed1": 64, "l0s_staged": 2, "l0s_exp": 2,
                                 "l0s_probs": 2, "l0s_pt_taken": 2,
                                 "l0s_u_taken": 2}, None, l0_front, l0_back)
            seen.up("l0s_exp")
            pe.wait_ge(sig["l0s_u_taken"], seen.up("l0s_u_taken"))
            wide(4, w("l0x_v"), l0_ut).then_inc(sig["lin_ready"], 1)
            pe.wait_ge(sig["lin_taken"], seen.up("lin_taken"))
            project(l0_ct, w("l0x_o"))

            pe.wait_ge(sig["w_l0"], 16)
            turn(XN)
            for t in range(NT):
                m = pe.matmul(bank(t), XNT[:, P * t:P * t + P], w("l0a_qkvg"), start=True, stop=True)
                m.then_inc(sig["l0a_mm"], 1)
            pe.wait_ge(sig["l0a_qk"], seen.up("l0a_qk", 2))
            lk = ar(0, 2048).rearrange("p (t n) -> p t n", t=NT)
            for hh in range(2):
                m = pe.matmul(bank(hh), w("blockones"), lk[:, 4 * hh:4 * hh + 4, 128:256], start=True, stop=True)
            m.then_inc(sig["l0a_ksum"], 1)
            turn(Z, "stream_ready")
            project(ZT, w("l0a_o"))

            turn(XN)
            for t in range(NT):
                m = pe.matmul(PS[:, 6, 8 * t:8 * t + 8], XNT[:, P * t:P * t + P], w("l0f_gate"),
                              start=True, stop=True)
            m.then_inc(sig["gate_mm"], 1)
            ff("l0f", XNT)

            pe.wait_ge(sig["l1x_w_landed"], 16)
            pe.wait_ge(sig["resid_done"], seen.up("resid_done", 3))
            for m_out in range(2):
                for odd in range(2):
                    r = slice(64 * odd, 64 * odd + 64)
                    for k in range(2):
                        for e in range(4):
                            m = pe.matmul(PS[:, 4 * m_out + 2 * odd + k, 128 * e:128 * e + 128],
                                          y_w[r, 2 * m_out, 4 * k + e, :], y_w[r, 2 * m_out + 1, 4 * k + e, :],
                                          start=True, stop=True)
                        m.then_inc(sig["y_w_ready"], 1)
            pe.wait_ge(sig["y_w_taken"], seen.up("y_w_taken", 8))
            turn(XN)

            def y_q(b):
                for h in range(H):
                    m = pe.matmul(PS[:, 0, 32 * h:32 * h + 32], y_A[:, y_at(h), :], XNT[:, bass.ds(b * 32, 32)],
                                  start=True, stop=True)
                m.then_inc(sig["yq_ready"], 1)

            def y_s(b, q):
                pe.wait_ge(sig[f"ctx_landed{q}"], seen.up(f"ctx_landed{q}", 48))
                pe.wait_ge(sig["yq_taken"], seen.up("yq_taken"))
                if not (isinstance(b, int) and b == 0):
                    pe.wait_ge(sig["yclip"], seen.up("yclip"))
                for c in range(2):
                    pe.matmul(bank(1 + c), c_T[q][:, P * c:P * c + P], y_Q[q], start=True, stop=True)
                m = pe.matmul(PS[0:1, 3, :], c_T[q][:, 256:257], y_Q[q], start=True, stop=True)
                m.then_inc(sig["ys_ready"], 1)

            def y_u(q):
                pe.wait_ge(sig["yexp"], seen.up("yexp"))
                for g in range(HG):
                    o = PS[:, 4 + g // 2, FQ * (g % 2):FQ * (g % 2) + FQ]
                    for c in range(2):
                        pe.matmul(o, y_P[q][:, c, P * g:P * g + P], c_N[q][:, c, :], start=(c == 0), stop=False)
                    m = pe.matmul(o, y_P[q][0:1, 2, P * g:P * g + P], c_L[q], start=False, stop=True)
                m.then_inc(sig["yu_ready"], 1)

            def y_o(b):
                pe.wait_ge(sig["yu_taken"], seen.up("yu_taken"))
                for g in range(HG):
                    m = pe.transpose(PS[:, 6, P * g:P * g + P], y_U[:, g, :], ident)
                m.then_inc(sig["yt_ready"], 1)
                pe.wait_ge(sig["yt_taken"], seen.up("yt_taken"))
                if not (isinstance(b, int) and b == 0):
                    pe.wait_ge(sig["yo_taken"], seen.up("yo_taken"))
                for h in range(H):
                    m = pe.matmul(PS[:, 7, 0:32], y_M[:, y_at(h), :], y_V[:, 32 * h:32 * h + 32],
                                  start=(h == 0), stop=(h == H - 1))
                m.then_inc(sig["yo_ready"], 1)

            y_q(0)
            y_s(0, 0)
            y_q(1)
            y_u(0)
            y_s(1, 1)
            y_o(0)

            def y_body(i):
                for k in range(2):
                    y_q(i * 2 + (2 + k))
                    y_u(1 - k)
                    y_s(i * 2 + (2 + k), k)
                    y_o(i * 2 + (1 + k))
            seen.loop(B // 2 - 1, {"ctx_landed0": 48, "ctx_landed1": 48, "yq_taken": 2, "yclip": 2,
                                "yexp": 2, "yu_taken": 2,
                                "yt_taken": 2, "yo_taken": 2}, y_body)
            y_u(1)
            y_o(B - 1)
            seen.up("yclip")
            pe.wait_ge(sig["yo_taken"], seen.up("yo_taken"))
            for t in range(NT):
                m = pe.transpose(PS[:, 6 + t // 4, 128 * (t % 4):128 * (t % 4) + 128], OT[:, P * t:P * t + P], ident)
            m.then_inc(sig["proj_ready"], 1)

            def core():
                pe.wait_ge(sig["c_in"], seen.up("c_in"))
                for half in range(2):
                    for nn in range(16):
                        n = 16 * half + nn
                        for g in range(HG):
                            r = slice(32 * g, 32 * g + 32)
                            m = pe.matmul(PS[:, g, 32 * nn:32 * nn + 32], c_qb[r, P * n:P * n + P],
                                          c_k[r, 32 * n:32 * n + 32], start=True, stop=True)
                    m.then_inc(sig["c_scores"], 1)
                    pe.wait_ge(sig["c_probs"], seen.up("c_probs"))
                    for nn in range(16):
                        m = pe.transpose(PS[:, 4 + nn // 4, 128 * (nn % 4):128 * (nn % 4) + 128],
                                         c_p2[:, P * nn:P * nn + P], ident)
                    m.then_inc(sig["c_pt"], 1)
                    pe.wait_ge(sig["c_pt_taken"], seen.up("c_pt_taken"))
                    for nn in range(16):
                        n = 16 * half + nn
                        for g in range(HG):
                            r = slice(32 * g, 32 * g + 32)
                            m = pe.matmul(PS[r, nn // 4, 128 * (nn % 4):128 * (nn % 4) + 128],
                                          c_vt[r, 32 * n:32 * n + 32], c_pt[r, P * nn:P * nn + P],
                                          start=True, stop=True)
                    m.then_inc(sig["c_pv"], 1)
                    pe.wait_ge(sig["c_masked"], seen.up("c_masked"))

            def self_attention(q, k, v, o):
                turn(XN)
                wide(2, w(q), XNT)
                wide(4, w(k), XNT)
                wide(6, w(v), XNT).then_inc(sig["lin_ready"], 1)
                core()
                project(OT, w(o))

            pe.wait_ge(sig["w_l1"], 16)
            self_attention("l1a_q", "l1a_k", "l1a_v", "l1a_o")

            turn(XN)
            for t in range(NT):
                m = pe.matmul(PS[:, 6, 4 * t:4 * t + 4], XNT[:, P * t:P * t + P], w("l1f_gate"),
                              start=True, stop=True)
            for hh in range(2):
                m = pe.matmul(PS[0:64, 2 + hh, :], w("l1f_dp1"), XNT[:, 512 * hh:512 * hh + 512],
                              start=True, stop=True)
            m.then_inc(sig["gate_mm"], 1)
            pe.wait_ge(sig["gate_hidden"], seen.up("gate_hidden"))
            for t in range(NT):
                m = pe.matmul(PS[:, 7, t:t + 1], g_h[0:64, P * t:P * t + P], w("l1f_dp2")[0:64, :],
                              start=True, stop=True)
            m.then_inc(sig["gate_mm"], 1)
            ff("l1f", XNT)

            def cross(kname, vname):
                def front(b, q, first):
                    nb = 32 if kname == "l2x_k" else 16
                    pe.wait_ge(sig[f"ctx_landed{q}"], seen.up(f"ctx_landed{q}", nb))
                    if not (first and isinstance(b, int) and b < 2):
                        pe.wait_ge(sig["xu_taken"], seen.up("xu_taken"))
                    m = pe.matmul(PS[:, 0, 0:KEYS], w(kname), c_T[q][:, 0:KEYS], start=True, stop=True)
                    m.then_inc(sig["xk_ready"], 1)
                    if not (isinstance(b, int) and b == 0):
                        pe.wait_ge(sig["xv_taken"], seen.up("xv_taken"))
                    for c in range(2):
                        pe.matmul(PS[:, 1, P * c:P * c + P], c_T[q][:, P * c:P * c + P], w(vname),
                                  start=True, stop=True)
                    m = pe.matmul(PS[0:4, 1, 256:384], c_T[q][:, 256:260], w(vname), start=True, stop=True)
                    m.then_inc(sig["xv_ready"], 1)
                    pe.wait_ge(sig["xk_taken"], seen.up("xk_taken"))
                    pe.wait_ge(sig["xqb"], seen.up("xqb"))
                    if not (isinstance(b, int) and b == 0):
                        pe.wait_ge(sig["xexp"], seen.up("xexp"))
                    for g in range(HG):
                        m = pe.matmul(PS[:, 2 + g, 0:KEYS], x_qb[q][:, P * g:P * g + P], x_k[q],
                                      start=True, stop=True)
                    m.then_inc(sig["xs_ready"], 1)

                def back(b, q, first):
                    pe.wait_ge(sig["xp_ready"], seen.up("xp_ready"))
                    for c in range(2):
                        for g in range(HG):
                            pe.transpose(PS[:, 6 + c, P * g:P * g + P], x_p[q][:, g, P * c:P * c + P], ident)
                    m = pe.transpose(PS[0:4, 0, 257:385], x_p[q][:, :, 256], ident)
                    m.then_inc(sig["xpt_ready"], 1)
                    pe.wait_ge(sig["xpt_a"], seen.up("xpt_a"))
                    pe.wait_ge(sig["xpt_d"], seen.up("xpt_d"))
                    for g in range(HG):
                        for c in range(2):
                            pe.matmul(PS[32 * g:32 * g + 32, 0, 384:512], x_v[q][:, c, 32 * g:32 * g + 32],
                                      x_pt[q][:, c, P * g:P * g + P], start=(c == 0), stop=False,
                                      skip_group_check=True)
                    m = pe.matmul(PS[:, 0, 384:512], x_vl[q][0:4, :], x_pl[q][0:4, :], start=False, stop=True,
                                  skip_group_check=True)
                    m.then_inc(sig["xu_ready"], 1)
                seen.skewed(B, {f"ctx_landed{q}": 32 if kname == "l2x_k" else 16 for q in range(2)} |
                         {k: 2 for k in "xu_taken xv_taken xk_taken xqb xexp xp_ready xpt_a xpt_d".split()}, None, front, back)
                seen.up("xexp")
                seen.up("xv_taken")
                pe.wait_ge(sig["xu_taken"], seen.up("xu_taken", 2))
                pe.wait_ge(sig["x_out"], seen.up("x_out", B))

            pe.wait_ge(sig["w_l2"], 16)
            turn(XN)
            wide(2, w("l2x_q"), XNT).then_inc(sig["xq_mm"], 1)
            cross("l2x_k", "l2x_v")
            project(OT, w("l2x_o"))
            turn(Z, "stream_ready")
            ff("l2x", ZT)

            turn(XN)
            for name in ("l2a_q", "l2a_k", "l2a_v"):
                for cc in range(2):
                    if not (name == "l2a_q" and cc == 0):
                        pe.wait_ge(sig["pair_taken"], seen.up("pair_taken"))
                    for c in range(8):
                        for u in range(4):
                            m = pe.matmul(PS[32 * u:32 * u + 32, c // 2, 256 * (c % 2):256 * (c % 2) + 256],
                                          w(name)[:, 32 * (8 * cc + c):32 * (8 * cc + c) + 32],
                                          XNT[:, 256 * u:256 * u + 256], start=True, stop=True)
                    m.then_inc(sig["pair_ready"], 1)
            pe.wait_ge(sig["pair_taken"], seen.up("pair_taken"))
            core()
            big = c_big.rearrange("p (m j r c) -> p m j r c", m=32, j=4, r=2)
            for c in range(H):
                for u in range(4):
                    r = slice(32 * u, 32 * u + 32)
                    rhs = big[r, :, :, :, c].rearrange("p m j r -> p (m j) r")
                    m = pe.matmul(PS[:, 4 + u, 0:256], w("l2a_o")[r, P * c:P * c + P], rhs,
                                  start=(c == 0), stop=(c == H - 1))
            m.then_inc(sig["lin_ready"], 1)
            pe.wait_ge(sig["lin_taken"], seen.up("lin_taken"))
            for t in range(NT):
                m = pe.transpose(PS[:, 2 + t // 4, 128 * (t % 4):128 * (t % 4) + 128], ZT[:, P * t:P * t + P], ident)
            m.then_inc(sig["proj_ready"], 1)
            turn(Z)
            wide(2, w("l2a_w1"), ZT).then_inc(sig["lin_ready"], 1)
            pe.wait_ge(sig["lin_taken"], seen.up("lin_taken"))
            project(OT, w("l2a_w2"))

            def moe_round(r):
                turn(XN) if r == 0 else turn(Y, "stream_ready")
                src = XNT if r == 0 else ZT
                for t in range(NT):
                    m = pe.matmul(PS[:, 6, 4 * t:4 * t + 4], src[:, P * t:P * t + P],
                                  w("l2f_gate")[:, 4 * r:4 * r + 4], start=True, stop=True)
                m.then_inc(sig["gate_mm"], 1)
                ff("l2f", src)
            for r in range(4):
                moe_round(r)

            pe.wait_ge(sig["w_l3"], 16)
            turn(XN)
            wide(2, w("l3x_q"), XNT).then_inc(sig["xq_mm"], 1)
            cross("l3x_k", "l3x_v")
            project(OT, w("l3x_o"))
            self_attention("l3a_q", "l3a_k", "l3a_v", "l3a_o")
            turn(XN)
            wide(6, w("l3f_u1"), XNT).then_inc(sig["lin_ready"], 1)
            pe.wait_ge(sig["lin_taken"], seen.up("lin_taken"))
            ff("l3f", f_pt)
            turn(ACC, None)
            project(ZT, w("l3f_v2"))

        @block.scalar
        def _(act):
            seen = Tally(act)

            def f(o, i, fn=ACT.Identity, **k):
                return act.activation(o, i, fn, **k)

            def norm_std():
                act.wait_ge(sig["var_ready"], seen.up("var_ready"))
                f(SD[:, 1, :], SD[:, 0, :], ACT.Sqrt).then_inc(sig["std_ready"], 1)
                act.wait_ge(sig["std_ready"], seen.up("std_ready"))

            def turned(dst):
                act.wait_ge(sig["turned"], seen.up("turned"))
                act.copy(dst, PSF[:, 0:TOK]).then_inc(sig["turned_taken"], 1)
                act.wait_ge(sig["turned_taken"], seen.up("turned_taken"))

            def ff(layer, rows=None):
                gated, fn, _ = LAYERS_FF[layer]
                nu = FF_UNITS[layer][1]

                def half(q, hh, landed=False):
                    if gated:
                        for c in range(2):
                            act.wait_ge(sig["up_ready"], seen.up("up_ready"))
                            if not landed:
                                act.wait_ge(sig["h_ready"], seen.up("h_ready"))
                            f(f_s[c], PS[:, 2 * c, :], fn).then_inc(sig["act_half"], 1)
                            act.wait_ge(sig["act_half"], seen.up("act_half"))
                        return
                    for c in range(2):
                        act.wait_ge(sig["up_ready"], seen.up("up_ready"))
                        if c == 0 and not landed:
                            act.wait_ge(sig["down_ready"], seen.up("down_ready"))
                        f(f_h[hh][:, c, :], PS[:, 2 * c, :], fn,
                                 bias=WB[:, q, 3 * UNIT + c:3 * UNIT + c + 1]).then_inc(sig["h_ready"], 1)
                        act.wait_ge(sig["h_ready"], seen.up("h_ready"))
                half(0, 0, True)
                half(0, 1, not gated)
                trips = (nu - 2) // 2
                if trips > 0:
                    def body(i):
                        for q in (1, 0):
                            for hh in range(2):
                                half(q, hh)
                    per = {"up_ready": 8, "act_half": 8, "h_ready": 8} if gated else \
                        {"up_ready": 8, "h_ready": 8, "down_ready": 4}
                    seen.loop(trips, per, body)
                half(1, 0)
                half(1, 1)
                if nu % 2:
                    half(0, 0)
                    half(0, 1)
                if gated:
                    seen.up("h_ready", 2)
                    seen.up("down_ready", 2 * nu)
                else:
                    seen.up("down_ready", 2)

            act.wait_ge(sig["w_first"], 16)
            norm_std()
            turned(XNT[:, :])
            act.wait_ge(sig["lin_ready"], seen.up("lin_ready"))
            f(l0_qt, PSF[:, 1024:2048], bias=col("l0x_bq")).then_inc(sig["lin_taken"], 1)
            act.wait_ge(sig["lin_taken"], seen.up("lin_taken"))
            act.wait_ge(sig["lin_ready"], seen.up("lin_ready"))
            f(l0_qp, PSF[:, 2048:3072], scale=float(P) ** -0.5).then_inc(sig["l0s_q_ready"], 1)
            act.wait_ge(sig["l0s_q_ready"], seen.up("l0s_q_ready"))

            def l0_exp(s, q, first):
                act.wait_ge(sig["l0s_max"], seen.up("l0s_max"))
                if not (isinstance(s, int) and s < 2):
                    act.wait_ge(sig["l0s_pt"], seen.up("l0s_pt"))
                f(l0_p[q], PS[:, 0, 0:KEYS], ACT.Exp, bias=l0_neg[q], accum_out=l0_sum[q]).then_inc(sig["l0s_exp"], 1)
                act.wait_ge(sig["l0s_exp"], seen.up("l0s_exp"))
            l0_exp(0, 0, True)
            l0_exp(1, 1, True)
            seen.loop(L0X_STEPS // 2 - 1, {"l0s_max": 2, "l0s_pt": 2, "l0s_exp": 2},
                   lambda i: (l0_exp(None, 0, False), l0_exp(None, 1, False)))
            seen.up("l0s_pt", 2)
            act.wait_ge(sig["lin_ready"], seen.up("lin_ready"))
            f(l0_ct, PSF[:, 2048:3072], bias=col("l0x_bv")).then_inc(sig["lin_taken"], 1)
            act.wait_ge(sig["lin_taken"], seen.up("lin_taken"))

            norm_std()
            turned(XNT[:, :])
            le = ar(2048, 2048).rearrange("p (t n) -> p t n", t=NT)
            lv = ar(4096, 1024).rearrange("p (t n) -> p t n", t=NT)
            lg = ar(5120, 1024).rearrange("p (t n) -> p t n", t=NT)
            act.wait_ge(sig["l0a_mm"], seen.up("l0a_mm", NT))
            f(le, PS[:, :, 0:256], ACT.Exp).then_inc(sig["act_ran"], 1)
            act.wait_ge(sig["act_ran"], seen.up("act_ran"))
            act.copy(lv, PS[:, :, 256:384]).then_inc(sig["act_ran"], 1)
            act.wait_ge(sig["act_ran"], seen.up("act_ran"))
            f(lg, PS[:, :, 384:512], ACT.Silu).then_inc(sig["l0a_act"], 1)
            act.wait_ge(sig["l0a_act"], seen.up("l0a_act"))
            norm_std()
            turned(ZT[:, :])

            norm_std()
            turned(XNT[:, :])
            act.wait_ge(sig["gate_mm"], seen.up("gate_mm"))
            f(g_e, PS[:, 6, 0:64], ACT.Sigmoid).then_inc(sig["gate_act"], 1)
            act.wait_ge(sig["gate_act"], seen.up("gate_act"))
            ff("l0f")

            for k in range(8):
                act.wait_ge(sig["y_w_ready"], seen.up("y_w_ready"))
                if k < 4:
                    dst, sc = y_A[:, 4 * k:4 * k + 4, :], float(DH1) ** -0.5
                else:
                    dst, sc = y_M[:, 4 * k - 16:4 * k - 12, :], 1.0
                f(dst, PS[:, k, :].rearrange("p (h n) -> p h n", h=4), scale=sc).then_inc(sig["y_w_taken"], 1)
                act.wait_ge(sig["y_w_taken"], seen.up("y_w_taken"))
            norm_std()
            turned(XNT[:, :])

            def y_q(q):
                act.wait_ge(sig["yq_ready"], seen.up("yq_ready"))
                act.copy(y_Q[q], PS[:, 0, :]).then_inc(sig["yq_taken"], 1)
                act.wait_ge(sig["yq_taken"], seen.up("yq_taken"))

            def y_exp(b, q, first):
                act.wait_ge(sig["yclip"], seen.up("yclip"))
                if not (first and isinstance(b, int) and b < 2):
                    act.wait_ge(sig["yu_ready"], seen.up("yu_ready"))
                f(y_P[q][:, 0:2, :], y_C[:, 0:2, :], ACT.Exp).then_inc(sig["act_ran"], 1)
                act.wait_ge(sig["act_ran"], seen.up("act_ran"))
                f(y_P[q][0:1, 2, :], y_C[0:1, 2, :], ACT.Exp).then_inc(sig["yexp"], 1)
                act.wait_ge(sig["yexp"], seen.up("yexp"))

            def y_t(b, q, first):
                act.wait_ge(sig["yt_ready"], seen.up("yt_ready"))
                if not (isinstance(b, int) and b == 0):
                    act.wait_ge(sig["yo_ready"], seen.up("yo_ready"))
                act.copy(y_V, PS[:, 6, :]).then_inc(sig["yt_taken"], 1)
                act.wait_ge(sig["yt_taken"], seen.up("yt_taken"))
            y_q(0)
            y_exp(0, 0, True)
            y_q(1)
            y_exp(1, 1, True)
            y_t(0, 0, True)

            def y_body(i):
                for k in range(2):
                    y_q(k)
                    y_exp(None, k, False)
                    y_t(None, 1 - k, False)
            seen.loop(B // 2 - 1, {"yq_ready": 2, "yq_taken": 2, "yclip": 2, "yu_ready": 2, "act_ran": 2, "yexp": 2,
                                "yt_ready": 2, "yo_ready": 2, "yt_taken": 2}, y_body)
            y_t(None, 1, False)
            seen.up("yu_ready", 2)
            seen.up("yo_ready")

            def core():
                for half in range(2):
                    act.wait_ge(sig["c_shift"], seen.up("c_shift"))
                    f(c_p, c_p, ACT.Exp).then_inc(sig["c_exp"], 1)
                    act.wait_ge(sig["c_exp"], seen.up("c_exp"))
                    act.wait_ge(sig["c_pt"], seen.up("c_pt"))
                    if half:
                        act.wait_ge(sig["c_pv"], seen.up("c_pv", 0))
                    act.copy(c_pt, PSF[:, 2048:4096]).then_inc(sig["c_pt_taken"], 1)
                    act.wait_ge(sig["c_pt_taken"], seen.up("c_pt_taken"))
                    seen.up("c_pv")

            def self_attention(scale, second_norm=False):
                norm_std()
                turned(XNT[:, :])
                act.wait_ge(sig["lin_ready"], seen.up("lin_ready"))
                f(c_q, PSF[:, 1024:2048], scale=scale).then_inc(sig["act_ran"], 1)
                act.wait_ge(sig["act_ran"], seen.up("act_ran"))
                act.copy(c_k, PSF[:, 2048:3072]).then_inc(sig["act_ran"], 1)
                act.wait_ge(sig["act_ran"], seen.up("act_ran"))
                act.copy(c_v, PSF[:, 3072:4096]).then_inc(sig["qkv_taken"], 1)
                act.wait_ge(sig["qkv_taken"], seen.up("qkv_taken"))
                if second_norm:
                    norm_std()
                core()

            self_attention(float(DK) ** -0.5)

            norm_std()
            turned(XNT[:, :])
            act.wait_ge(sig["gate_mm"], seen.up("gate_mm"))
            f(g_h[0:64, :], PSF[0:64, 1024:2048], ACT.Relu, bias=col("l1f_dpb1")[0:64, :]).then_inc(sig["gate_hidden"], 1)
            act.wait_ge(sig["gate_hidden"], seen.up("gate_hidden"))
            act.wait_ge(sig["gate_entropy"], seen.up("gate_entropy"))
            f(g_z[:, 2, :], g_z[:, 1, :], ACT.Exp, scale=-1.0).then_inc(sig["gate_act"], 1)
            act.wait_ge(sig["gate_act"], seen.up("gate_act"))
            f(g_z[:, 3, :], g_z[:, 2, :], ACT.Ln, bias=SM[:, 500:501]).then_inc(sig["gate_act"], 1)
            act.wait_ge(sig["gate_act"], seen.up("gate_act"))
            act.wait_ge(sig["gate_shift"], seen.up("gate_shift"))
            f(g_e[:, 0:32], g_e[:, 0:32], ACT.Exp).then_inc(sig["gate_act"], 1)
            act.wait_ge(sig["gate_act"], seen.up("gate_act"))
            ff("l1f")

            def cross(bk):
                def kt(q):
                    act.wait_ge(sig["xk_ready"], seen.up("xk_ready"))
                    bias = col(bk) if bk else 0.0
                    (f(x_k[q], PS[:, 0, 0:KEYS], bias=bias) if bk else act.copy(x_k[q], PS[:, 0, 0:KEYS])).then_inc(sig["xk_taken"], 1)
                    act.wait_ge(sig["xk_taken"], seen.up("xk_taken"))

                def front(b, q, first):
                    kt(q)
                    act.wait_ge(sig["xmax"], seen.up("xmax"))
                    for g in range(HG):
                        src = x_s[:, g, :] if not bk else PS[:, 2 + g, 0:KEYS]
                        ins = f(x_p[q][:, g, :], src, ACT.Exp, bias=x_neg[q][:, g:g + 1],
                                accum_out=x_sum[q][:, g:g + 1])
                        name = "xexp" if g == HG - 1 else "act_ran"
                        ins.then_inc(sig[name], 1)
                        act.wait_ge(sig[name], seen.up(name))

                def back(b, q, first):
                    act.wait_ge(sig["xpt_ready"], seen.up("xpt_ready"))
                    if not (first and isinstance(b, int) and b < 2):
                        act.wait_ge(sig["xu_ready"], seen.up("xu_ready"))
                    act.copy(x_pt[q][:, 0, :], PS[:, 6, :]).then_inc(sig["xpt_a"], 1)
                    act.wait_ge(sig["xpt_a"], seen.up("xpt_a"))
                seen.skewed(B, {"act_ran": 6} | {k: 2 for k in "xk_ready xk_taken xmax xexp xpt_ready xu_ready xpt_a".split()},
                         None, front, back)
                seen.up("xu_ready", 2)

            norm_std()
            turned(XNT[:, :])
            cross(None)
            norm_std()
            turned(ZT[:, :])
            ff("l2x")
            norm_std()

            norm_std()
            turned(XNT[:, :])
            core()
            act.wait_ge(sig["lin_ready"], seen.up("lin_ready"))
            act.copy(ZT[:, :].rearrange("p (u n) -> p u n", u=4), PS[:, 4:8, 0:256]).then_inc(sig["lin_taken"], 1)
            act.wait_ge(sig["lin_taken"], seen.up("lin_taken"))
            norm_std()
            turned(ZT[:, :])
            act.wait_ge(sig["lin_ready"], seen.up("lin_ready"))
            f(OT[:, :], PSF[:, 1024:2048], bias=col("l2a_b1")).then_inc(sig["lin_taken"], 1)
            act.wait_ge(sig["lin_taken"], seen.up("lin_taken"))
            norm_std()

            norm_std()
            for r in range(4):
                turned(XNT[:, :] if r == 0 else ZT[:, :])
                act.wait_ge(sig["gate_shift"], seen.up("gate_shift"))
                f(g_e[:, 0:32], g_e[:, 0:32], ACT.Exp).then_inc(sig["gate_act"], 1)
                act.wait_ge(sig["gate_act"], seen.up("gate_act"))
                ff("l2f")

            norm_std()
            turned(XNT[:, :])
            cross("l3x_bk")
            self_attention(float(DK) ** -0.5, True)
            norm_std()
            turned(XNT[:, :])
            act.wait_ge(sig["lin_ready"], seen.up("lin_ready"))
            act.copy(f_pt, PSF[:, 3072:4096]).then_inc(sig["lin_taken"], 1)
            act.wait_ge(sig["lin_taken"], seen.up("lin_taken"))
            ff("l3f")
            turned(ZT[:, :])

        @block.vector
        def _(dve):
            seen = Tally(dve)

            def tt(o, a, b, op):
                return dve.tensor_tensor(o, a, b, op)

            def layernorm(src, dst, eps, signal=True):
                for t in range(NT):
                    dve.bn_stats(ST[:, t, :], src[:, t, :]).then_inc(sig["dve_ran"], 1)
                    seen.up("dve_ran")
                    if t == NT - 1:
                        dve.wait_ge(sig["dve_ran"], seen.up("dve_ran", 0))
                for t in range(NT):
                    dve.bn_aggr(MV[:, t, :], ST[:, t, :]).then_inc(sig["dve_ran"], 1)
                    seen.up("dve_ran")
                    if t == NT - 1:
                        dve.wait_ge(sig["dve_ran"], seen.up("dve_ran", 0))
                dve.tensor_scalar(SD[:, 0, :], MV[:, :, 1], eps, None, ALU.add).then_inc(sig["var_ready"], 1)
                dve.wait_ge(sig["var_ready"], seen.up("var_ready"))
                dve.wait_ge(sig["std_ready"], seen.up("std_ready"))
                dve.reciprocal(SD[:, 1, :], SD[:, 1, :]).then_inc(sig["dve_ran"], 1)
                dve.wait_ge(sig["dve_ran"], seen.up("dve_ran"))
                for t in range(NT):
                    ins = dve.tensor_scalar(dst[:, t, :], src[:, t, :], MV[:, t, 0:1], SD[:, 1, t:t + 1],
                                            ALU.subtract, ALU.mult)
                    name = "norm_ready" if signal else "dve_ran"
                    ins.then_inc(sig[name], 1)
                    seen.up(name)
                    if t == NT - 1:
                        dve.wait_ge(sig[name], seen.up(name, 0))

            def affine(dst, g, b):
                tt(dst, dst, rows_t(g), ALU.mult).then_inc(sig["dve_ran"], 1)
                dve.wait_ge(sig["dve_ran"], seen.up("dve_ran"))
                return tt(dst, dst, rows_t(b), ALU.add)

            def residual():
                dve.wait_ge(sig["proj_ready"], seen.up("proj_ready"))
                tt(flat(X), PSF[:, 3072:4096], flat(X), ALU.add).then_inc(sig["resid_done"], 1)
                dve.wait_ge(sig["resid_done"], seen.up("resid_done"))

            def rank_gates(E, low):
                pairs = NT * E * E
                v = lambda a: a[:, 0:pairs].rearrange("p (t e j) -> p t e j", t=NT, e=E)
                gl = g_l[:, 0:NT * E].rearrange("p (t e) -> p t e", t=NT)
                other = gl.unsqueeze(2).broadcast_to([P, NT, E, E])
                own = gl.unsqueeze(3).broadcast_to([P, NT, E, E])
                lw = low.rearrange("p (e j) -> p e j", e=E).unsqueeze(1).broadcast_to([P, NT, E, E])
                tt(v(g_a), other, own, ALU.is_equal).then_inc(sig["dve_ran"], 1)
                dve.wait_ge(sig["dve_ran"], seen.up("dve_ran"))
                tt(v(g_a), v(g_a), lw, ALU.mult).then_inc(sig["dve_ran"], 1)
                dve.wait_ge(sig["dve_ran"], seen.up("dve_ran"))
                tt(v(g_b), other, own, ALU.is_gt).then_inc(sig["dve_ran"], 1)
                dve.wait_ge(sig["dve_ran"], seen.up("dve_ran"))
                tt(v(g_a), v(g_a), v(g_b), ALU.add).then_inc(sig["dve_ran"], 1)
                dve.wait_ge(sig["dve_ran"], seen.up("dve_ran"))
                rk = g_rank[:, 0:NT * E]
                dve.tensor_reduce(rk, g_a[:, 0:pairs].rearrange("p (m j) -> p m j", j=E), AX, ALU.add).then_inc(sig["dve_ran"], 1)
                dve.wait_ge(sig["dve_ran"], seen.up("dve_ran"))

            def share(E, weights):
                rk = g_rank[:, 0:NT * E].rearrange("p (t e) -> p t e", t=NT)
                we = weights[:, 0:NT * E].rearrange("p (t e) -> p t e", t=NT)
                tt(rk, rk, we, ALU.mult).then_inc(sig["dve_ran"], 1)
                dve.wait_ge(sig["dve_ran"], seen.up("dve_ran"))
                dve.tensor_reduce(g_m, rk, AX, ALU.add).then_inc(sig["dve_ran"], 1)
                dve.wait_ge(sig["dve_ran"], seen.up("dve_ran"))
                dve.reciprocal(g_m, g_m).then_inc(sig["dve_ran"], 1)
                dve.wait_ge(sig["dve_ran"], seen.up("dve_ran"))
                tt(f_w[:, :, 0:E], rk, g_m.unsqueeze(2).broadcast_to([P, NT, E]), ALU.mult).then_inc(sig["expert_weights"], 1)
                dve.wait_ge(sig["expert_weights"], seen.up("expert_weights"))

            def softmax_gates():
                gl = g_l[:, 0:32].rearrange("p (t e) -> p t e", t=NT)
                ge = g_e[:, 0:32].rearrange("p (t e) -> p t e", t=NT)
                dve.tensor_reduce(g_m, gl, AX, ALU.max).then_inc(sig["dve_ran"], 1)
                dve.wait_ge(sig["dve_ran"], seen.up("dve_ran"))
                tt(ge, gl, g_m.unsqueeze(2).broadcast_to([P, NT, 4]), ALU.subtract).then_inc(sig["gate_shift"], 1)
                dve.wait_ge(sig["gate_shift"], seen.up("gate_shift"))

            def ff(layer):
                gated, _, weighed = LAYERS_FF[layer]
                u0, nu = FF_UNITS[layer]

                def hidden(hh):
                    for c in range(2):
                        dve.wait_ge(sig["act_half"], seen.up("act_half"))
                        tt(f_h[hh][:, c, :], PS[:, 2 * c + 1, :], f_s[c], ALU.mult).then_inc(sig["h_ready"], 1)
                        dve.wait_ge(sig["h_ready"], seen.up("h_ready"))

                def add(e, hh):
                    dve.wait_ge(sig["down_ready"], seen.up("down_ready"))
                    for t in range(4):
                        y = PS[:, 4 + hh, 128 * t:128 * t + 128]
                        a = ACC[:, 4 * hh + t, :]
                        if weighed:
                            ins = dve.scalar_tensor_tensor(out=a, in0=y, scalar=f_w[:, 4 * hh + t, bass.ds(e, 1)],
                                                           in1=a, op0=ALU.mult, op1=ALU.add)
                        else:
                            ins = tt(a, y, a, ALU.add)
                        name = "down_used" if t == 3 else "dve_ran"
                        ins.then_inc(sig[name], 1)
                        seen.up(name)
                        if t == 3:
                            dve.wait_ge(sig[name], seen.up(name, 0))

                def unit(e):
                    for hh in range(2):
                        hidden(1 - hh)
                        add(e, hh)
                if gated:
                    hidden(0)
                    unit(8)
                    seen.loop(3, {"act_half": 8, "h_ready": 8, "down_ready": 4, "down_used": 4, "dve_ran": 12},
                           lambda i: (unit(i * 2), unit(i * 2 + 1)))
                    unit(6)
                    hidden(1)
                    add(7, 0)
                    add(7, 1)
                else:
                    per = {"down_ready": 4, "down_used": 4, "dve_ran": 12}
                    if layer == "l2f":
                        seen.loop(nu // 2, per, lambda i: [add(i, hh) for q in range(2) for hh in range(2)])
                    elif layer == "l1f":
                        seen.loop(nu // 2, per, lambda i: [add(i * 2 + q, hh) for q in range(2) for hh in range(2)])
                    else:
                        for q in range(2):
                            for hh in range(2):
                                add(None, hh)

            dve.memset(SM[:, 500:501], 1.0).then_inc(sig["dve_ran"], 1)
            dve.wait_ge(sig["dve_ran"], seen.up("dve_ran"))

            dve.wait_ge(sig["x_landed"], 16)
            dve.wait_ge(sig["w_first"], 16)
            layernorm(X, XN, LN_EPS)

            def l0_norm(s, q):
                dve.wait_ge(sig["l0s_exp"], seen.up("l0s_exp"))
                dve.reciprocal(l0_sum[q], l0_sum[q]).then_inc(sig["dve_ran"], 1)
                dve.wait_ge(sig["dve_ran"], seen.up("dve_ran"))
                dve.tensor_scalar(l0_p[q], l0_p[q], l0_sum[q], None, ALU.mult).then_inc(sig["l0s_probs"], 1)
                dve.wait_ge(sig["l0s_probs"], seen.up("l0s_probs"))

            def l0_front(s, q, first):
                dve.wait_ge(sig["l0s_scores"], seen.up("l0s_scores"))
                dve.tensor_reduce(l0_neg[q], PS[:, 0, 0:KEYS], AX, ALU.max, negate=True).then_inc(sig["l0s_max"], 1)
                dve.wait_ge(sig["l0s_max"], seen.up("l0s_max"))
                l0_norm(s, q)

            def l0_back(s, q, first):
                dve.wait_ge(sig["l0s_pt"], seen.up("l0s_pt"))
                dve.tensor_copy(l0_pt[q][:, 0:2, :], PS[:, 1, 0:256].rearrange("p (c n) -> p c n", c=2)).then_inc(sig["dve_ran"], 1)
                dve.wait_ge(sig["dve_ran"], seen.up("dve_ran"))
                dve.tensor_copy(l0_pt[q][0:1, 2, :], PS[0:1, 1, 256:384]).then_inc(sig["l0s_pt_taken"], 1)
                dve.wait_ge(sig["l0s_pt_taken"], seen.up("l0s_pt_taken"))
                dve.wait_ge(sig["l0s_u"], seen.up("l0s_u"))
                dve.tensor_scalar(l0_ut[:, bass.ds(s * P, P)], PS[:, 2, 0:P], 1.0, None, ALU.mult).then_inc(sig["l0s_u_taken"], 1)
                dve.wait_ge(sig["l0s_u_taken"], seen.up("l0s_u_taken"))
            seen.skewed(L0X_STEPS, {"dve_ran": 4} | {k: 2 for k in "l0s_exp l0s_probs l0s_scores l0s_max l0s_pt "
                                                  "l0s_pt_taken l0s_u l0s_u_taken".split()},
                     None, l0_front, l0_back)
            dve.wait_ge(sig["bias_ready"], seen.up("bias_ready"))
            residual()

            layernorm(X, XN, LN_EPS)
            dve.wait_ge(sig["w_l0"], 16)
            dve.wait_ge(sig["rows_landed"], 16)
            lq = ar(0, 2048).rearrange("p (t n) -> p t n", t=NT)
            le = ar(2048, 2048).rearrange("p (t n) -> p t n", t=NT)
            lv = ar(4096, 1024)
            lg = ar(5120, 1024)
            dve.wait_ge(sig["l0a_mm"], seen.up("l0a_mm", NT))
            dve.wait_ge(sig["l0a_act"], seen.up("l0a_act"))
            dve.tensor_scalar(lq, PS[:, :, 0:256], 0.0, None, ALU.max).then_inc(sig["dve_ran"], 1)
            dve.wait_ge(sig["dve_ran"], seen.up("dve_ran"))
            for hh in range(2):
                s = slice(1024 * hh, 1024 * hh + 1024)
                dve.scalar_tensor_tensor(out=ar(0, 2048)[:, s], in0=ar(2048, 2048)[:, s], scalar=1.0,
                                                in1=ar(0, 2048)[:, s], op0=ALU.min, op1=ALU.add).then_inc(sig["l0a_qk"], 1)
                dve.wait_ge(sig["l0a_qk"], seen.up("l0a_qk"))
            qk = ar(2048, 1024)
            qs = ar(3072, 1024)
            v3 = lambda a: a.rearrange("p (t n) -> p t n", t=NT)
            tt(v3(qk), lq[:, :, 0:128], lq[:, :, 128:256], ALU.mult).then_inc(sig["dve_ran"], 1)
            dve.wait_ge(sig["dve_ran"], seen.up("dve_ran"))
            r1, r2 = SM[:, 600:728], SM[:, 728:856]
            dve.tensor_reduce(r1, qk.rearrange("p (m d) -> p m d", d=DK), AX, ALU.add).then_inc(sig["dve_ran"], 1)
            dve.wait_ge(sig["dve_ran"], seen.up("dve_ran"))
            dve.wait_ge(sig["l0a_ksum"], seen.up("l0a_ksum"))
            tt(v3(qs), PSF[:, 0:1024].rearrange("p (t n) -> p t n", t=NT), lq[:, :, 0:128], ALU.mult).then_inc(sig["dve_ran"], 1)
            dve.wait_ge(sig["dve_ran"], seen.up("dve_ran"))
            dve.tensor_reduce(r2, qs.rearrange("p (m d) -> p m d", d=DK), AX, ALU.add).then_inc(sig["dve_ran"], 1)
            dve.wait_ge(sig["dve_ran"], seen.up("dve_ran"))
            dve.tensor_scalar(r2, r2, 1e-6, None, ALU.add).then_inc(sig["dve_ran"], 1)
            dve.wait_ge(sig["dve_ran"], seen.up("dve_ran"))
            dve.reciprocal(r2, r2).then_inc(sig["dve_ran"], 1)
            dve.wait_ge(sig["dve_ran"], seen.up("dve_ran"))
            tt(r1, r1, r2, ALU.mult).then_inc(sig["dve_ran"], 1)
            dve.wait_ge(sig["dve_ran"], seen.up("dve_ran"))
            tt(lv.rearrange("p (m d) -> p m d", d=DK), lv.rearrange("p (m d) -> p m d", d=DK),
                   r1.unsqueeze(2).broadcast_to([P, 128, DK]), ALU.mult).then_inc(sig["dve_ran"], 1)
            dve.wait_ge(sig["dve_ran"], seen.up("dve_ran"))
            layernorm(v3(lv), Z, 1e-5, signal=False)
            affine(Z[:, :, :], "l0a_gamma", "l0a_beta").then_inc(sig["dve_ran"], 1)
            dve.wait_ge(sig["dve_ran"], seen.up("dve_ran"))
            tt(flat(Z), flat(Z), lg, ALU.mult).then_inc(sig["stream_ready"], 1)
            dve.wait_ge(sig["stream_ready"], seen.up("stream_ready"))
            residual()

            layernorm(X, XN, LN_EPS)
            seen.up("gate_mm")
            dve.wait_ge(sig["gate_act"], seen.up("gate_act"))
            dve.tensor_copy(g_l, g_e).then_inc(sig["dve_ran"], 1)
            dve.wait_ge(sig["dve_ran"], seen.up("dve_ran"))
            rank_gates(8, w("rank_low8"))
            dve.tensor_scalar(g_rank, g_rank, 2.0, None, ALU.is_lt).then_inc(sig["dve_ran"], 1)
            dve.wait_ge(sig["dve_ran"], seen.up("dve_ran"))
            share(8, g_e)
            dve.tensor_scalar(f_w[:, :, 0:8], f_w[:, :, 0:8], 1.0 / 3.0, None, ALU.mult).then_inc(sig["dve_ran"], 1)
            dve.wait_ge(sig["dve_ran"], seen.up("dve_ran"))
            dve.memset(f_w[:, :, 8:9], 1.0 / 3.0).then_inc(sig["dve_ran"], 1)
            dve.wait_ge(sig["dve_ran"], seen.up("dve_ran"))
            dve.memset(flat(ACC), 0.0).then_inc(sig["dve_ran"], 1)
            dve.wait_ge(sig["dve_ran"], seen.up("dve_ran"))
            ff("l0f")
            tt(flat(X), flat(X), flat(ACC), ALU.add).then_inc(sig["resid_done"], 1)
            dve.wait_ge(sig["resid_done"], seen.up("resid_done"))

            layernorm(X, XN, LN_EPS)
            dve.wait_ge(sig["mask_landed"], seen.up("mask_landed", 32))
            dve.tensor_scalar(y_hi[:, 0:2, :], MK[:, 0:2, :], 10.0, -5.0, ALU.mult, ALU.add).then_inc(sig["dve_ran"], 1)
            dve.wait_ge(sig["dve_ran"], seen.up("dve_ran"))
            dve.tensor_scalar(y_hi[0:1, 2, :], MK[0:1, 2, :], 10.0, -5.0, ALU.mult, ALU.add).then_inc(sig["dve_ran"], 1)
            dve.wait_ge(sig["dve_ran"], seen.up("dve_ran"))

            def y_clip(b, q, first):
                dve.wait_ge(sig["ys_ready"], seen.up("ys_ready"))
                if not (isinstance(b, int) and b == 0):
                    dve.wait_ge(sig["yexp"], seen.up("yexp"))
                for c in range(3):
                    r = slice(0, P) if c < 2 else slice(0, 1)
                    ins = dve.tensor_scalar(y_C[r, c, :], PS[r, 1 + c, :], -5.0, y_hi[r, c, bass.ds(b, 1)],
                                            ALU.max, ALU.min)
                    name = "yclip" if c == 2 else "dve_ran"
                    ins.then_inc(sig[name], 1)
                    dve.wait_ge(sig[name], seen.up(name))

            def y_norm(b, q, first):
                dve.wait_ge(sig["yu_ready"], seen.up("yu_ready"))
                if not (isinstance(b, int) and b == 0):
                    dve.wait_ge(sig["yt_ready"], seen.up("yt_ready"))
                u = PS[:, 4:6, 0:2 * FQ].rearrange("p a (g f) -> p a g f", g=2)
                dve.reciprocal(y_r.rearrange("p (a g) -> p a g", a=2), u[:, :, :, P]).then_inc(sig["dve_ran"], 1)
                dve.wait_ge(sig["dve_ran"], seen.up("dve_ran"))
                for a in range(2):
                    ins = tt(y_U[:, 2 * a:2 * a + 2, :], u[:, a, :, 0:P],
                             y_r[:, 2 * a:2 * a + 2].unsqueeze(2).broadcast_to([P, 2, P]), ALU.mult)
                    name = "yu_taken" if a else "dve_ran"
                    ins.then_inc(sig[name], 1)
                    dve.wait_ge(sig[name], seen.up(name))

            def y_out(b):
                dve.wait_ge(sig["yo_ready"], seen.up("yo_ready"))
                dve.tensor_scalar(OT[:, bass.ds(b * 32, 32)], PS[:, 7, 0:32], 1.0, None, ALU.mult).then_inc(sig["yo_taken"], 1)
                dve.wait_ge(sig["yo_taken"], seen.up("yo_taken"))
            y_clip(0, 0, True)
            y_norm(0, 0, True)
            y_clip(1, 1, False)
            y_out(0)

            def y_body(i):
                for k in range(2):
                    y_norm(None, k, False)
                    y_clip(i * 2 + (2 + k), k, False)
                    y_out(i * 2 + (1 + k))
            seen.loop(B // 2 - 1, {"dve_ran": 8} | {k: 2 for k in "ys_ready yexp yclip yu_ready yt_ready yu_taken "
                                                 "yo_ready yo_taken".split()}, y_body)
            y_norm(None, 1, False)
            y_out(B - 1)
            seen.up("yexp")
            seen.up("yt_ready")
            dve.wait_ge(sig["bias_ready"], seen.up("bias_ready"))
            residual()

            def core(kind):
                for half in range(2):
                    v = lambda a: a.rearrange("p (g n k) -> p g n k", g=HG, n=16)
                    dve.wait_ge(sig["c_scores"], seen.up("c_scores"))
                    if half:
                        dve.wait_ge(sig["c_pt"], seen.up("c_pt", 0))
                    ps = PSF[:, 0:2048]
                    if kind == "causal":
                        cz = w("causal").unsqueeze(1).broadcast_to([P, 64, 32])
                        tt(c_p.rearrange("p (m k) -> p m k", k=32), ps.rearrange("p (m k) -> p m k", k=32),
                               cz, ALU.add).then_inc(sig["dve_ran"], 1)
                        dve.wait_ge(sig["dve_ran"], seen.up("dve_ran"))
                        src = c_p
                    else:
                        src = ps
                    s3 = src.rearrange("p (m k) -> p m k", k=32)
                    p3 = c_p.rearrange("p (m k) -> p m k", k=32)
                    dve.tensor_reduce(c_red, s3, AX, ALU.max).then_inc(sig["dve_ran"], 1)
                    dve.wait_ge(sig["dve_ran"], seen.up("dve_ran"))
                    tt(p3, s3, c_red.unsqueeze(2).broadcast_to([P, 64, 32]), ALU.subtract).then_inc(sig["c_shift"], 1)
                    dve.wait_ge(sig["c_shift"], seen.up("c_shift"))
                    dve.wait_ge(sig["c_exp"], seen.up("c_exp"))
                    dve.tensor_reduce(c_red, p3, AX, ALU.add).then_inc(sig["dve_ran"], 1)
                    dve.wait_ge(sig["dve_ran"], seen.up("dve_ran"))
                    dve.reciprocal(c_red, c_red).then_inc(sig["dve_ran"], 1)
                    dve.wait_ge(sig["dve_ran"], seen.up("dve_ran"))
                    out2 = c_p2.rearrange("p (n g k) -> p g n k", n=16, g=HG)
                    for g in range(HG):
                        rg = c_red[:, 16 * g:16 * g + 16].unsqueeze(2).broadcast_to([P, 16, 32])
                        ins = tt(out2[:, g], p3[:, 16 * g:16 * g + 16, :], rg, ALU.mult)
                        if kind != "pairs" and g == HG - 1:
                            ins.then_inc(sig["c_probs"], 1)
                            dve.wait_ge(sig["c_probs"], seen.up("c_probs"))
                        else:
                            ins.then_inc(sig["dve_ran"], 1)
                            dve.wait_ge(sig["dve_ran"], seen.up("dve_ran"))
                    if kind == "pairs":
                        for g in range(HG):
                            o = c_p2.rearrange("p (a m g k) -> p g a m k", a=4, m=4, g=HG)[:, g]
                            bias = c_relb.unsqueeze(1).broadcast_to([P, 4, 4, 32])
                            ins = tt(o, o, bias, ALU.add)
                            name = "c_probs" if g == HG - 1 else "dve_ran"
                            ins.then_inc(sig[name], 1)
                            dve.wait_ge(sig[name], seen.up(name))
                    dve.wait_ge(sig["c_pt"], seen.up("c_pt"))
                    dve.wait_ge(sig["c_pv"], seen.up("c_pv"))
                    dst = c_big[:, 2048 * half:2048 * half + 2048] if kind == "pairs" else c_big[:, 0:2048]
                    m4 = w("mask4").unsqueeze(1).unsqueeze(3).broadcast_to([P, 16, 4, 32])
                    ins = tt(dst.rearrange("p (n h q) -> p n h q", n=16, h=4),
                             ps.rearrange("p (n h q) -> p n h q", n=16, h=4), m4, ALU.mult)
                    if kind == "pairs":
                        ins.then_inc(sig["c_masked"], 1)
                        dve.wait_ge(sig["c_masked"], seen.up("c_masked"))
                    else:
                        ins.then_inc(sig["dve_ran"], 1)
                        dve.wait_ge(sig["dve_ran"], seen.up("dve_ran"))
                        o = OT[:, 512 * half:512 * half + 512].rearrange("p (n q) -> p n q", n=16)
                        dve.tensor_reduce(o, c_big[:, 0:2048].rearrange("p (n h q) -> p n q h", n=16, h=4),
                                                 AX, ALU.add).then_inc(sig["c_masked"], 1)
                        dve.wait_ge(sig["c_masked"], seen.up("c_masked"))

            def heads():
                dve.wait_ge(sig["qkv_taken"], seen.up("qkv_taken"))
                m4 = w("mask4").unsqueeze(1).unsqueeze(3).broadcast_to([P, 32, 4, 32])
                q4 = c_q.rearrange("p (n q) -> p n q", n=32).unsqueeze(2).broadcast_to([P, 32, 4, 32])
                tt(c_qb.rearrange("p (n h q) -> p n h q", n=32, h=4), q4, m4, ALU.mult).then_inc(sig["dve_ran"], 1)
                dve.wait_ge(sig["dve_ran"], seen.up("dve_ran"))
                dve.transpose(c_vt, c_v).then_inc(sig["c_in"], 1)
                dve.wait_ge(sig["c_in"], seen.up("c_in"))

            layernorm(X, XN, LN_EPS)
            dve.wait_ge(sig["w_l1"], 16)
            heads()
            core("causal")
            residual()

            layernorm(X, XN, LN_EPS)
            dve.wait_ge(sig["gate_mm"], seen.up("gate_mm", 2))
            ps = PS[:, 7, 0:NT]
            small = row("small")
            z = lambda j: g_z[:, j, :]
            dve.tensor_scalar(z(0), ps, small[:, SMALL_DPB2:SMALL_DPB2 + 1], None, ALU.add).then_inc(sig["dve_ran"], 1)
            dve.wait_ge(sig["dve_ran"], seen.up("dve_ran"))
            dve.tensor_scalar(z(1), z(0), -1.0, None, ALU.mult).then_inc(sig["dve_ran"], 1)
            dve.wait_ge(sig["dve_ran"], seen.up("dve_ran"))
            tt(z(1), z(0), z(1), ALU.max).then_inc(sig["gate_entropy"], 1)
            dve.wait_ge(sig["gate_entropy"], seen.up("gate_entropy"))
            dve.tensor_scalar(z(0), z(0), 0.0, None, ALU.max).then_inc(sig["dve_ran"], 1)
            dve.wait_ge(sig["dve_ran"], seen.up("dve_ran"))
            dve.wait_ge(sig["gate_act"], seen.up("gate_act", 2))
            tt(z(0), z(0), z(3), ALU.add).then_inc(sig["dve_ran"], 1)
            dve.wait_ge(sig["dve_ran"], seen.up("dve_ran"))
            dve.tensor_scalar(z(0), z(0), 0.5, 1.0 / 1.5, ALU.subtract, ALU.mult).then_inc(sig["dve_ran"], 1)
            dve.wait_ge(sig["dve_ran"], seen.up("dve_ran"))
            dve.tensor_scalar(z(0), z(0), 0.0, 1.0, ALU.max, ALU.min).then_inc(sig["dve_ran"], 1)
            dve.wait_ge(sig["dve_ran"], seen.up("dve_ran"))
            dve.tensor_scalar(z(0), z(0), 3.0, 1.0, ALU.mult, ALU.add).then_inc(sig["dve_ran"], 1)
            dve.wait_ge(sig["dve_ran"], seen.up("dve_ran"))
            dve.tensor_scalar(z(1), z(0), 1.5, 1.0, ALU.is_ge, ALU.add).then_inc(sig["dve_ran"], 1)
            dve.wait_ge(sig["dve_ran"], seen.up("dve_ran"))
            dve.tensor_scalar(z(4), z(0), 2.5, None, ALU.is_gt).then_inc(sig["dve_ran"], 1)
            dve.wait_ge(sig["dve_ran"], seen.up("dve_ran"))
            tt(z(1), z(1), z(4), ALU.add).then_inc(sig["dve_ran"], 1)
            dve.wait_ge(sig["dve_ran"], seen.up("dve_ran"))
            dve.tensor_scalar(z(4), z(0), 3.5, None, ALU.is_ge).then_inc(sig["dve_ran"], 1)
            dve.wait_ge(sig["dve_ran"], seen.up("dve_ran"))
            tt(z(1), z(1), z(4), ALU.add).then_inc(sig["dve_ran"], 1)
            dve.wait_ge(sig["dve_ran"], seen.up("dve_ran"))
            gb = small[:, SMALL_L1GATE:SMALL_L1GATE + 4].unsqueeze(1).broadcast_to([P, NT, 4])
            tt(g_l[:, 0:32].rearrange("p (t e) -> p t e", t=NT),
                   PS[:, 6, 0:32].rearrange("p (t e) -> p t e", t=NT), gb, ALU.add).then_inc(sig["dve_ran"], 1)
            dve.wait_ge(sig["dve_ran"], seen.up("dve_ran"))
            softmax_gates()
            rank_gates(4, w("rank_low4"))
            rk = g_rank[:, 0:32].rearrange("p (t e) -> p t e", t=NT)
            tt(rk, rk, z(1).unsqueeze(2).broadcast_to([P, NT, 4]), ALU.is_lt).then_inc(sig["dve_ran"], 1)
            dve.wait_ge(sig["dve_ran"], seen.up("dve_ran"))
            dve.wait_ge(sig["gate_act"], seen.up("gate_act"))
            share(4, g_e)
            dve.memset(flat(ACC), 0.0).then_inc(sig["dve_ran"], 1)
            dve.wait_ge(sig["dve_ran"], seen.up("dve_ran"))
            ff("l1f")
            tt(flat(X), flat(X), flat(ACC), ALU.add).then_inc(sig["dve_ran"], 1)
            dve.wait_ge(sig["dve_ran"], seen.up("dve_ran"))
            dve.wait_ge(sig["bias_ready"], seen.up("bias_ready"))
            tt(flat(X), flat(X), flat(ACCB), ALU.add).then_inc(sig["resid_done"], 1)
            dve.wait_ge(sig["resid_done"], seen.up("resid_done"))

            def take_queries(bq):
                dve.wait_ge(sig["xq_mm"], seen.up("xq_mm"))
                scale = float(DK) ** -0.5
                if bq:
                    ins = dve.tensor_scalar(x_q, PSF[:, 1024:2048], col(bq), scale, ALU.add, ALU.mult)
                else:
                    ins = dve.tensor_scalar(x_q, PSF[:, 1024:2048], scale, None, ALU.mult)
                ins.then_inc(sig["xq_ready"], 1)
                dve.wait_ge(sig["xq_ready"], seen.up("xq_ready"))

            def cross(bv, bias, nb):
                def front(b, q, first):
                    dve.wait_ge(sig["xv_ready"], seen.up("xv_ready"))
                    v = PS[:, 1, 0:256].rearrange("p (c n) -> p c n", c=2)
                    vl = PS[0:4, 1, 256:384]
                    if bv:
                        tt(x_v[q], v, row(bv).unsqueeze(1).broadcast_to([P, 2, P]), ALU.add).then_inc(sig["dve_ran"], 1)
                        dve.wait_ge(sig["dve_ran"], seen.up("dve_ran"))
                        tt(x_vl[q][0:4, :], vl, row(bv)[0:4, :], ALU.add).then_inc(sig["dve_ran"], 1)
                        dve.wait_ge(sig["dve_ran"], seen.up("dve_ran"))
                        ins = tt(x_vl[q][0:4, :], x_vl[q][0:4, :], w("mask_last")[0:4, :], ALU.mult)
                    else:
                        dve.tensor_copy(x_v[q], v).then_inc(sig["dve_ran"], 1)
                        dve.wait_ge(sig["dve_ran"], seen.up("dve_ran"))
                        ins = tt(x_vl[q][0:4, :], vl, w("mask_last")[0:4, :], ALU.mult)
                    ins.then_inc(sig["xv_taken"], 1)
                    dve.wait_ge(sig["xv_taken"], seen.up("xv_taken"))
                    dve.wait_ge(sig["xs_ready"], seen.up("xs_ready"))
                    s = PS[:, 2:6, 0:KEYS]
                    if bias:
                        dve.wait_ge(sig[f"ctx_landed{q}"], seen.up(f"ctx_landed{q}", nb))
                        if not (isinstance(b, int) and b == 0):
                            dve.wait_ge(sig["xexp"], seen.up("xexp", 0))
                        tt(x_s, s, c_F[q], ALU.add).then_inc(sig["dve_ran"], 1)
                        dve.wait_ge(sig["dve_ran"], seen.up("dve_ran"))
                        s = x_s
                    dve.tensor_reduce(x_neg[q], s, AX, ALU.max, negate=True).then_inc(sig["xmax"], 1)
                    dve.wait_ge(sig["xmax"], seen.up("xmax"))

                def norm(b, q):
                    dve.wait_ge(sig["xexp"], seen.up("xexp"))
                    dve.reciprocal(x_rec, x_sum[q]).then_inc(sig["dve_ran"], 1)
                    dve.wait_ge(sig["dve_ran"], seen.up("dve_ran"))
                    ins = tt(x_p[q], x_p[q], x_rec.unsqueeze(2).broadcast_to([P, HG, KEYS]), ALU.mult)
                    ins.then_inc(sig["xp_ready"], 1)
                    dve.wait_ge(sig["xp_ready"], seen.up("xp_ready"))

                def back(b, q):
                    dve.wait_ge(sig["xpt_ready"], seen.up("xpt_ready"))
                    dve.tensor_copy(x_pt[q][:, 1, :], PS[:, 7, :]).then_inc(sig["dve_ran"], 1)
                    dve.wait_ge(sig["dve_ran"], seen.up("dve_ran"))
                    dve.tensor_copy(x_pl[q][0:4, :], PS[0:4, 0, 257:385]).then_inc(sig["xpt_d"], 1)
                    dve.wait_ge(sig["xpt_d"], seen.up("xpt_d"))
                    dve.wait_ge(sig["xu_ready"], seen.up("xu_ready"))
                    m4 = w("mask4").unsqueeze(2).broadcast_to([P, 4, 32])
                    tt(x_t.rearrange("p (h q) -> p h q", h=4),
                              PS[:, 0, 384:512].rearrange("p (h q) -> p h q", h=4), m4, ALU.mult).then_inc(sig["xu_taken"], 1)
                    dve.wait_ge(sig["xu_taken"], seen.up("xu_taken"))
                    x4 = x_t.rearrange("p (h q) -> p h q", h=4)
                    tt(x4[:, 0:2, :], x4[:, 0:2, :], x4[:, 2:4, :], ALU.add).then_inc(sig["dve_ran"], 1)
                    dve.wait_ge(sig["dve_ran"], seen.up("dve_ran"))
                    tt(OT[:, bass.ds(b * 32, 32)], x4[:, 0, :], x4[:, 1, :], ALU.add).then_inc(sig["x_out"], 1)
                    dve.wait_ge(sig["x_out"], seen.up("x_out"))

                def fr(b, q, first):
                    front(b, q, first)

                front(0, 0, True)
                norm(0, 0)
                front(1, 1, True)
                back(0, 0)
                norm(1, 1)

                def body(i):
                    for k in range(2):
                        front(i * 2 + (2 + k), k, False)
                        back(i * 2 + (1 + k), 1 - k)
                        norm(None, k)
                per = {k: 2 for k in "xv_ready xv_taken xs_ready xmax xexp xp_ready xpt_ready xpt_d xu_ready "
                                     "xu_taken x_out".split()}
                n_ran = (4 if bv else 2) + (2 if bias else 0) + 2 + 4
                per["dve_ran"] = n_ran
                if bias:
                    per |= {"ctx_landed0": nb, "ctx_landed1": nb}
                seen.loop(B // 2 - 1, per, body)
                back(B - 1, 1)

            layernorm(X, XN, LN_EPS)
            dve.wait_ge(sig["w_l2"], 16)
            take_queries(None)
            for q in range(2):
                seen.up(f"ctx_landed{q}", 64 * (L0X_STEPS // 2) + 48 * (B // 2))
            cross(None, True, 32)
            dve.wait_ge(sig["proj_ready"], seen.up("proj_ready"))
            tt(flat(Y), PSF[:, 3072:4096], flat(XN), ALU.add).then_inc(sig["dve_ran"], 1)
            dve.wait_ge(sig["dve_ran"], seen.up("dve_ran"))
            layernorm(Y, Z, 1e-5, signal=False)
            affine(Z[:, :, :], "l2x_g1", "l2x_be1").then_inc(sig["stream_ready"], 1)
            dve.wait_ge(sig["stream_ready"], seen.up("stream_ready"))
            tt(ACC[:, :, :], Y[:, :, :], rows_t("l2x_b2"), ALU.add).then_inc(sig["dve_ran"], 1)
            dve.wait_ge(sig["dve_ran"], seen.up("dve_ran"))
            ff("l2x")
            layernorm(ACC, Z, 1e-5, signal=False)
            affine(Z[:, :, :], "l2x_g2", "l2x_be2").then_inc(sig["dve_ran"], 1)
            dve.wait_ge(sig["dve_ran"], seen.up("dve_ran"))
            tt(flat(X), flat(X), flat(Z), ALU.add).then_inc(sig["resid_done"], 1)
            dve.wait_ge(sig["resid_done"], seen.up("resid_done"))

            layernorm(X, XN, LN_EPS)
            dve.wait_ge(sig["relb_landed"], 64)
            for j in range(4):
                r = slice(32 * j, 32 * j + 32)
                dve.tensor_copy(c_rel2[r].rearrange("p k m -> p m k"),
                                    ACCB[r, 0:4, :].rearrange("p t n -> p (t n)")
                                    .rearrange("p (k m j) -> p j m k", k=32, m=4)[:, j]).then_inc(sig["dve_ran"], 1)
                dve.wait_ge(sig["dve_ran"], seen.up("dve_ran"))
            oh = w("onehot").rearrange("p (k u) -> p k u", k=32)
            for m4i in range(4):
                rb = c_rel2[:, :, m4i].unsqueeze(1).broadcast_to([P, 32, 32])
                tt(c_p[:, 0:1024].rearrange("p (k u) -> p k u", k=32), oh, rb, ALU.mult).then_inc(sig["dve_ran"], 1)
                dve.wait_ge(sig["dve_ran"], seen.up("dve_ran"))
                dve.tensor_reduce(c_relb[:, m4i, :], c_p[:, 0:1024].rearrange("p (k u) -> p k u", k=32),
                                      AX, ALU.add).then_inc(sig["dve_ran"], 1)
                dve.wait_ge(sig["dve_ran"], seen.up("dve_ran"))
            mp = w("mask_pair").rearrange("p (m r) -> p m r", r=2)
            for name, dst in (("l2a_bq", c_qb), ("l2a_bk", c_big), ("l2a_bv", c_big)):
                for cc in range(2):
                    dve.wait_ge(sig["pair_ready"], seen.up("pair_ready"))
                    for c in range(8):
                        o = dst.rearrange("p (m r c) -> p m r c", r=2, c=H)[:, :, :, 8 * cc + c]
                        i0 = PS[:, c // 2, 256 * (c % 2):256 * (c % 2) + 256].rearrange("p (m r) -> p m r", r=2)
                        ins = dve.scalar_tensor_tensor(out=o, in0=i0, scalar=col(name, 16)[:, 8 * cc + c:8 * cc + c + 1],
                                                       in1=mp, op0=ALU.add, op1=ALU.mult)
                        if c == 7 and (cc == 0 or name == "l2a_bq"):
                            ins.then_inc(sig["pair_taken"], 1)
                            dve.wait_ge(sig["pair_taken"], seen.up("pair_taken"))
                        else:
                            ins.then_inc(sig["dve_ran"], 1)
                            dve.wait_ge(sig["dve_ran"], seen.up("dve_ran"))
                    if cc == 1 and name != "l2a_bq":
                        o = c_k if name == "l2a_bk" else c_v
                        dve.tensor_reduce(o.rearrange("p (m i) -> p m i", m=32),
                                                 c_big.rearrange("p (m j i) -> p m i j", m=32, j=4), AX, ALU.add).then_inc(sig["pair_taken"], 1)
                        dve.wait_ge(sig["pair_taken"], seen.up("pair_taken"))
            dve.transpose(c_vt, c_v).then_inc(sig["c_in"], 1)
            dve.wait_ge(sig["c_in"], seen.up("c_in"))
            core("pairs")
            dve.wait_ge(sig["proj_ready"], seen.up("proj_ready"))
            tt(flat(Y), PSF[:, 1024:2048], flat(XN), ALU.add).then_inc(sig["dve_ran"], 1)
            dve.wait_ge(sig["dve_ran"], seen.up("dve_ran"))
            tt(Y[:, :, :], Y[:, :, :], rows_t("l2a_bo"), ALU.add).then_inc(sig["dve_ran"], 1)
            dve.wait_ge(sig["dve_ran"], seen.up("dve_ran"))
            layernorm(Y, Z, 0.0)
            dve.wait_ge(sig["proj_ready"], seen.up("proj_ready"))
            tt(flat(Z), PSF[:, 3072:4096], flat(Z), ALU.add).then_inc(sig["dve_ran"], 1)
            dve.wait_ge(sig["dve_ran"], seen.up("dve_ran"))
            tt(Z[:, :, :], Z[:, :, :], rows_t("l2a_b2"), ALU.add).then_inc(sig["dve_ran"], 1)
            dve.wait_ge(sig["dve_ran"], seen.up("dve_ran"))
            layernorm(Z, Y, 0.0, signal=False)
            tt(flat(X), flat(X), flat(Y), ALU.add).then_inc(sig["resid_done"], 1)
            dve.wait_ge(sig["resid_done"], seen.up("resid_done"))

            layernorm(X, XN, LN_EPS)
            dve.tensor_copy(flat(Y), flat(XN)).then_inc(sig["dve_ran"], 1)
            dve.wait_ge(sig["dve_ran"], seen.up("dve_ran"))
            for r in range(4):
                dve.wait_ge(sig["gate_mm"], seen.up("gate_mm"))
                gb = small[:, SMALL_L2GATE + 4 * r:SMALL_L2GATE + 4 * r + 4].unsqueeze(1).broadcast_to([P, NT, 4])
                tt(g_l[:, 0:32].rearrange("p (t e) -> p t e", t=NT),
                       PS[:, 6, 0:32].rearrange("p (t e) -> p t e", t=NT), gb, ALU.add).then_inc(sig["dve_ran"], 1)
                dve.wait_ge(sig["dve_ran"], seen.up("dve_ran"))
                softmax_gates()
                rank_gates(4, w("rank_low4"))
                dve.tensor_scalar(g_rank[:, 0:32], g_rank[:, 0:32], 2.0, None, ALU.is_lt).then_inc(sig["dve_ran"], 1)
                dve.wait_ge(sig["dve_ran"], seen.up("dve_ran"))
                dve.wait_ge(sig["gate_act"], seen.up("gate_act"))
                share(4, g_e)
                dve.tensor_copy(flat(ACC), flat(Y)).then_inc(sig["dve_ran"], 1)
                dve.wait_ge(sig["dve_ran"], seen.up("dve_ran"))
                ff("l2f")
                dve.wait_ge(sig["bias_ready"], seen.up("bias_ready"))
                ins = tt(flat(Y), flat(ACC), flat(ACCB), ALU.add)
                name = "stream_ready" if r < 3 else "dve_ran"
                ins.then_inc(sig[name], 1)
                dve.wait_ge(sig[name], seen.up(name))
            tt(flat(X), flat(X), flat(Y), ALU.add).then_inc(sig["resid_done"], 1)
            dve.wait_ge(sig["resid_done"], seen.up("resid_done"))

            layernorm(X, XN, LN_EPS)
            dve.wait_ge(sig["w_l3"], 16)
            take_queries("l3x_bq")
            cross("l3x_bv", False, 16)
            dve.wait_ge(sig["bias_ready"], seen.up("bias_ready"))
            residual()

            layernorm(X, XN, LN_EPS)
            layernorm(XN, Z, 1e-5, signal=False)
            affine(Z[:, :, :], "l3a_lng", "l3a_lnb").then_inc(sig["dve_ran"], 1)
            dve.wait_ge(sig["dve_ran"], seen.up("dve_ran"))
            heads()
            core("plain")
            dve.wait_ge(sig["bias_ready"], seen.up("bias_ready"))
            tt(flat(X), flat(X), flat(Z), ALU.add).then_inc(sig["dve_ran"], 1)
            dve.wait_ge(sig["dve_ran"], seen.up("dve_ran"))
            residual()

            layernorm(X, XN, LN_EPS)
            dve.memset(flat(ACC), 0.0).then_inc(sig["dve_ran"], 1)
            dve.wait_ge(sig["dve_ran"], seen.up("dve_ran"))
            ff("l3f")
            dve.wait_ge(sig["bias_ready"], seen.up("bias_ready"))
            residual()

        @block.gpsimd
        def _(pool):
            seen = Tally(pool)
            for g in ("l0", "l1", "l2", "l3"):
                a, cols = SPANS["group_" + g]
                if g == "l1":
                    pool.dma_start(RB[:, :, :], wrows.rearrange("a r n -> (a) r n").broadcast_to([P, len(ROWS), P])
                                   ).then_inc(sig["rows_landed"], 16)
                    pool.dma_start(MK[:, 0:2, :], mask[0:2 * P, :].rearrange("(c p) b -> p c b", c=2))\
                        .then_inc(sig["mask_landed"], 16)
                    pool.dma_start(MK[0:1, 2, :], mask[2 * P:KEYS, :]).then_inc(sig["mask_landed"], 16)
                pool.dma_start(W[:, a:a + cols], wpack[:, a:a + cols]).then_inc(sig["w_" + g], 16)
            pool.wait_ge(sig["w_l0"], 16)
            pool.wait_ge(sig["rows_landed"], 16)
            ready = sig["rows_landed"]

            def bias(name):
                pool.tensor_tensor(X[:, :, :], X[:, :, :], rows_t(name), ALU.add).then_inc(sig["bias_ready"], 1)
                pool.wait_ge(sig["bias_ready"], seen.up("bias_ready"))

            pool.wait_ge(sig["norm_ready"], seen.up("norm_ready", NT))
            pool.wait_ge(sig["l0s_q_ready"], seen.up("l0s_q_ready"))

            def stage(s, q, first):
                if not (first and isinstance(s, int) and s < 2):
                    pool.wait_ge(sig["l0s_scores"], seen.up("l0s_scores"))
                pool.wait_ge(ready, 16)
                pool.tensor_copy(l0_qs[q], l0_qp[:, bass.ds(s * P, P)]).then_inc(sig["l0s_staged"], 1)
                pool.wait_ge(sig["l0s_staged"], seen.up("l0s_staged"))
            stage(0, 0, True)
            stage(1, 1, True)
            seen.loop(L0X_STEPS // 2 - 1, {"l0s_scores": 2, "l0s_staged": 2},
                   lambda i: (stage(i * 2 + 2, 0, False), stage(i * 2 + 3, 1, False)))
            bias("l0x_bo")
            pool.wait_ge(sig["norm_ready"], seen.up("norm_ready", 2 * NT))
            pool.dma_start(ar(8192, 4096), l1x_w).then_inc(sig["l1x_w_landed"], 16)
            seen.up("expert_weights")

            pool.wait_ge(sig["norm_ready"], seen.up("norm_ready", NT))
            bias("l1x_bo")
            seen.up("norm_ready", NT)

            def expert_bias(names):
                pool.wait_ge(sig["expert_weights"], seen.up("expert_weights"))
                for e, name in enumerate(names):
                    we = f_w[:, :, e:e + 1].broadcast_to([P, NT, P])
                    dst = ACCB if e == 0 else Z
                    pool.tensor_tensor(dst[:, :, :], rows_t(name), we, ALU.mult).then_inc(sig["pool_ran"], 1)
                    pool.wait_ge(sig["pool_ran"], seen.up("pool_ran"))
                    if e:
                        ins = pool.tensor_tensor(ACCB[:, :, :], ACCB[:, :, :], Z[:, :, :], ALU.add)
                        name = "bias_ready" if e == 3 else "pool_ran"
                        ins.then_inc(sig[name], 1)
                        pool.wait_ge(sig[name], seen.up(name))

            pool.wait_ge(sig["norm_ready"], seen.up("norm_ready", NT))
            expert_bias([f"l1f_b2_{e}" for e in range(4)])

            def spread():
                pool.wait_ge(sig["xq_ready"], seen.up("xq_ready"))
                m16 = w("mask16").unsqueeze(2).broadcast_to([P, H, 32])

                def go(b, q, first):
                    if not (first and isinstance(b, int) and b < 2):
                        pool.wait_ge(sig["xs_ready"], seen.up("xs_ready"))
                    pool.wait_ge(ready, 16)
                    qv = x_q[:, bass.ds(b * 32, 32)].unsqueeze(1).broadcast_to([P, H, 32])
                    pool.tensor_tensor(x_qb[q].rearrange("p (h q) -> p h q", h=H), qv, m16, ALU.mult).then_inc(sig["xqb"], 1)
                    pool.wait_ge(sig["xqb"], seen.up("xqb"))
                go(0, 0, True)
                go(1, 1, True)
                seen.loop(B // 2 - 1, {"xs_ready": 2, "xqb": 2}, lambda i: (go(i * 2 + 2, 0, False),
                                                                         go(i * 2 + 3, 1, False)))
                seen.up("xs_ready", 2)

            pool.wait_ge(sig["norm_ready"], seen.up("norm_ready", NT))
            pool.wait_ge(sig["resid_done"], seen.up("resid_done", 6))
            for j in range(4):
                pool.dma_start(ACCB[32 * j:32 * j + 32, 0:4, :].rearrange("p t n -> p (t n)"),
                               relb.broadcast_to([32, 512])).then_inc(sig["relb_landed"], 16)
            spread()
            seen.up("norm_ready", 2 * NT)

            pool.wait_ge(sig["norm_ready"], seen.up("norm_ready", NT))
            for r in range(4):
                expert_bias([f"l2f_b2_{e}" for e in range(4)])

            pool.wait_ge(sig["norm_ready"], seen.up("norm_ready", NT))
            bias("l3x_bo")
            spread()
            pool.wait_ge(sig["norm_ready"], seen.up("norm_ready", NT))
            bias("l3a_bp")
            pool.wait_ge(sig["norm_ready"], seen.up("norm_ready", NT))
            bias("l3f_b2")

    return nc



def kernel(**inputs):
    import numpy as np
    import concourse.bacc as bacc
    from concourse import mybir as mb
    from concourse.bass_utils import run_bass_kernel_spmd

    a = {k: np.asarray(v) for k, v in inputs.items()}
    f = np.float32
    wp = np.zeros((P, WTOTAL), f)

    def put(name, m):
        at, n = SPANS[name]
        m = np.asarray(m)
        wp[:m.shape[0], at:at + m.shape[1]] = m

    put("ident", np.eye(P, dtype=f))
    put("l0x_q", a["L0_xattn_Wq"].T)
    put("l0x_k", a["L0_xattn_Wk"])
    put("l0x_v", a["L0_xattn_Wv"].T)
    put("l0x_o", a["L0_xattn_Wo"].T)
    p = np.arange(P)
    put("blockones", (p[:, None] // 32 == p[None, :] // 32).astype(f))
    put("l0a_qkvg", np.concatenate([a["L0_attn_W" + c] for c in "qkvg"], 1))
    put("l0a_o", a["L0_attn_Wo"])
    put("l0f_gate", a["L0_ffn_Wg"])
    for E in (8, 4):
        e = np.arange(E)
        put(f"rank_low{E}", np.broadcast_to((e[None, :] < e[:, None]).astype(f).reshape(1, -1), (P, E * E)))
    put("mask4", ((p[:, None] % 32) // 8 == np.arange(4)[None, :]).astype(f))
    put("mask16", (p[:, None] // 8 == np.arange(16)[None, :]).astype(f))
    put("mask_last", (np.arange(4)[:, None] == p[None, :] // 32).astype(f))
    put("l1a_q", a["L1_attn_wq"].T)
    rep4 = np.array([8 * g + d for g in range(4) for m in range(4) for d in range(8)])
    put("l1a_k", a["L1_attn_wk"][rep4].T)
    put("l1a_v", a["L1_attn_wv"][rep4].T)
    put("l1a_o", a["L1_attn_wo"].T)
    put("causal", np.where(np.arange(32)[None, :] > (p[:, None] % 32), f(-1e30), f(0)))
    put("l1f_gate", a["L1_ffn_gate_w"])
    put("l1f_dp1", a["L1_ffn_dp_w1"])
    put("l1f_dp2", a["L1_ffn_dp_w2"])
    for c in "qkvo":
        put("l2x_" + c, a["L2_xattn_W" + c].T)
        put("l3x_" + c, a["L3_xattn_W" + c].T)
    jd = p % 32 % 8
    for c in "qkv":
        wt = a["L2_attn_W" + c].T
        put("l2a_" + c, np.concatenate([wt[:, 8 * k + jd[:32]] for k in range(16)], 1))
    wt = a["L2_attn_Wo"].T
    put("l2a_o", np.concatenate([wt[8 * k + jd] for k in range(16)], 1))
    put("l2a_w1", a["L2_attn_W1"].T)
    put("l2a_w2", a["L2_attn_W2"].T)
    put("mask_pair", np.repeat(np.tile(((p[:, None] % 32) // 8 == np.arange(4)[None, :]).astype(f), (1, 32)), 2, 1))
    put("onehot", np.tile(one_hot_buckets().reshape(32, 1024), (4, 1)))
    put("l2f_gate", np.concatenate(list(a["L2_ffn_Wg"]), 1))
    for i, c in enumerate("qkv"):
        put("l3a_" + c, a["L3_attn_W_qkv"][128 * i:128 * i + 128].T)
    put("l3a_o", a["L3_attn_W_proj"].T)
    put("l3f_u1", a["L3_ffn_U1"])
    put("l3f_v2", a["L3_ffn_V2"])

    def put_col(name, v):
        at = SPANS["cols"][0] + COLS[name]
        v = np.asarray(v)
        wp[:v.shape[0], at:at + v.shape[1]] = v
    put_col("l0x_bq", a["L0_xattn_bq"][:, None])
    put_col("l0x_bv", a["L0_xattn_bv"][:, None])
    put_col("l3x_bq", a["L3_xattn_bq"][:, None])
    put_col("l3x_bk", a["L3_xattn_bk"][:, None])
    put_col("l2a_b1", a["L2_attn_b1"][:, None])
    put_col("l1f_dpb1", a["L1_ffn_dp_b1"][:, None])
    for c in "qkv":
        put_col("l2a_b" + c, a["L2_attn_b" + c].reshape(16, 8)[:, jd].T)

    rows = np.zeros((1, len(ROWS), P), f)
    src = {"l0x_bo": "L0_xattn_bo", "l0a_gamma": "L0_attn_gamma", "l0a_beta": "L0_attn_beta",
           "l1x_bo": "L1_xattn_bo", "l2x_b2": "L2_xattn_b2", "l2x_g1": "L2_xattn_g1", "l2x_be1": "L2_xattn_be1",
           "l2x_g2": "L2_xattn_g2", "l2x_be2": "L2_xattn_be2", "l2a_bo": "L2_attn_bo", "l2a_b2": "L2_attn_b2",
           "l3x_bv": "L3_xattn_bv", "l3x_bo": "L3_xattn_bo", "l3a_bp": "L3_attn_b_proj",
           "l3a_lng": "L3_attn_ln_gamma", "l3a_lnb": "L3_attn_ln_beta", "l3f_b2": "L3_ffn_b2"}
    for k, v in src.items():
        rows[0, ROWS.index(k)] = a[v]
    for e in range(4):
        rows[0, ROWS.index(f"l1f_b2_{e}")] = a["L1_ffn_eb2"][e]
        rows[0, ROWS.index(f"l2f_b2_{e}")] = a["L2_ffn_b2"][e]
    small = rows[0, ROWS.index("small")]
    small[SMALL_L1GATE:SMALL_L1GATE + 4] = a["L1_ffn_gate_b"]
    small[SMALL_DPB2:SMALL_DPB2 + 1] = a["L1_ffn_dp_b2"]
    small[SMALL_L2GATE:SMALL_L2GATE + 16] = a["L2_ffn_bg"].reshape(-1)

    def two(m):
        return m.reshape(8, 2, 64, P).transpose(1, 2, 0, 3).reshape(P, 1, 8, P)
    wkv = a["L1_xattn_Wkv"]
    l1x_w = np.concatenate([two(a["L1_xattn_Wq"].T), two(wkv[:, :1024].T), two(wkv[:, 1024:].T),
                            two(a["L1_xattn_Wo"])], 1).reshape(P, 4096)

    units = np.zeros((N_UNITS, P, WCOLS), f)

    def unit(i, w1, w3, b1, w2):
        units[i, :w1.shape[0], 0:UNIT] = w1
        if w3 is not None:
            units[i, :, UNIT:2 * UNIT] = w3
        if b1 is not None:
            units[i, :, 3 * UNIT:] = b1.reshape(2, P).T
        for c in range(2):
            units[i, :, 2 * UNIT + P * c:2 * UNIT + P * c + w2.shape[1]] = w2[P * c:P * c + P]
    u0 = FF_UNITS["l0f"][0]
    unit(u0, a["L0_ffn_Ws1"], a["L0_ffn_Ws3"], None, a["L0_ffn_Ws2"])
    for e in range(8):
        unit(u0 + 1 + e, a["L0_ffn_We1"][e], a["L0_ffn_We3"][e], None, a["L0_ffn_We2"][e])
    for e in range(4):
        unit(FF_UNITS["l1f"][0] + e, a["L1_ffn_ew1"][e], None, a["L1_ffn_eb1"][e], a["L1_ffn_ew2"][e])
    for k in range(2):
        s = slice(UNIT * k, UNIT * k + UNIT)
        unit(FF_UNITS["l2x"][0] + k, a["L2_xattn_W1"].T[:, s], None, a["L2_xattn_b1"][s], a["L2_xattn_W2"].T[s])
        unit(FF_UNITS["l3f"][0] + k, a["L3_ffn_V1"][:, s], None, a["L3_ffn_b1"][s], a["L3_ffn_U2"][s])
        for e in range(4):
            unit(FF_UNITS["l2f"][0] + 2 * e + k, a["L2_ffn_W1"][e][:, s], None, a["L2_ffn_b1"][e][s],
                 a["L2_ffn_W2"][e][s])

    ctxv = a["ctx_1024"]
    ctxT = np.zeros((B, P, KPAD), f)
    ctxT[:, :, :KEYS] = ctxv.transpose(0, 2, 1)
    ctxT[:, :, KEYS:] = ctxv[:, 256, :, None]
    ctxN = np.ones((B, KEYS, FQ), f)
    ctxN[:, :, :P] = ctxv
    mask_words = np.zeros((KEYS, B, 4), np.uint8)
    mask_words[:, :, 0] = a["mask_BxS2_bk1"].T
    arrays = {
        "ctxT": ctxT, "ctxN": ctxN,
        "fside": np.ascontiguousarray(a["fside_Bx16xSxS2_0"]).reshape(B, H * S, KEYS),
        "mask": mask_words.view(np.int32).reshape(KEYS, B),
        "wpack": wp, "wrows": rows, "l1x_w": l1x_w, "units": units,
        "relb": np.ascontiguousarray(a["L2_attn_rel_bias"]).reshape(1, 512),
        "x": np.ascontiguousarray(a["x"]).reshape(TOK, P),
    }
    nc = bacc.Bacc("TRN2", target_bir_lowering=False, num_devices=1)
    ap = {n: nc.dram_tensor("in_" + n, v.shape, mb.dt.from_np(v.dtype), kind="ExternalInput").ap()
          for n, v in arrays.items()}
    out = nc.dram_tensor("out_x", (TOK, P), F32, kind="ExternalOutput").ap()
    tiles = lambda t: t.rearrange("(t p) d -> p t d", p=P)
    perceiver(nc, ap["ctxT"], ap["ctxN"], ap["fside"], ap["mask"], ap["wpack"], ap["wrows"], ap["l1x_w"],
              ap["units"], ap["relb"], tiles(ap["x"]), tiles(out))
    r = run_bass_kernel_spmd(nc, [{"in_" + n: v for n, v in arrays.items()}], core_ids=[0])
    return r.results[0]["out_x"].reshape(B, S, P)


def one_hot_buckets():
    import math

    import numpy as np
    rel = np.arange(32)[:, None] - np.arange(32)[None, :]
    n = -rel
    ret = (n < 0).astype(np.int32) * 16
    n = np.abs(n)
    large = 8 + (np.log(np.maximum(n, 1).astype(np.float32) / 8) / math.log(128 / 8) * 8).astype(np.int32)
    bucket = ret + np.where(n < 8, n, np.minimum(large, 15))
    return (bucket[:, :, None] == np.arange(32)).astype(np.float32)
```

```python
from contextlib import ExitStack

import concourse.bass as bass
from concourse import mybir

F32 = mybir.dt.float32
I32 = mybir.dt.int32
ALU = mybir.AluOpType
ACT = mybir.ActivationFunctionType
AX = mybir.AxisListType.X

P = 128
B = 32
S = 32
NT = B * S // P
TOK = B * S
KEYS = 257
KPAD = 260
H = 16
HG = 4
DK = 8
FQ = P + 1
DH1 = 64
UNIT = 256
WCOLS = 3 * UNIT + 2
LN_EPS = 1e-5
L0X_STEPS = B // 4


def weight_plan():
    groups = {
        "first": [("ident", 128), ("l0x_q", 128), ("l0x_k", 128), ("l0x_v", 128), ("l0x_o", 128),
                  ("cols", 64)],
        "l0": [("blockones", 128), ("l0a_qkvg", 512), ("l0a_o", 128), ("l0f_gate", 8), ("rank_low8", 64),
               ("rank_low4", 16), ("mask4", 4), ("mask16", 16), ("mask_last", 128),
               ("head_mask", 128), ("fold", 32)],
        "l1": [("l1a_q", 128), ("l1a_k", 128), ("l1a_v", 128), ("l1a_o", 128), ("causal", 32),
               ("l1f_gate", 4), ("l1f_dp1", 64), ("l1f_dp2", 1)],
        "l2": [("l2x_q", 128), ("l2x_k", 128), ("l2x_v", 128), ("l2x_o", 128), ("l2a_q", 512),
               ("l2a_k", 512), ("l2a_v", 512), ("l2a_o", 2048), ("l2a_w1", 128), ("l2a_w2", 128),
               ("mask_pair", 256), ("onehot", 1024), ("l2f_gate", 16)],
        "l3": [("l3x_q", 128), ("l3x_k", 128), ("l3x_v", 128), ("l3x_o", 128), ("l3a_q", 128),
               ("l3a_k", 128), ("l3a_v", 128), ("l3a_o", 128), ("l3f_u1", 128), ("l3f_v2", 128)],
    }
    at, spans = 0, {}
    for g, items in groups.items():
        a0 = at
        for name, n in items:
            spans[name] = (at, n)
            at += n
        spans["group_" + g] = (a0, at - a0)
    return spans, at


SPANS, WTOTAL = weight_plan()

ROWS = ["l0x_bo", "l0a_gamma", "l0a_beta", "l1x_bo", "l1f_b2_0", "l1f_b2_1", "l1f_b2_2", "l1f_b2_3",
        "l2x_b2", "l2x_g1", "l2x_be1", "l2x_g2", "l2x_be2", "l2a_bo", "l2a_b2",
        "l2f_b2_0", "l2f_b2_1", "l2f_b2_2", "l2f_b2_3", "l3x_bo", "l3a_bp", "l3a_lng",
        "l3a_lnb", "l3f_b2", "small"]
SMALL_L1GATE, SMALL_DPB2, SMALL_L2GATE = 0, 4, 8

COLS = {"l0x_bq": 0, "l0x_bv": 1, "l3x_bq": 2, "l3x_bk": 3, "l2a_b1": 4, "l1f_dpb1": 5, "l3x_bv": 6,
        "l2a_bq": 8, "l2a_bk": 24, "l2a_bv": 40}

FF_UNITS = {"l0f": (0, 9), "l1f": (9, 4), "l2x": (13, 2), "l2f": (15, 8), "l3f": (23, 2)}
N_UNITS = 25


class Tally:

    def __init__(self, eng):
        self.eng, self.n = eng, {}
        self.i, self.per, self.start = None, {}, {}

    def value(self, name):
        v = self.n[name]
        return v + self.i * self.per[name] if self.i is not None and self.per.get(name) else v

    def up(self, name, k=1):
        self.n[name] = self.n.get(name, 0) + k
        return self.value(name)

    def loop(self, trips, per, body):
        self.start = dict(self.n)
        with self.eng.Fori(0, trips, 1) as i:
            self.i, self.per = i, per
            body(i)
            self.i, self.per = None, {}
        rise = {k: v - self.start.get(k, 0) for k, v in self.n.items() if v != self.start.get(k, 0)}
        assert rise == per, f"{self.eng.engine}: {rise}"
        for k, v in rise.items():
            self.n[k] = self.start.get(k, 0) + trips * v

    def skewed(self, steps, per, head, front, back):
        front(0, 0, True)
        front(1, 1, True)
        back(0, 0, True)
        front(2, 0, False)
        back(1, 1, True)

        def body(i):
            front(i * 2 + 3, 1, False)
            back(i * 2 + 2, 0, False)
            front(i * 2 + 4, 0, False)
            back(i * 2 + 3, 1, False)
        self.loop((steps - 4) // 2, per, body)
        front(steps - 1, 1, False)
        back(steps - 2, 0, False)
        back(steps - 1, 1, False)


def perceiver(nc, ctxT, ctxN, fside, mask, wpack, wrows, l1x_w, units, relb, x_in, out):
    ctx = ExitStack()
    with ctx:
        def sb(name, shape, dt=F32):
            return ctx.enter_context(nc.sbuf_tensor(name, shape, dt))

        W = sb("W", [P, WTOTAL])
        RB = sb("RB", [P, len(ROWS), P])
        X = sb("X", [P, NT, P])
        XN = sb("XN", [P, NT, P])
        XNT = sb("XNT", [P, TOK])
        Y = sb("Y", [P, NT, P])
        Z = sb("Z", [P, NT, P])
        ZT = sb("ZT", [P, TOK])
        OT = sb("OT", [P, TOK])
        ACC = sb("ACC", [P, NT, P])
        ACCB = sb("ACCB", [P, NT, P])
        CTX = sb("CTX", [P, 2, 2592])
        WB = sb("WB", [P, 2, WCOLS])
        ST = sb("ST", [P, NT, 6])
        MV = sb("MV", [P, NT, 2])
        SD = sb("SD", [P, 2, NT])
        SM = sb("SM", [P, 1200])
        AR = sb("AR", [P, 18432])
        MK = sb("MK", [P, 3, B], I32)
        PS = ctx.enter_context(nc.psum_tensor("PS", [P, 8, 512], F32))
        PSF = PS[:, :, :].rearrange("p b n -> p (b n)")

        def w(name):
            a, n = SPANS[name]
            return W[:, a:a + n]

        def row(name):
            return RB[:, ROWS.index(name), :]

        def rows_t(name, nt=NT):
            return row(name).unsqueeze(1).broadcast_to([P, nt, P])

        def col(name, n=1):
            a = SPANS["cols"][0] + COLS[name]
            return W[:, a:a + n]

        def ar(a, n):
            return AR[:, a:a + n]

        ident = w("ident")

        names = """act_ran dve_ran pool_ran
            x_landed w_first w_l0 w_l1 w_l2 w_l3 rows_landed l1x_w_landed mask_landed relb_landed
            ctx_landed0 ctx_landed1 ctx_landed2 ctx_landed3 unit_landed0 unit_landed1 out_landed
            var_ready std_ready norm_ready stream_ready turned turned_taken
            lin_ready lin_taken proj_ready bias_ready resid_done
            l0s_q_ready l0s_staged l0s_scores l0s_max l0s_exp l0s_probs l0s_pt l0s_pt_taken l0s_u l0s_u_taken
            l0a_mm l0a_act l0a_qk l0a_ksum
            gate_mm gate_hidden gate_entropy gate_shift gate_act expert_weights
            up_ready act_half h_ready down_ready down_used
            y_w_ready y_w_taken yq_ready yq_taken ys_ready yclip yexp yu_ready yu_taken yt_ready yt_taken
            yo_ready yo_taken y_padded
            xq_mm xq_ready xk_ready xk_taken xv_ready xv_taken xvl_taken xqb xs_ready xs_added xmax xexp
            xsum_spread xpl_ready xpl_taken xpt_ready xpt_a xpt_d
            xu_ready xu_taken x_out
            qkv_taken c_in c_scores c_shift c_exp c_probs c_pt c_pt_taken c_pv c_masked
            pair_ready pair_taken""".split()
        sig = {n: ctx.enter_context(nc.semaphore(n)) for n in names}
        block = ctx.enter_context(nc.Block())

        l0_cT = [CTX[:, q, 0:4 * KPAD].rearrange("p (j k) -> p j k", j=4) for q in range(2)]
        l0_cn = [CTX[:, q, 1040:1040 + 8 * FQ].rearrange("p (j c f) -> p j c f", j=4, c=2) for q in range(2)]
        l0_cl = [CTX[0:1, q, 2072:2072 + 4 * FQ].rearrange("p (j f) -> p j f", j=4) for q in range(2)]
        l0_qp = ar(0, TOK)
        l0_qt = ar(TOK, TOK)
        l0_qs = [ar(2048 + 128 * q, 128) for q in range(2)]
        l0_p = [ar(2304 + KEYS * q, KEYS) for q in range(2)]
        l0_pt = [ar(2820 + 384 * q, 384).rearrange("p (c n) -> p c n", c=3) for q in range(2)]
        l0_ut = ar(3588, TOK)
        l0_ct = ar(4612, TOK)
        l0_neg = [SM[:, 0 + q:1 + q] for q in range(2)]
        l0_sum = [SM[:, 2 + q:3 + q] for q in range(2)]
        c_buf = lambda k, a, n: CTX[:, k // 2, 1296 * (k % 2) + a:1296 * (k % 2) + a + n]
        c_T = [c_buf(k, 0, KPAD) for k in range(4)]
        c_N = [c_buf(k, KPAD, 2 * FQ).rearrange("p (c f) -> p c f", c=2) for k in range(4)]
        c_F = [c_buf(k, KPAD, HG * KEYS).rearrange("p (g k) -> p g k", g=HG) for k in range(4)]
        y_w = ar(8192, 4096).rearrange("p (m h n) -> p m h n", m=4, h=8)
        y_A = ar(0, 2048).rearrange("p (h n) -> p h n", h=H)
        y_M = ar(2048, 2048).rearrange("p (h n) -> p h n", h=H)
        y_Q = ar(4096, 2048).rearrange("p (b h n) -> p b h n", b=4, h=H)
        y_V = ar(6144, 2048).rearrange("p (h b n) -> p h b n", h=H, b=4)
        y_C = ar(12288, 1536).rearrange("p (c n) -> p c n", c=3)
        y_U = ar(13824, 512).rearrange("p (g n) -> p g n", g=4)
        y_P = [ar(14336 + 1536 * q, 1536).rearrange("p (c n) -> p c n", c=3) for q in range(2)]
        y_last = [ar(17408 + FQ * k, FQ) for k in range(4)]
        y_hi = ar(17924, 3 * B).rearrange("p (c b) -> p c b", c=3)
        y_r = SM[:, 8:12]
        y_at = lambda h: 8 * (h % 2) + h // 2
        x_q = ar(0, TOK)
        x_qb = [ar(1024 + 512 * q, 512) for q in range(2)]
        x_k = [ar(2048 + 257 * q, 257) for q in range(2)]
        x_v = [ar(2564 + 256 * k, 256).rearrange("p (c n) -> p c n", c=2) for k in range(4)]
        x_vl = [ar(3588 + 128 * k, 128) for k in range(4)]
        x_p = [ar(4100 + 1028 * q, 1028).rearrange("p (g k) -> p g k", g=HG) for q in range(2)]
        x_s = ar(6156, 1028).rearrange("p (g k) -> p g k", g=HG)
        x_pt = ar(7184, 1024).rearrange("p (c n) -> p c n", c=2)
        x_pl = ar(8208, 128)
        x_r = [ar(8336 + 128 * q, 128) for q in range(2)]
        x_t = ar(8592, 128)
        x_neg = [SM[:, 16 + 4 * q:20 + 4 * q] for q in range(2)]
        x_sum = [SM[:, 24 + 4 * q:28 + 4 * q] for q in range(2)]
        x_rec = SM[:, 32:64]
        c_qb = ar(0, 4096)
        c_k = ar(4096, 1024)
        c_v = ar(5120, 1024)
        c_q = ar(6144, 1024)
        c_vt = ar(6144, 1024)
        c_p = ar(7168, 2048)
        c_p2 = ar(9216, 2048)
        c_pt = ar(11264, 2048)
        c_big = ar(13312, 4096)
        c_red = SM[:, 64:128]
        c_relb = ar(17408, 128).rearrange("p (m k) -> p m k", m=4)
        c_rel2 = ar(17536, 128).rearrange("p (k m) -> p k m", k=32)
        flat = lambda a: a[:, :, :].rearrange("p t n -> p (t n)")
        f_h = [ar(1024 * q, 1024).rearrange("p (c n) -> p c n", c=2) for q in range(2)]
        f_s = [ar(2048 + 512 * c, 512) for c in range(2)]
        f_pt = ar(3072, TOK)
        f_w = SM[:, 128:200].rearrange("p (t e) -> p t e", t=NT)

        g_l = SM[:, 200:264]
        g_e = SM[:, 264:328]
        g_m = SM[:, 328:336]
        g_k = SM[:, 336:344]
        g_rank = SM[:, 344:408]
        g_a = ar(4096, 512)
        g_b = ar(4608, 512)
        g_h = ar(5120, TOK)
        g_z = SM[:, 408:480].rearrange("p (j t) -> p j t", j=9)

        LAYERS_FF = {
            "l0f": (True, ACT.Silu, True), "l1f": (False, ACT.Relu, True),
            "l2x": (False, ACT.Gelu, False), "l2f": (False, ACT.Gelu_apprx_tanh, True),
            "l3f": (False, ACT.Gelu_apprx_tanh, False)}

        @block.sync
        def _(sp):
            seen = Tally(sp)
            sp.dma_start(X[:, :, :], x_in).then_inc(sig["x_landed"], 16)
            a, cols = SPANS["group_first"]
            sp.dma_start(W[:, a:a + cols], wpack[:, a:a + cols]).then_inc(sig["w_first"], 16)

            def load_units(layer, trips=1):
                u0, nu = FF_UNITS[layer]

                if seen.n.get("down_ready"):
                    sp.wait_ge(sig["down_ready"], seen.up("down_ready", 0))

                def load(u, q, free):
                    if free:
                        sp.wait_ge(sig["down_ready"], seen.up("down_ready", 2))
                    sp.dma_start(WB[:, q, :], units[bass.ds(u, 1), :, :].rearrange("u p n -> (u p) n"))\
                        .then_inc(sig[f"unit_landed{q}"], 16)
                if layer == "l0f":
                    load(0, 0, False)
                    load(1, 1, False)
                    seen.loop(3, {"down_ready": 4}, lambda i: (load(i * 2 + 2, 0, True), load(i * 2 + 3, 1, True)))
                    load(8, 0, True)
                    seen.up("down_ready", 4)
                elif layer == "l2f":
                    load(u0, 0, False)
                    load(u0 + 1, 1, False)
                    for r in range(4):
                        seen.loop(3, {"down_ready": 4}, lambda i: (load(i * 2 + (u0 + 2), 0, True),
                                                                load(i * 2 + (u0 + 3), 1, True)))
                        if r < 3:
                            load(u0, 0, True)
                            load(u0 + 1, 1, True)
                    seen.up("down_ready", 4)
                else:
                    load(u0, 0, False)
                    load(u0 + 1, 1, False)
                    if nu == 4:
                        load(u0 + 2, 0, True)
                        load(u0 + 3, 1, True)
                    seen.up("down_ready", 4)

            def l0_load(s, q, first):
                if not (first and (isinstance(s, int) and s < 2)):
                    sp.wait_ge(sig["l0s_u"], seen.up("l0s_u"))
                d = sig[f"ctx_landed{q}"]
                src = ctxT[bass.ds(s * 4, 4), :, :].rearrange("j p k -> p j k")
                sp.dma_start(l0_cT[q], src).then_inc(d, 16)
                for c in range(2):
                    src = ctxN[bass.ds(s * 4, 4), c * P:(c + 1) * P, :].rearrange("j p f -> p j f")
                    sp.dma_start(l0_cn[q][:, :, c, :], src).then_inc(d, 16)
                src = ctxN[bass.ds(s * 4, 4), 2 * P:KEYS, :].rearrange("j p f -> p j f")
                sp.dma_start(l0_cl[q], src).then_inc(d, 16)
            l0_load(0, 0, True)
            l0_load(1, 1, True)
            seen.loop(L0X_STEPS // 2 - 1, {"l0s_u": 2},
                   lambda i: (l0_load(i * 2 + 2, 0, False), l0_load(i * 2 + 3, 1, False)))
            seen.up("l0s_u", 2)
            load_units("l0f")

            def l1_load(b, k, free):
                if free:
                    sp.wait_ge(sig["yu_ready"], seen.up("yu_ready"))
                d = sig[f"ctx_landed{k}"]
                sp.dma_start(c_T[k], ctxT[bass.ds(b, 1), :, :].rearrange("j p k -> (j p) k")).then_inc(d, 16)
                src = ctxN[bass.ds(b, 1), 0:2 * P, :].rearrange("j (c p) f -> (j p) c f", c=2)
                sp.dma_start(c_N[k], src).then_inc(d, 16)
                sp.dma_start(y_last[k][0:1, :], ctxN[bass.ds(b, 1), 2 * P:KEYS, :].rearrange("j p f -> (j p) f"))\
                    .then_inc(d, 16)

            def l1_loads(c, free):
                for k in range(4):
                    l1_load(c * 4 + k, k, free)
            sp.wait_ge(sig["l0s_u"], seen.up("l0s_u", 0))
            sp.wait_ge(sig["y_padded"], 1)
            l1_loads(0, False)
            seen.loop(B // 4 - 1, {"yu_ready": 4}, lambda i: l1_loads(i + 1, True))
            seen.up("yu_ready", 4)
            load_units("l1f")

            def x_load(b, k, free, with_bias):
                if free:
                    sp.wait_ge(sig["xmax"], seen.up("xmax"))
                    sp.wait_ge(sig["xs_ready"], seen.up("xs_ready"))
                d = sig[f"ctx_landed{k}"]
                sp.dma_start(c_T[k], ctxT[bass.ds(b, 1), :, :].rearrange("j p k -> (j p) k")).then_inc(d, 16)
                if with_bias:
                    src = fside[bass.ds(b, 1), :, :].rearrange("j (g p) k -> (j p) g k", g=HG)
                    sp.dma_start(c_F[k], src).then_inc(d, 16)

            def x_loads(with_bias):
                for k in range(4):
                    x_load(k, k, False, with_bias)
                seen.loop(B // 4 - 1, {"xmax": 4, "xs_ready": 4},
                          lambda i: [x_load(i * 4 + (4 + k), k, True, with_bias) for k in range(4)])
                seen.up("xmax", 4)
                seen.up("xs_ready", 4)
            sp.wait_ge(sig["yu_ready"], seen.up("yu_ready", 0))
            x_loads(True)
            load_units("l2x")
            load_units("l2f")
            sp.wait_ge(sig["xmax"], seen.up("xmax", 0))
            sp.wait_ge(sig["xs_ready"], seen.up("xs_ready", 0))
            x_loads(False)
            load_units("l3f")
            sp.wait_ge(sig["resid_done"], seen.up("resid_done", 12))
            sp.dma_start(out, X[:, :, :]).then_inc(sig["out_landed"], 16)
            sp.wait_ge(sig["out_landed"], 16)

        @block.tensor
        def _(pe):
            seen = Tally(pe)
            bank = lambda k: PS[:, k, :]

            def turn(src, ready="norm_ready"):
                if ready == "stream_ready":
                    pe.wait_ge(sig[ready], seen.up(ready))
                for t in range(NT):
                    if ready == "norm_ready":
                        pe.wait_ge(sig[ready], seen.up(ready))
                    m = pe.transpose(PS[:, t // 4, 128 * (t % 4):128 * (t % 4) + 128], src[:, t, :], ident)
                m.then_inc(sig["turned"], 1)
                pe.wait_ge(sig["turned_taken"], seen.up("turned_taken"))

            def wide(k, weight, src):
                for hh in range(2):
                    m = pe.matmul(bank(k + hh), weight, src[:, 512 * hh:512 * hh + 512], start=True, stop=True)
                return m

            def project(src, weight):
                for t in range(NT):
                    m = pe.matmul(PS[:, 6 + t // 4, 128 * (t % 4):128 * (t % 4) + 128],
                                  src[:, P * t:P * t + P], weight, start=True, stop=True)
                m.then_inc(sig["proj_ready"], 1)

            def ff(layer, src):
                gated = LAYERS_FF[layer][0]
                u0, nu = FF_UNITS[layer]
                def up(q, hh, first=False):
                    if hh == 0:
                        pe.wait_ge(sig[f"unit_landed{q}"], seen.up(f"unit_landed{q}", 16))
                    for c in range(2):
                        if not first:
                            pe.wait_ge(sig["h_ready"], seen.up("h_ready"))
                        m = pe.matmul(bank(2 * c), WB[:, q, 128 * c:128 * c + 128],
                                      src[:, 512 * hh:512 * hh + 512], start=True, stop=True)
                        if gated:
                            m = pe.matmul(bank(2 * c + 1), WB[:, q, UNIT + 128 * c:UNIT + 128 * c + 128],
                                          src[:, 512 * hh:512 * hh + 512], start=True, stop=True)
                        m.then_inc(sig["up_ready"], 1)

                def down(q, hh, first=False):
                    if not first:
                        pe.wait_ge(sig["down_used"], seen.up("down_used"))
                    for t in range(4):
                        for c in range(2):
                            m = pe.matmul(PS[:, 4 + hh, 128 * t:128 * t + 128],
                                          f_h[hh][:, c, 128 * t:128 * t + 128],
                                          WB[:, q, 2 * UNIT + 128 * c:2 * UNIT + 128 * c + 128],
                                          start=(c == 0), stop=(c == 1))
                    m.then_inc(sig["down_ready"], 1)

                up(0, 0, first=True)
                up(0, 1)
                down(0, 0, first=True)
                up(1, 0)
                down(0, 1, first=True)

                def body(i):
                    up(1, 1)
                    down(1, 0)
                    up(0, 0)
                    down(1, 1)
                    up(0, 1)
                    down(0, 0)
                    up(1, 0)
                    down(0, 1)
                trips = (nu - 2) // 2
                if trips > 0:
                    seen.loop(trips, {"unit_landed0": 16, "unit_landed1": 16, "h_ready": 8, "down_used": 4}, body)
                up(1, 1)
                down(1, 0)
                if nu % 2:
                    up(0, 0)
                    down(1, 1)
                    up(0, 1)
                    down(0, 0)
                    pe.wait_ge(sig["h_ready"], seen.up("h_ready", 2))
                    down(0, 1)
                else:
                    pe.wait_ge(sig["h_ready"], seen.up("h_ready", 2))
                    down(1, 1)
                pe.wait_ge(sig["down_used"], seen.up("down_used", 2))

            pe.wait_ge(sig["w_first"], 16)
            turn(XN)
            wide(2, w("l0x_q"), XNT).then_inc(sig["lin_ready"], 1)
            pe.wait_ge(sig["lin_taken"], seen.up("lin_taken"))
            wide(4, w("l0x_k"), l0_qt).then_inc(sig["lin_ready"], 1)

            def l0_front(s, q, first):
                pe.wait_ge(sig[f"ctx_landed{q}"], seen.up(f"ctx_landed{q}", 64))
                pe.wait_ge(sig["l0s_staged"], seen.up("l0s_staged"))
                if not (isinstance(s, int) and s == 0):
                    pe.wait_ge(sig["l0s_exp"], seen.up("l0s_exp"))
                for j in range(4):
                    m = pe.matmul(PS[32 * j:32 * j + 32, 0, 0:KEYS], l0_qs[q][:, 32 * j:32 * j + 32],
                                  l0_cT[q][:, j, 0:KEYS], start=True, stop=True)
                m.then_inc(sig["l0s_scores"], 1)

            def l0_back(s, q, first):
                pe.wait_ge(sig["l0s_probs"], seen.up("l0s_probs"))
                for c in range(2):
                    m = pe.transpose(PS[:, 1, 128 * c:128 * c + 128], l0_p[q][:, 128 * c:128 * c + 128], ident)
                m = pe.transpose(PS[0:1, 1, 256:384], l0_p[q][:, 256:257], ident)
                m.then_inc(sig["l0s_pt"], 1)
                pe.wait_ge(sig["l0s_pt_taken"], seen.up("l0s_pt_taken"))
                if not (isinstance(s, int) and s == 0):
                    pe.wait_ge(sig["l0s_u_taken"], seen.up("l0s_u_taken"))
                for j in range(4):
                    for c in range(2):
                        pe.matmul(PS[:, 2, 32 * j:32 * j + 32], l0_cn[q][:, j, c, 0:P],
                                  l0_pt[q][:, c, 32 * j:32 * j + 32], start=(c == 0), stop=False)
                    m = pe.matmul(PS[:, 2, 32 * j:32 * j + 32], l0_cl[q][0:1, j, 0:P],
                                  l0_pt[q][0:1, 2, 32 * j:32 * j + 32], start=False, stop=True)
                m.then_inc(sig["l0s_u"], 1)
            seen.skewed(L0X_STEPS, {"ctx_landed0": 64, "ctx_landed1": 64, "l0s_staged": 2, "l0s_exp": 2,
                                 "l0s_probs": 2, "l0s_pt_taken": 2,
                                 "l0s_u_taken": 2}, None, l0_front, l0_back)
            seen.up("l0s_exp")
            pe.wait_ge(sig["l0s_u_taken"], seen.up("l0s_u_taken"))
            wide(4, w("l0x_v"), l0_ut).then_inc(sig["lin_ready"], 1)
            pe.wait_ge(sig["lin_taken"], seen.up("lin_taken"))
            project(l0_ct, w("l0x_o"))

            pe.wait_ge(sig["w_l0"], 16)
            turn(XN)
            for t in range(NT):
                m = pe.matmul(bank(t), XNT[:, P * t:P * t + P], w("l0a_qkvg"), start=True, stop=True)
                m.then_inc(sig["l0a_mm"], 1)
            pe.wait_ge(sig["l0a_qk"], seen.up("l0a_qk", 2))
            lk = ar(0, 2048).rearrange("p (t n) -> p t n", t=NT)
            for hh in range(2):
                m = pe.matmul(bank(hh), w("blockones"), lk[:, 4 * hh:4 * hh + 4, 128:256], start=True, stop=True)
            m.then_inc(sig["l0a_ksum"], 1)
            turn(Z, "stream_ready")
            project(ZT, w("l0a_o"))

            turn(XN)
            for t in range(NT):
                m = pe.matmul(PS[:, 6, 8 * t:8 * t + 8], XNT[:, P * t:P * t + P], w("l0f_gate"),
                              start=True, stop=True)
            m.then_inc(sig["gate_mm"], 1)
            ff("l0f", XNT)

            pe.wait_ge(sig["l1x_w_landed"], 16)
            pe.wait_ge(sig["resid_done"], seen.up("resid_done", 3))
            for m_out in range(2):
                for odd in range(2):
                    r = slice(64 * odd, 64 * odd + 64)
                    for k in range(2):
                        for e in range(4):
                            m = pe.matmul(PS[:, 4 * m_out + 2 * odd + k, 128 * e:128 * e + 128],
                                          y_w[r, 2 * m_out, 4 * k + e, :], y_w[r, 2 * m_out + 1, 4 * k + e, :],
                                          start=True, stop=True)
                        m.then_inc(sig["y_w_ready"], 1)
            pe.wait_ge(sig["y_w_taken"], seen.up("y_w_taken", 8))
            turn(XN)

            def y_q(c, j):
                if j >= 2:
                    pe.wait_ge(sig["yq_taken"], seen.up("yq_taken"))
                elif j == 1 and not (isinstance(c, int) and c < 2):
                    pe.wait_ge(sig["yo_taken"], seen.up("yo_taken"))
                for e in range(4):
                    m = pe.matmul(PS[:, 7 * (j % 2), P * e:P * e + P], y_A[:, y_at(4 * j + e), :],
                                  XNT[:, bass.ds(c * P, P)], start=True, stop=True)
                m.then_inc(sig["yq_ready"], 1)

            def y_s(k, first):
                pe.wait_ge(sig[f"ctx_landed{k}"], seen.up(f"ctx_landed{k}", 48))
                if k == 0:
                    pe.wait_ge(sig["yq_taken"], seen.up("yq_taken", 2))
                if not (first and k == 0):
                    pe.wait_ge(sig["yclip"], seen.up("yclip"))
                rhs = y_Q[:, k, :, :].rearrange("p h n -> p (h n)")
                for c in range(2):
                    pe.matmul(bank(1 + c), c_T[k][:, P * c:P * c + P], rhs, start=True, stop=True)
                m = pe.matmul(PS[0:1, 3, :], c_T[k][:, 256:257], rhs, start=True, stop=True)
                m.then_inc(sig["ys_ready"], 1)

            def y_t(k, first):
                pe.wait_ge(sig["yu_taken"], seen.up("yu_taken"))
                if k > 0:
                    pe.wait_ge(sig["yt_taken"], seen.up("yt_taken"))
                for g in range(HG):
                    m = pe.transpose(PS[:, 6, P * g:P * g + P], y_U[:, g, :], ident)
                m.then_inc(sig["yt_ready"], 1)

            def y_u(k):
                q = k % 2
                pe.wait_ge(sig["yexp"], seen.up("yexp"))
                for g in range(HG):
                    o = PS[:, 4 + g // 2, FQ * (g % 2):FQ * (g % 2) + FQ]
                    for c in range(3):
                        m = pe.matmul(o, y_P[q][:, c, P * g:P * g + P], y_last[k] if c == 2 else c_N[k][:, c, :],
                                      start=(c == 0), stop=(c == 2))
                m.then_inc(sig["yu_ready"], 1)

            def y_o():
                pe.wait_ge(sig["yt_taken"], seen.up("yt_taken"))
                for h in range(H):
                    m = pe.matmul(PS[:, 7, 0:P], y_M[:, y_at(h), :], y_V[:, h, :, :].rearrange("p b n -> p (b n)"),
                                  start=(h == 0), stop=(h == H - 1))
                m.then_inc(sig["yo_ready"], 1)

            def y_chunk(c, first=False, last=False):
                for k in range(4):
                    y_s(k, first)
                    if k == 3 and not last:
                        y_q(c + 1, 0)
                        y_q(c + 1, 1)
                    if not first or k >= 2:
                        y_t((k - 2) % 4, first)
                    if k == 3 and not last:
                        y_q(c + 1, 2)
                        y_q(c + 1, 3)
                    if not first or k >= 1:
                        y_u((k - 1) % 4)
                    if k == 1 and not first:
                        y_o()

            for j in range(4):
                y_q(0, j)
            y_chunk(0, first=True)
            y_chunk(1)
            seen.loop(B // 4 - 3, {f"ctx_landed{k}": 48 for k in range(4)} | {k: 4 for k in (
                "yq_taken", "yclip", "yexp", "yu_taken", "yt_taken")} | {"yo_taken": 1}, lambda i: y_chunk(i + 2))
            y_chunk(B // 4 - 1, last=True)
            y_t(2, False)
            y_u(3)
            y_t(3, False)
            pe.wait_ge(sig["yo_taken"], seen.up("yo_taken"))
            y_o()
            seen.up("yclip")
            pe.wait_ge(sig["yo_taken"], seen.up("yo_taken"))
            for t in range(NT):
                m = pe.transpose(PS[:, 6 + t // 4, 128 * (t % 4):128 * (t % 4) + 128], OT[:, P * t:P * t + P], ident)
            m.then_inc(sig["proj_ready"], 1)

            def core():
                pe.wait_ge(sig["c_in"], seen.up("c_in"))
                for half in range(2):
                    for nn in range(16):
                        n = 16 * half + nn
                        for g in range(HG):
                            r = slice(32 * g, 32 * g + 32)
                            m = pe.matmul(PS[:, g, 32 * nn:32 * nn + 32], c_qb[r, P * n:P * n + P],
                                          c_k[r, 32 * n:32 * n + 32], start=True, stop=True)
                    m.then_inc(sig["c_scores"], 1)
                    pe.wait_ge(sig["c_probs"], seen.up("c_probs"))
                    for nn in range(16):
                        m = pe.transpose(PS[:, 4 + nn // 4, 128 * (nn % 4):128 * (nn % 4) + 128],
                                         c_p2[:, P * nn:P * nn + P], ident)
                    m.then_inc(sig["c_pt"], 1)
                    pe.wait_ge(sig["c_pt_taken"], seen.up("c_pt_taken"))
                    for nn in range(16):
                        n = 16 * half + nn
                        for g in range(HG):
                            r = slice(32 * g, 32 * g + 32)
                            m = pe.matmul(PS[r, nn // 4, 128 * (nn % 4):128 * (nn % 4) + 128],
                                          c_vt[r, 32 * n:32 * n + 32], c_pt[r, P * nn:P * nn + P],
                                          start=True, stop=True)
                    m.then_inc(sig["c_pv"], 1)
                    pe.wait_ge(sig["c_masked"], seen.up("c_masked"))

            def self_attention(q, k, v, o):
                turn(XN)
                wide(2, w(q), XNT)
                wide(4, w(k), XNT)
                wide(6, w(v), XNT).then_inc(sig["lin_ready"], 1)
                core()
                project(OT, w(o))

            pe.wait_ge(sig["w_l1"], 16)
            self_attention("l1a_q", "l1a_k", "l1a_v", "l1a_o")

            turn(XN)
            for t in range(NT):
                m = pe.matmul(PS[:, 6, 4 * t:4 * t + 4], XNT[:, P * t:P * t + P], w("l1f_gate"),
                              start=True, stop=True)
            for hh in range(2):
                m = pe.matmul(PS[0:64, 2 + hh, :], w("l1f_dp1"), XNT[:, 512 * hh:512 * hh + 512],
                              start=True, stop=True)
            m.then_inc(sig["gate_mm"], 1)
            pe.wait_ge(sig["gate_hidden"], seen.up("gate_hidden"))
            for t in range(NT):
                m = pe.matmul(PS[:, 7, t:t + 1], g_h[0:64, P * t:P * t + P], w("l1f_dp2")[0:64, :],
                              start=True, stop=True)
            m.then_inc(sig["gate_mm"], 1)
            ff("l1f", XNT)

            def cross(kname, vname, biased):
                def x_kv(k, first):
                    pe.wait_ge(sig[f"ctx_landed{k}"], seen.up(f"ctx_landed{k}", 32 if biased else 16))
                    m = pe.matmul(PS[:, 0, 0:KEYS], w(kname), c_T[k][:, 0:KEYS], start=True, stop=True)
                    m.then_inc(sig["xk_ready"], 1)
                    if not first:
                        pe.wait_ge(sig["xpl_taken"], seen.up("xpl_taken"))
                    for c in range(2):
                        pe.matmul(PS[:, 1, P * c:P * c + P], c_T[k][:, P * c:P * c + P], w(vname),
                                  start=True, stop=True)
                    m = pe.matmul(PS[0:4, 1, 256:384], c_T[k][:, 256:260], w(vname), start=True, stop=True)
                    m.then_inc(sig["xv_ready"], 1)

                def x_s(q, first):
                    pe.wait_ge(sig["xk_taken"], seen.up("xk_taken"))
                    pe.wait_ge(sig["xqb"], seen.up("xqb"))
                    if not first and biased:
                        pe.wait_ge(sig["xs_added"], seen.up("xs_added"))
                    elif not first:
                        pe.wait_ge(sig["xexp"], seen.up("xexp"))
                    for g in range(HG):
                        m = pe.matmul(PS[:, 2 + g, 0:KEYS], x_qb[q][:, P * g:P * g + P], x_k[q],
                                      start=True, stop=True)
                    m.then_inc(sig["xs_ready"], 1)

                def x_turn(q, first, last=False):
                    if biased or last:
                        pe.wait_ge(sig["xexp"], seen.up("xexp"))
                    if not last:
                        pe.wait_ge(sig["xv_taken"], seen.up("xv_taken"))
                        pe.wait_ge(sig["xvl_taken"], seen.up("xvl_taken"))
                    if not first:
                        pe.wait_ge(sig["x_out"], seen.up("x_out"))
                    m = pe.transpose(PS[0:4, 1, 384:512], x_p[q][:, :, 256], ident)
                    m.then_inc(sig["xpl_ready"], 1)
                    for c in range(2):
                        for g in range(HG):
                            m = pe.transpose(PS[:, 6 + c, P * g:P * g + P], x_p[q][:, g, P * c:P * c + P], ident)
                    m.then_inc(sig["xpt_ready"], 1)

                def x_pv(k, last=False):
                    q = k % 2
                    if last:
                        pe.wait_ge(sig["xpl_taken"], seen.up("xpl_taken"))
                    pe.wait_ge(sig["xsum_spread"], seen.up("xsum_spread"))
                    pe.wait_ge(sig["xpt_a"], seen.up("xpt_a"))
                    pe.wait_ge(sig["xpt_d"], seen.up("xpt_d"))
                    pe.matmul(PS[:, 7, 0:32], x_r[q], w("fold"), start=True, stop=True)
                    for g in range(HG):
                        for c in range(2):
                            pe.matmul(PS[32 * g:32 * g + 32, 6, 0:128], x_v[k][:, c, 32 * g:32 * g + 32],
                                      x_pt[:, c, P * g:P * g + P], start=(c == 0), stop=False,
                                      skip_group_check=True)
                    m = pe.matmul(PS[:, 6, 0:128], x_vl[k][0:4, :], x_pl[0:4, :], start=False, stop=True,
                                  skip_group_check=True)
                    m.then_inc(sig["xu_ready"], 1)

                def x_four(first=False, last=False):
                    for k in range(4):
                        x_s(k % 2, first and k == 0)
                        if not (first and k == 0):
                            x_turn((k - 1) % 2, first and k == 1)
                        if first and k == 0:
                            pe.wait_ge(sig["xv_taken"], seen.up("xv_taken"))
                            pe.wait_ge(sig["xvl_taken"], seen.up("xvl_taken"))
                        end = last and k == 3
                        if not end:
                            x_kv((k + 1) % 4, first and k == 0)
                        if not (first and k == 0):
                            x_pv((k - 1) % 4, last=end)

                x_kv(0, True)
                x_four(first=True)
                seen.loop(B // 4 - 2, {f"ctx_landed{k}": 32 if biased else 16 for k in range(4)} |
                          ({"xs_added": 4} if biased else {}) |
                          {k: 4 for k in "xk_taken xv_taken xvl_taken xqb xexp xpl_taken xpt_a xpt_d xsum_spread "
                                         "x_out".split()}, lambda i: x_four())
                x_four(last=True)
                x_turn(1, False, last=True)
                x_pv(3, last=True)
                if biased:
                    seen.up("xs_added")
                pe.wait_ge(sig["x_out"], seen.up("x_out", 1 if biased else 2))

            pe.wait_ge(sig["w_l2"], 16)
            turn(XN)
            wide(2, w("l2x_q"), XNT).then_inc(sig["xq_mm"], 1)
            cross("l2x_k", "l2x_v", True)
            project(OT, w("l2x_o"))
            turn(Z, "stream_ready")
            ff("l2x", ZT)

            turn(XN)
            for name in ("l2a_q", "l2a_k", "l2a_v"):
                for cc in range(2):
                    if not (name == "l2a_q" and cc == 0):
                        pe.wait_ge(sig["pair_taken"], seen.up("pair_taken"))
                    for c in range(8):
                        for u in range(4):
                            m = pe.matmul(PS[32 * u:32 * u + 32, c // 2, 256 * (c % 2):256 * (c % 2) + 256],
                                          w(name)[:, 32 * (8 * cc + c):32 * (8 * cc + c) + 32],
                                          XNT[:, 256 * u:256 * u + 256], start=True, stop=True)
                    m.then_inc(sig["pair_ready"], 1)
            pe.wait_ge(sig["pair_taken"], seen.up("pair_taken"))
            core()
            big = c_big.rearrange("p (m j r c) -> p m j r c", m=32, j=4, r=2)
            for c in range(H):
                for u in range(4):
                    r = slice(32 * u, 32 * u + 32)
                    rhs = big[r, :, :, :, c].rearrange("p m j r -> p (m j) r")
                    m = pe.matmul(PS[:, 4 + u, 0:256], w("l2a_o")[r, P * c:P * c + P], rhs,
                                  start=(c == 0), stop=(c == H - 1))
            m.then_inc(sig["lin_ready"], 1)
            pe.wait_ge(sig["lin_taken"], seen.up("lin_taken"))
            for t in range(NT):
                m = pe.transpose(PS[:, 2 + t // 4, 128 * (t % 4):128 * (t % 4) + 128], ZT[:, P * t:P * t + P], ident)
            m.then_inc(sig["proj_ready"], 1)
            turn(Z)
            wide(2, w("l2a_w1"), ZT).then_inc(sig["lin_ready"], 1)
            pe.wait_ge(sig["lin_taken"], seen.up("lin_taken"))
            project(OT, w("l2a_w2"))

            def moe_round(r):
                turn(XN) if r == 0 else turn(Y, "stream_ready")
                src = XNT if r == 0 else ZT
                for t in range(NT):
                    m = pe.matmul(PS[:, 6, 4 * t:4 * t + 4], src[:, P * t:P * t + P],
                                  w("l2f_gate")[:, 4 * r:4 * r + 4], start=True, stop=True)
                m.then_inc(sig["gate_mm"], 1)
                ff("l2f", src)
            for r in range(4):
                moe_round(r)

            pe.wait_ge(sig["w_l3"], 16)
            turn(XN)
            wide(2, w("l3x_q"), XNT).then_inc(sig["xq_mm"], 1)
            cross("l3x_k", "l3x_v", False)
            project(OT, w("l3x_o"))
            self_attention("l3a_q", "l3a_k", "l3a_v", "l3a_o")
            turn(XN)
            wide(6, w("l3f_u1"), XNT).then_inc(sig["lin_ready"], 1)
            pe.wait_ge(sig["lin_taken"], seen.up("lin_taken"))
            ff("l3f", f_pt)
            turn(ACC, None)
            project(ZT, w("l3f_v2"))

        @block.scalar
        def _(act):
            seen = Tally(act)

            def f(o, i, fn=ACT.Identity, **k):
                return act.activation(o, i, fn, **k)

            def norm_std():
                act.wait_ge(sig["var_ready"], seen.up("var_ready"))
                f(SD[:, 1, :], SD[:, 0, :], ACT.Sqrt).then_inc(sig["std_ready"], 1)
                act.wait_ge(sig["std_ready"], seen.up("std_ready"))

            def turned(dst):
                act.wait_ge(sig["turned"], seen.up("turned"))
                act.copy(dst, PSF[:, 0:TOK]).then_inc(sig["turned_taken"], 1)
                act.wait_ge(sig["turned_taken"], seen.up("turned_taken"))

            def ff(layer, rows=None):
                gated, fn, _ = LAYERS_FF[layer]
                nu = FF_UNITS[layer][1]

                def half(q, hh, landed=False):
                    if gated:
                        for c in range(2):
                            act.wait_ge(sig["up_ready"], seen.up("up_ready"))
                            if not landed:
                                act.wait_ge(sig["h_ready"], seen.up("h_ready"))
                            f(f_s[c], PS[:, 2 * c, :], fn).then_inc(sig["act_half"], 1)
                            act.wait_ge(sig["act_half"], seen.up("act_half"))
                        return
                    for c in range(2):
                        act.wait_ge(sig["up_ready"], seen.up("up_ready"))
                        if c == 0 and not landed:
                            act.wait_ge(sig["down_ready"], seen.up("down_ready"))
                        f(f_h[hh][:, c, :], PS[:, 2 * c, :], fn,
                                 bias=WB[:, q, 3 * UNIT + c:3 * UNIT + c + 1]).then_inc(sig["h_ready"], 1)
                        act.wait_ge(sig["h_ready"], seen.up("h_ready"))
                half(0, 0, True)
                half(0, 1, not gated)
                trips = (nu - 2) // 2
                if trips > 0:
                    def body(i):
                        for q in (1, 0):
                            for hh in range(2):
                                half(q, hh)
                    per = {"up_ready": 8, "act_half": 8, "h_ready": 8} if gated else \
                        {"up_ready": 8, "h_ready": 8, "down_ready": 4}
                    seen.loop(trips, per, body)
                half(1, 0)
                half(1, 1)
                if nu % 2:
                    half(0, 0)
                    half(0, 1)
                if gated:
                    seen.up("h_ready", 2)
                    seen.up("down_ready", 2 * nu)
                else:
                    seen.up("down_ready", 2)

            act.wait_ge(sig["w_first"], 16)
            norm_std()
            turned(XNT[:, :])
            act.wait_ge(sig["lin_ready"], seen.up("lin_ready"))
            f(l0_qt, PSF[:, 1024:2048], bias=col("l0x_bq")).then_inc(sig["lin_taken"], 1)
            act.wait_ge(sig["lin_taken"], seen.up("lin_taken"))
            act.wait_ge(sig["lin_ready"], seen.up("lin_ready"))
            f(l0_qp, PSF[:, 2048:3072], scale=float(P) ** -0.5).then_inc(sig["l0s_q_ready"], 1)
            act.wait_ge(sig["l0s_q_ready"], seen.up("l0s_q_ready"))

            def l0_exp(s, q, first):
                act.wait_ge(sig["l0s_max"], seen.up("l0s_max"))
                if not (isinstance(s, int) and s < 2):
                    act.wait_ge(sig["l0s_pt"], seen.up("l0s_pt"))
                f(l0_p[q], PS[:, 0, 0:KEYS], ACT.Exp, bias=l0_neg[q], accum_out=l0_sum[q]).then_inc(sig["l0s_exp"], 1)
                act.wait_ge(sig["l0s_exp"], seen.up("l0s_exp"))
            l0_exp(0, 0, True)
            l0_exp(1, 1, True)
            seen.loop(L0X_STEPS // 2 - 1, {"l0s_max": 2, "l0s_pt": 2, "l0s_exp": 2},
                   lambda i: (l0_exp(None, 0, False), l0_exp(None, 1, False)))
            seen.up("l0s_pt", 2)
            act.wait_ge(sig["lin_ready"], seen.up("lin_ready"))
            f(l0_ct, PSF[:, 2048:3072], bias=col("l0x_bv")).then_inc(sig["lin_taken"], 1)
            act.wait_ge(sig["lin_taken"], seen.up("lin_taken"))

            norm_std()
            turned(XNT[:, :])
            le = ar(2048, 2048).rearrange("p (t n) -> p t n", t=NT)
            lv = ar(4096, 1024).rearrange("p (t n) -> p t n", t=NT)
            lg = ar(5120, 1024).rearrange("p (t n) -> p t n", t=NT)
            act.wait_ge(sig["l0a_mm"], seen.up("l0a_mm", NT))
            f(le, PS[:, :, 0:256], ACT.Exp).then_inc(sig["act_ran"], 1)
            act.wait_ge(sig["act_ran"], seen.up("act_ran"))
            act.copy(lv, PS[:, :, 256:384]).then_inc(sig["act_ran"], 1)
            act.wait_ge(sig["act_ran"], seen.up("act_ran"))
            f(lg, PS[:, :, 384:512], ACT.Silu).then_inc(sig["l0a_act"], 1)
            act.wait_ge(sig["l0a_act"], seen.up("l0a_act"))
            norm_std()
            turned(ZT[:, :])

            norm_std()
            turned(XNT[:, :])
            act.wait_ge(sig["gate_mm"], seen.up("gate_mm"))
            f(g_e, PS[:, 6, 0:64], ACT.Sigmoid).then_inc(sig["gate_act"], 1)
            act.wait_ge(sig["gate_act"], seen.up("gate_act"))
            ff("l0f")

            for k in range(8):
                act.wait_ge(sig["y_w_ready"], seen.up("y_w_ready"))
                if k < 4:
                    dst, sc = y_A[:, 4 * k:4 * k + 4, :], float(DH1) ** -0.5
                else:
                    dst, sc = y_M[:, 4 * k - 16:4 * k - 12, :], 1.0
                f(dst, PS[:, k, :].rearrange("p (h n) -> p h n", h=4), scale=sc).then_inc(sig["y_w_taken"], 1)
                act.wait_ge(sig["y_w_taken"], seen.up("y_w_taken"))
            norm_std()
            turned(XNT[:, :])

            def y_q(j, first):
                act.wait_ge(sig["yq_ready"], seen.up("yq_ready"))
                if j == 0 and not first:
                    act.wait_ge(sig["ys_ready"], seen.up("ys_ready", 4))
                act.copy(y_Q[:, :, 4 * j:4 * j + 4, :],
                         PS[:, 7 * (j % 2), :].rearrange("p (h b n) -> p b h n", h=4, b=4)).then_inc(sig["yq_taken"], 1)
                act.wait_ge(sig["yq_taken"], seen.up("yq_taken"))

            def y_exp(k, first):
                q = k % 2
                act.wait_ge(sig["yclip"], seen.up("yclip"))
                if not (first and k < 2):
                    act.wait_ge(sig["yu_ready"], seen.up("yu_ready"))
                f(y_P[q][:, 0:2, :], y_C[:, 0:2, :], ACT.Exp).then_inc(sig["act_ran"], 1)
                act.wait_ge(sig["act_ran"], seen.up("act_ran"))
                f(y_P[q][0:1, 2, :], y_C[0:1, 2, :], ACT.Exp).then_inc(sig["yexp"], 1)
                act.wait_ge(sig["yexp"], seen.up("yexp"))

            def y_t(k, first):
                act.wait_ge(sig["yt_ready"], seen.up("yt_ready"))
                if k == 0 and not first:
                    act.wait_ge(sig["yo_ready"], seen.up("yo_ready"))
                act.copy(y_V[:, :, k, :], PS[:, 6, :].rearrange("p (h n) -> p h n", h=H)).then_inc(sig["yt_taken"], 1)
                act.wait_ge(sig["yt_taken"], seen.up("yt_taken"))

            def y_chunk(first=False, last=False):
                for k in range(4):
                    if k == 3 and not last:
                        y_q(0, False)
                        y_q(1, False)
                    if not first or k >= 2:
                        y_t((k - 2) % 4, first)
                    if k == 3 and not last:
                        y_q(2, False)
                        y_q(3, False)
                    y_exp(k, first)
            act.wait_ge(sig["y_padded"], 1)
            for j in range(4):
                y_q(j, True)
            y_chunk(first=True)
            seen.loop(B // 4 - 2, {k: 4 for k in ("yq_ready", "ys_ready", "yq_taken", "yclip", "yu_ready", "act_ran",
                                                  "yexp", "yt_ready", "yt_taken")} | {"yo_ready": 1},
                      lambda i: y_chunk())
            y_chunk(last=True)
            y_t(2, False)
            y_t(3, False)
            seen.up("ys_ready", 4)
            seen.up("yu_ready", 2)
            seen.up("yo_ready")

            def core():
                for half in range(2):
                    act.wait_ge(sig["c_shift"], seen.up("c_shift"))
                    f(c_p, c_p, ACT.Exp).then_inc(sig["c_exp"], 1)
                    act.wait_ge(sig["c_exp"], seen.up("c_exp"))
                    act.wait_ge(sig["c_pt"], seen.up("c_pt"))
                    if half:
                        act.wait_ge(sig["c_pv"], seen.up("c_pv", 0))
                    act.copy(c_pt, PSF[:, 2048:4096]).then_inc(sig["c_pt_taken"], 1)
                    act.wait_ge(sig["c_pt_taken"], seen.up("c_pt_taken"))
                    seen.up("c_pv")

            def self_attention(scale, second_norm=False):
                norm_std()
                turned(XNT[:, :])
                act.wait_ge(sig["lin_ready"], seen.up("lin_ready"))
                f(c_q, PSF[:, 1024:2048], scale=scale).then_inc(sig["act_ran"], 1)
                act.wait_ge(sig["act_ran"], seen.up("act_ran"))
                act.copy(c_k, PSF[:, 2048:3072]).then_inc(sig["act_ran"], 1)
                act.wait_ge(sig["act_ran"], seen.up("act_ran"))
                act.copy(c_v, PSF[:, 3072:4096]).then_inc(sig["qkv_taken"], 1)
                act.wait_ge(sig["qkv_taken"], seen.up("qkv_taken"))
                if second_norm:
                    norm_std()
                core()

            self_attention(float(DK) ** -0.5)

            norm_std()
            turned(XNT[:, :])
            act.wait_ge(sig["gate_mm"], seen.up("gate_mm"))
            f(g_h[0:64, :], PSF[0:64, 1024:2048], ACT.Relu, bias=col("l1f_dpb1")[0:64, :]).then_inc(sig["gate_hidden"], 1)
            act.wait_ge(sig["gate_hidden"], seen.up("gate_hidden"))
            act.wait_ge(sig["gate_entropy"], seen.up("gate_entropy"))
            f(g_z[:, 2, :], g_z[:, 1, :], ACT.Exp, scale=-1.0).then_inc(sig["gate_act"], 1)
            act.wait_ge(sig["gate_act"], seen.up("gate_act"))
            f(g_z[:, 3, :], g_z[:, 2, :], ACT.Ln, bias=SM[:, 500:501]).then_inc(sig["gate_act"], 1)
            act.wait_ge(sig["gate_act"], seen.up("gate_act"))
            act.wait_ge(sig["gate_shift"], seen.up("gate_shift"))
            f(g_e[:, 0:32], g_e[:, 0:32], ACT.Exp).then_inc(sig["gate_act"], 1)
            act.wait_ge(sig["gate_act"], seen.up("gate_act"))
            ff("l1f")

            def cross(bk):
                def x_kv(k):
                    act.wait_ge(sig["xk_ready"], seen.up("xk_ready"))
                    f(x_k[k % 2], PS[:, 0, 0:KEYS], bias=col(bk) if bk else 0.0).then_inc(sig["xk_taken"], 1)
                    act.wait_ge(sig["xk_taken"], seen.up("xk_taken"))
                    act.wait_ge(sig["xv_ready"], seen.up("xv_ready"))
                    act.copy(x_v[k], PS[:, 1, 0:256].rearrange("p (c n) -> p c n", c=2)).then_inc(sig["xv_taken"], 1)
                    act.wait_ge(sig["xv_taken"], seen.up("xv_taken"))

                def x_turned():
                    act.wait_ge(sig["xpl_ready"], seen.up("xpl_ready"))
                    act.copy(x_pl[0:4, :], PS[0:4, 1, 384:512]).then_inc(sig["xpl_taken"], 1)
                    act.wait_ge(sig["xpl_taken"], seen.up("xpl_taken"))
                    act.wait_ge(sig["xpt_ready"], seen.up("xpt_ready"))
                    act.copy(x_pt[:, 0, :], PS[:, 6, :]).then_inc(sig["xpt_a"], 1)
                    act.wait_ge(sig["xpt_a"], seen.up("xpt_a"))

                def x_exp(q):
                    act.wait_ge(sig["xmax"], seen.up("xmax"))
                    for g in range(HG):
                        src = x_s[:, g, :] if not bk else PS[:, 2 + g, 0:KEYS]
                        ins = f(x_p[q][:, g, :], src, ACT.Exp, bias=x_neg[q][:, g:g + 1],
                                accum_out=x_sum[q][:, g:g + 1])
                        name = "xexp" if g == HG - 1 else "act_ran"
                        ins.then_inc(sig[name], 1)
                        act.wait_ge(sig[name], seen.up(name))

                def x_four(first=False, last=False):
                    for k in range(4):
                        if not (first and k == 0):
                            x_turned()
                        if not (last and k == 3):
                            x_kv((k + 1) % 4)
                        x_exp(k % 2)
                x_kv(0)
                x_four(first=True)
                seen.loop(B // 4 - 2, {"act_ran": 12} | {k: 4 for k in "xk_ready xk_taken xv_ready xv_taken xpl_ready "
                          "xpl_taken xpt_ready xpt_a xmax xexp".split()}, lambda i: x_four())
                x_four(last=True)
                x_turned()

            norm_std()
            turned(XNT[:, :])
            cross(None)
            norm_std()
            turned(ZT[:, :])
            ff("l2x")
            norm_std()

            norm_std()
            turned(XNT[:, :])
            core()
            act.wait_ge(sig["lin_ready"], seen.up("lin_ready"))
            act.copy(ZT[:, :].rearrange("p (u n) -> p u n", u=4), PS[:, 4:8, 0:256]).then_inc(sig["lin_taken"], 1)
            act.wait_ge(sig["lin_taken"], seen.up("lin_taken"))
            norm_std()
            turned(ZT[:, :])
            act.wait_ge(sig["lin_ready"], seen.up("lin_ready"))
            f(OT[:, :], PSF[:, 1024:2048], bias=col("l2a_b1")).then_inc(sig["lin_taken"], 1)
            act.wait_ge(sig["lin_taken"], seen.up("lin_taken"))
            norm_std()

            norm_std()
            for r in range(4):
                turned(XNT[:, :] if r == 0 else ZT[:, :])
                act.wait_ge(sig["gate_shift"], seen.up("gate_shift"))
                f(g_e[:, 0:32], g_e[:, 0:32], ACT.Exp).then_inc(sig["gate_act"], 1)
                act.wait_ge(sig["gate_act"], seen.up("gate_act"))
                ff("l2f")

            norm_std()
            turned(XNT[:, :])
            cross("l3x_bk")
            self_attention(float(DK) ** -0.5, True)
            norm_std()
            turned(XNT[:, :])
            act.wait_ge(sig["lin_ready"], seen.up("lin_ready"))
            act.copy(f_pt, PSF[:, 3072:4096]).then_inc(sig["lin_taken"], 1)
            act.wait_ge(sig["lin_taken"], seen.up("lin_taken"))
            ff("l3f")
            turned(ZT[:, :])

        @block.vector
        def _(dve):
            seen = Tally(dve)

            def tt(o, a, b, op):
                return dve.tensor_tensor(o, a, b, op)

            def layernorm(src, dst, eps, signal=True):
                for t in range(NT):
                    dve.bn_stats(ST[:, t, :], src[:, t, :]).then_inc(sig["dve_ran"], 1)
                    seen.up("dve_ran")
                    if t == NT - 1:
                        dve.wait_ge(sig["dve_ran"], seen.up("dve_ran", 0))
                for t in range(NT):
                    dve.bn_aggr(MV[:, t, :], ST[:, t, :]).then_inc(sig["dve_ran"], 1)
                    seen.up("dve_ran")
                    if t == NT - 1:
                        dve.wait_ge(sig["dve_ran"], seen.up("dve_ran", 0))
                dve.tensor_scalar(SD[:, 0, :], MV[:, :, 1], eps, None, ALU.add).then_inc(sig["var_ready"], 1)
                dve.wait_ge(sig["var_ready"], seen.up("var_ready"))
                dve.wait_ge(sig["std_ready"], seen.up("std_ready"))
                dve.reciprocal(SD[:, 1, :], SD[:, 1, :]).then_inc(sig["dve_ran"], 1)
                dve.wait_ge(sig["dve_ran"], seen.up("dve_ran"))
                for t in range(NT):
                    ins = dve.tensor_scalar(dst[:, t, :], src[:, t, :], MV[:, t, 0:1], SD[:, 1, t:t + 1],
                                            ALU.subtract, ALU.mult)
                    name = "norm_ready" if signal else "dve_ran"
                    ins.then_inc(sig[name], 1)
                    seen.up(name)
                    if t == NT - 1:
                        dve.wait_ge(sig[name], seen.up(name, 0))

            def affine(dst, g, b):
                tt(dst, dst, rows_t(g), ALU.mult).then_inc(sig["dve_ran"], 1)
                dve.wait_ge(sig["dve_ran"], seen.up("dve_ran"))
                return tt(dst, dst, rows_t(b), ALU.add)

            def residual():
                dve.wait_ge(sig["proj_ready"], seen.up("proj_ready"))
                tt(flat(X), PSF[:, 3072:4096], flat(X), ALU.add).then_inc(sig["resid_done"], 1)
                dve.wait_ge(sig["resid_done"], seen.up("resid_done"))

            def rank_gates(E, low):
                pairs = NT * E * E
                v = lambda a: a[:, 0:pairs].rearrange("p (t e j) -> p t e j", t=NT, e=E)
                gl = g_l[:, 0:NT * E].rearrange("p (t e) -> p t e", t=NT)
                other = gl.unsqueeze(2).broadcast_to([P, NT, E, E])
                own = gl.unsqueeze(3).broadcast_to([P, NT, E, E])
                lw = low.rearrange("p (e j) -> p e j", e=E).unsqueeze(1).broadcast_to([P, NT, E, E])
                tt(v(g_a), other, own, ALU.is_equal).then_inc(sig["dve_ran"], 1)
                dve.wait_ge(sig["dve_ran"], seen.up("dve_ran"))
                tt(v(g_a), v(g_a), lw, ALU.mult).then_inc(sig["dve_ran"], 1)
                dve.wait_ge(sig["dve_ran"], seen.up("dve_ran"))
                tt(v(g_b), other, own, ALU.is_gt).then_inc(sig["dve_ran"], 1)
                dve.wait_ge(sig["dve_ran"], seen.up("dve_ran"))
                tt(v(g_a), v(g_a), v(g_b), ALU.add).then_inc(sig["dve_ran"], 1)
                dve.wait_ge(sig["dve_ran"], seen.up("dve_ran"))
                rk = g_rank[:, 0:NT * E]
                dve.tensor_reduce(rk, g_a[:, 0:pairs].rearrange("p (m j) -> p m j", j=E), AX, ALU.add).then_inc(sig["dve_ran"], 1)
                dve.wait_ge(sig["dve_ran"], seen.up("dve_ran"))

            def share(E, weights):
                rk = g_rank[:, 0:NT * E].rearrange("p (t e) -> p t e", t=NT)
                we = weights[:, 0:NT * E].rearrange("p (t e) -> p t e", t=NT)
                tt(rk, rk, we, ALU.mult).then_inc(sig["dve_ran"], 1)
                dve.wait_ge(sig["dve_ran"], seen.up("dve_ran"))
                dve.tensor_reduce(g_m, rk, AX, ALU.add).then_inc(sig["dve_ran"], 1)
                dve.wait_ge(sig["dve_ran"], seen.up("dve_ran"))
                dve.reciprocal(g_m, g_m).then_inc(sig["dve_ran"], 1)
                dve.wait_ge(sig["dve_ran"], seen.up("dve_ran"))
                tt(f_w[:, :, 0:E], rk, g_m.unsqueeze(2).broadcast_to([P, NT, E]), ALU.mult).then_inc(sig["expert_weights"], 1)
                dve.wait_ge(sig["expert_weights"], seen.up("expert_weights"))

            def softmax_gates():
                gl = g_l[:, 0:32].rearrange("p (t e) -> p t e", t=NT)
                ge = g_e[:, 0:32].rearrange("p (t e) -> p t e", t=NT)
                dve.tensor_reduce(g_m, gl, AX, ALU.max).then_inc(sig["dve_ran"], 1)
                dve.wait_ge(sig["dve_ran"], seen.up("dve_ran"))
                tt(ge, gl, g_m.unsqueeze(2).broadcast_to([P, NT, 4]), ALU.subtract).then_inc(sig["gate_shift"], 1)
                dve.wait_ge(sig["gate_shift"], seen.up("gate_shift"))

            def ff(layer):
                gated, _, weighed = LAYERS_FF[layer]
                u0, nu = FF_UNITS[layer]

                def hidden(hh):
                    for c in range(2):
                        dve.wait_ge(sig["act_half"], seen.up("act_half"))
                        tt(f_h[hh][:, c, :], PS[:, 2 * c + 1, :], f_s[c], ALU.mult).then_inc(sig["h_ready"], 1)
                        dve.wait_ge(sig["h_ready"], seen.up("h_ready"))

                def add(e, hh):
                    dve.wait_ge(sig["down_ready"], seen.up("down_ready"))
                    for t in range(4):
                        y = PS[:, 4 + hh, 128 * t:128 * t + 128]
                        a = ACC[:, 4 * hh + t, :]
                        if weighed:
                            ins = dve.scalar_tensor_tensor(out=a, in0=y, scalar=f_w[:, 4 * hh + t, bass.ds(e, 1)],
                                                           in1=a, op0=ALU.mult, op1=ALU.add)
                        else:
                            ins = tt(a, y, a, ALU.add)
                        name = "down_used" if t == 3 else "dve_ran"
                        ins.then_inc(sig[name], 1)
                        seen.up(name)
                        if t == 3:
                            dve.wait_ge(sig[name], seen.up(name, 0))

                def unit(e):
                    for hh in range(2):
                        hidden(1 - hh)
                        add(e, hh)
                if gated:
                    hidden(0)
                    unit(8)
                    seen.loop(3, {"act_half": 8, "h_ready": 8, "down_ready": 4, "down_used": 4, "dve_ran": 12},
                           lambda i: (unit(i * 2), unit(i * 2 + 1)))
                    unit(6)
                    hidden(1)
                    add(7, 0)
                    add(7, 1)
                else:
                    per = {"down_ready": 4, "down_used": 4, "dve_ran": 12}
                    if layer == "l2f":
                        seen.loop(nu // 2, per, lambda i: [add(i, hh) for q in range(2) for hh in range(2)])
                    elif layer == "l1f":
                        seen.loop(nu // 2, per, lambda i: [add(i * 2 + q, hh) for q in range(2) for hh in range(2)])
                    else:
                        for q in range(2):
                            for hh in range(2):
                                add(None, hh)

            dve.memset(SM[:, 500:501], 1.0).then_inc(sig["dve_ran"], 1)
            dve.wait_ge(sig["dve_ran"], seen.up("dve_ran"))

            dve.wait_ge(sig["x_landed"], 16)
            dve.wait_ge(sig["w_first"], 16)
            layernorm(X, XN, LN_EPS)

            def l0_norm(s, q):
                dve.wait_ge(sig["l0s_exp"], seen.up("l0s_exp"))
                dve.reciprocal(l0_sum[q], l0_sum[q]).then_inc(sig["dve_ran"], 1)
                dve.wait_ge(sig["dve_ran"], seen.up("dve_ran"))
                dve.tensor_scalar(l0_p[q], l0_p[q], l0_sum[q], None, ALU.mult).then_inc(sig["l0s_probs"], 1)
                dve.wait_ge(sig["l0s_probs"], seen.up("l0s_probs"))

            def l0_front(s, q, first):
                dve.wait_ge(sig["l0s_scores"], seen.up("l0s_scores"))
                dve.tensor_reduce(l0_neg[q], PS[:, 0, 0:KEYS], AX, ALU.max, negate=True).then_inc(sig["l0s_max"], 1)
                dve.wait_ge(sig["l0s_max"], seen.up("l0s_max"))
                l0_norm(s, q)

            def l0_back(s, q, first):
                dve.wait_ge(sig["l0s_pt"], seen.up("l0s_pt"))
                dve.tensor_copy(l0_pt[q][:, 0:2, :], PS[:, 1, 0:256].rearrange("p (c n) -> p c n", c=2)).then_inc(sig["dve_ran"], 1)
                dve.wait_ge(sig["dve_ran"], seen.up("dve_ran"))
                dve.tensor_copy(l0_pt[q][0:1, 2, :], PS[0:1, 1, 256:384]).then_inc(sig["l0s_pt_taken"], 1)
                dve.wait_ge(sig["l0s_pt_taken"], seen.up("l0s_pt_taken"))
                dve.wait_ge(sig["l0s_u"], seen.up("l0s_u"))
                dve.tensor_scalar(l0_ut[:, bass.ds(s * P, P)], PS[:, 2, 0:P], 1.0, None, ALU.mult).then_inc(sig["l0s_u_taken"], 1)
                dve.wait_ge(sig["l0s_u_taken"], seen.up("l0s_u_taken"))
            seen.skewed(L0X_STEPS, {"dve_ran": 4} | {k: 2 for k in "l0s_exp l0s_probs l0s_scores l0s_max l0s_pt "
                                                  "l0s_pt_taken l0s_u l0s_u_taken".split()},
                     None, l0_front, l0_back)
            dve.wait_ge(sig["bias_ready"], seen.up("bias_ready"))
            residual()

            layernorm(X, XN, LN_EPS)
            dve.wait_ge(sig["w_l0"], 16)
            dve.wait_ge(sig["rows_landed"], 16)
            lq = ar(0, 2048).rearrange("p (t n) -> p t n", t=NT)
            le = ar(2048, 2048).rearrange("p (t n) -> p t n", t=NT)
            lv = ar(4096, 1024)
            lg = ar(5120, 1024)
            dve.wait_ge(sig["l0a_mm"], seen.up("l0a_mm", NT))
            dve.wait_ge(sig["l0a_act"], seen.up("l0a_act"))
            dve.tensor_scalar(lq, PS[:, :, 0:256], 0.0, None, ALU.max).then_inc(sig["dve_ran"], 1)
            dve.wait_ge(sig["dve_ran"], seen.up("dve_ran"))
            for hh in range(2):
                s = slice(1024 * hh, 1024 * hh + 1024)
                dve.scalar_tensor_tensor(out=ar(0, 2048)[:, s], in0=ar(2048, 2048)[:, s], scalar=1.0,
                                                in1=ar(0, 2048)[:, s], op0=ALU.min, op1=ALU.add).then_inc(sig["l0a_qk"], 1)
                dve.wait_ge(sig["l0a_qk"], seen.up("l0a_qk"))
            qk = ar(2048, 1024)
            qs = ar(3072, 1024)
            v3 = lambda a: a.rearrange("p (t n) -> p t n", t=NT)
            tt(v3(qk), lq[:, :, 0:128], lq[:, :, 128:256], ALU.mult).then_inc(sig["dve_ran"], 1)
            dve.wait_ge(sig["dve_ran"], seen.up("dve_ran"))
            r1, r2 = SM[:, 600:728], SM[:, 728:856]
            dve.tensor_reduce(r1, qk.rearrange("p (m d) -> p m d", d=DK), AX, ALU.add).then_inc(sig["dve_ran"], 1)
            dve.wait_ge(sig["dve_ran"], seen.up("dve_ran"))
            dve.wait_ge(sig["l0a_ksum"], seen.up("l0a_ksum"))
            tt(v3(qs), PSF[:, 0:1024].rearrange("p (t n) -> p t n", t=NT), lq[:, :, 0:128], ALU.mult).then_inc(sig["dve_ran"], 1)
            dve.wait_ge(sig["dve_ran"], seen.up("dve_ran"))
            dve.tensor_reduce(r2, qs.rearrange("p (m d) -> p m d", d=DK), AX, ALU.add).then_inc(sig["dve_ran"], 1)
            dve.wait_ge(sig["dve_ran"], seen.up("dve_ran"))
            dve.tensor_scalar(r2, r2, 1e-6, None, ALU.add).then_inc(sig["dve_ran"], 1)
            dve.wait_ge(sig["dve_ran"], seen.up("dve_ran"))
            dve.reciprocal(r2, r2).then_inc(sig["dve_ran"], 1)
            dve.wait_ge(sig["dve_ran"], seen.up("dve_ran"))
            tt(r1, r1, r2, ALU.mult).then_inc(sig["dve_ran"], 1)
            dve.wait_ge(sig["dve_ran"], seen.up("dve_ran"))
            tt(lv.rearrange("p (m d) -> p m d", d=DK), lv.rearrange("p (m d) -> p m d", d=DK),
                   r1.unsqueeze(2).broadcast_to([P, 128, DK]), ALU.mult).then_inc(sig["dve_ran"], 1)
            dve.wait_ge(sig["dve_ran"], seen.up("dve_ran"))
            layernorm(v3(lv), Z, 1e-5, signal=False)
            affine(Z[:, :, :], "l0a_gamma", "l0a_beta").then_inc(sig["dve_ran"], 1)
            dve.wait_ge(sig["dve_ran"], seen.up("dve_ran"))
            tt(flat(Z), flat(Z), lg, ALU.mult).then_inc(sig["stream_ready"], 1)
            dve.wait_ge(sig["stream_ready"], seen.up("stream_ready"))
            residual()

            layernorm(X, XN, LN_EPS)
            seen.up("gate_mm")
            dve.wait_ge(sig["gate_act"], seen.up("gate_act"))
            dve.tensor_copy(g_l, g_e).then_inc(sig["dve_ran"], 1)
            dve.wait_ge(sig["dve_ran"], seen.up("dve_ran"))
            rank_gates(8, w("rank_low8"))
            dve.tensor_scalar(g_rank, g_rank, 2.0, None, ALU.is_lt).then_inc(sig["dve_ran"], 1)
            dve.wait_ge(sig["dve_ran"], seen.up("dve_ran"))
            share(8, g_e)
            dve.tensor_scalar(f_w[:, :, 0:8], f_w[:, :, 0:8], 1.0 / 3.0, None, ALU.mult).then_inc(sig["dve_ran"], 1)
            dve.wait_ge(sig["dve_ran"], seen.up("dve_ran"))
            dve.memset(f_w[:, :, 8:9], 1.0 / 3.0).then_inc(sig["dve_ran"], 1)
            dve.wait_ge(sig["dve_ran"], seen.up("dve_ran"))
            dve.memset(flat(ACC), 0.0).then_inc(sig["dve_ran"], 1)
            dve.wait_ge(sig["dve_ran"], seen.up("dve_ran"))
            ff("l0f")
            tt(flat(X), flat(X), flat(ACC), ALU.add).then_inc(sig["resid_done"], 1)
            dve.wait_ge(sig["resid_done"], seen.up("resid_done"))

            layernorm(X, XN, LN_EPS)
            dve.wait_ge(sig["mask_landed"], seen.up("mask_landed", 32))
            dve.tensor_scalar(y_hi[:, 0:2, :], MK[:, 0:2, :], 10.0, -5.0, ALU.mult, ALU.add).then_inc(sig["dve_ran"], 1)
            dve.wait_ge(sig["dve_ran"], seen.up("dve_ran"))
            dve.tensor_scalar(y_hi[0:1, 2, :], MK[0:1, 2, :], 10.0, -5.0, ALU.mult, ALU.add).then_inc(sig["dve_ran"], 1)
            dve.wait_ge(sig["dve_ran"], seen.up("dve_ran"))

            def y_clip(b, first):
                dve.wait_ge(sig["ys_ready"], seen.up("ys_ready"))
                if not first:
                    dve.wait_ge(sig["yexp"], seen.up("yexp"))
                for c in range(3):
                    r = slice(0, P) if c < 2 else slice(0, 1)
                    ins = dve.tensor_scalar(y_C[r, c, :], PS[r, 1 + c, :], -5.0, y_hi[r, c, bass.ds(b, 1)],
                                            ALU.max, ALU.min)
                    name = "yclip" if c == 2 else "dve_ran"
                    ins.then_inc(sig[name], 1)
                    dve.wait_ge(sig[name], seen.up(name))

            def y_norm(first):
                dve.wait_ge(sig["yu_ready"], seen.up("yu_ready"))
                if not first:
                    dve.wait_ge(sig["yt_ready"], seen.up("yt_ready"))
                u = PS[:, 4:6, 0:2 * FQ].rearrange("p a (g f) -> p a g f", g=2)
                dve.reciprocal(y_r.rearrange("p (a g) -> p a g", a=2), u[:, :, :, P]).then_inc(sig["dve_ran"], 1)
                dve.wait_ge(sig["dve_ran"], seen.up("dve_ran"))
                for a in range(2):
                    ins = tt(y_U[:, 2 * a:2 * a + 2, :], u[:, a, :, 0:P],
                             y_r[:, 2 * a:2 * a + 2].unsqueeze(2).broadcast_to([P, 2, P]), ALU.mult)
                    name = "yu_taken" if a else "dve_ran"
                    ins.then_inc(sig[name], 1)
                    dve.wait_ge(sig[name], seen.up(name))

            def y_out(c):
                dve.wait_ge(sig["yo_ready"], seen.up("yo_ready"))
                dve.tensor_copy(OT[:, bass.ds(c * P, P)], PS[:, 7, 0:P]).then_inc(sig["yo_taken"], 1)
                dve.wait_ge(sig["yo_taken"], seen.up("yo_taken"))

            def y_chunk(c, first=False):
                for k in range(4):
                    y_clip(c * 4 + k, first and k == 0)
                    if not first or k >= 1:
                        y_norm(first and k == 1)
                    if k == 1 and not first:
                        y_out(c - 1)
            y_chunk(0, first=True)
            seen.loop(B // 4 - 1, {"dve_ran": 16, "yo_ready": 1, "yo_taken": 1} | {k: 4 for k in (
                "ys_ready", "yexp", "yclip", "yu_ready", "yt_ready", "yu_taken")}, lambda i: y_chunk(i + 1))
            y_norm(False)
            y_out(B // 4 - 1)
            seen.up("yexp")
            seen.up("yt_ready")
            dve.wait_ge(sig["bias_ready"], seen.up("bias_ready"))
            residual()

            def core(kind):
                for half in range(2):
                    v = lambda a: a.rearrange("p (g n k) -> p g n k", g=HG, n=16)
                    dve.wait_ge(sig["c_scores"], seen.up("c_scores"))
                    if half:
                        dve.wait_ge(sig["c_pt"], seen.up("c_pt", 0))
                    ps = PSF[:, 0:2048]
                    if kind == "causal":
                        cz = w("causal").unsqueeze(1).broadcast_to([P, 64, 32])
                        tt(c_p.rearrange("p (m k) -> p m k", k=32), ps.rearrange("p (m k) -> p m k", k=32),
                               cz, ALU.add).then_inc(sig["dve_ran"], 1)
                        dve.wait_ge(sig["dve_ran"], seen.up("dve_ran"))
                        src = c_p
                    else:
                        src = ps
                    s3 = src.rearrange("p (m k) -> p m k", k=32)
                    p3 = c_p.rearrange("p (m k) -> p m k", k=32)
                    dve.tensor_reduce(c_red, s3, AX, ALU.max).then_inc(sig["dve_ran"], 1)
                    dve.wait_ge(sig["dve_ran"], seen.up("dve_ran"))
                    tt(p3, s3, c_red.unsqueeze(2).broadcast_to([P, 64, 32]), ALU.subtract).then_inc(sig["c_shift"], 1)
                    dve.wait_ge(sig["c_shift"], seen.up("c_shift"))
                    dve.wait_ge(sig["c_exp"], seen.up("c_exp"))
                    dve.tensor_reduce(c_red, p3, AX, ALU.add).then_inc(sig["dve_ran"], 1)
                    dve.wait_ge(sig["dve_ran"], seen.up("dve_ran"))
                    dve.reciprocal(c_red, c_red).then_inc(sig["dve_ran"], 1)
                    dve.wait_ge(sig["dve_ran"], seen.up("dve_ran"))
                    out2 = c_p2.rearrange("p (n g k) -> p g n k", n=16, g=HG)
                    for g in range(HG):
                        rg = c_red[:, 16 * g:16 * g + 16].unsqueeze(2).broadcast_to([P, 16, 32])
                        ins = tt(out2[:, g], p3[:, 16 * g:16 * g + 16, :], rg, ALU.mult)
                        if kind != "pairs" and g == HG - 1:
                            ins.then_inc(sig["c_probs"], 1)
                            dve.wait_ge(sig["c_probs"], seen.up("c_probs"))
                        else:
                            ins.then_inc(sig["dve_ran"], 1)
                            dve.wait_ge(sig["dve_ran"], seen.up("dve_ran"))
                    if kind == "pairs":
                        for g in range(HG):
                            o = c_p2.rearrange("p (a m g k) -> p g a m k", a=4, m=4, g=HG)[:, g]
                            bias = c_relb.unsqueeze(1).broadcast_to([P, 4, 4, 32])
                            ins = tt(o, o, bias, ALU.add)
                            name = "c_probs" if g == HG - 1 else "dve_ran"
                            ins.then_inc(sig[name], 1)
                            dve.wait_ge(sig[name], seen.up(name))
                    dve.wait_ge(sig["c_pt"], seen.up("c_pt"))
                    dve.wait_ge(sig["c_pv"], seen.up("c_pv"))
                    dst = c_big[:, 2048 * half:2048 * half + 2048] if kind == "pairs" else c_big[:, 0:2048]
                    m4 = w("mask4").unsqueeze(1).unsqueeze(3).broadcast_to([P, 16, 4, 32])
                    ins = tt(dst.rearrange("p (n h q) -> p n h q", n=16, h=4),
                             ps.rearrange("p (n h q) -> p n h q", n=16, h=4), m4, ALU.mult)
                    if kind == "pairs":
                        ins.then_inc(sig["c_masked"], 1)
                        dve.wait_ge(sig["c_masked"], seen.up("c_masked"))
                    else:
                        ins.then_inc(sig["dve_ran"], 1)
                        dve.wait_ge(sig["dve_ran"], seen.up("dve_ran"))
                        o = OT[:, 512 * half:512 * half + 512].rearrange("p (n q) -> p n q", n=16)
                        dve.tensor_reduce(o, c_big[:, 0:2048].rearrange("p (n h q) -> p n q h", n=16, h=4),
                                                 AX, ALU.add).then_inc(sig["c_masked"], 1)
                        dve.wait_ge(sig["c_masked"], seen.up("c_masked"))

            def heads():
                dve.wait_ge(sig["qkv_taken"], seen.up("qkv_taken"))
                m4 = w("mask4").unsqueeze(1).unsqueeze(3).broadcast_to([P, 32, 4, 32])
                q4 = c_q.rearrange("p (n q) -> p n q", n=32).unsqueeze(2).broadcast_to([P, 32, 4, 32])
                tt(c_qb.rearrange("p (n h q) -> p n h q", n=32, h=4), q4, m4, ALU.mult).then_inc(sig["dve_ran"], 1)
                dve.wait_ge(sig["dve_ran"], seen.up("dve_ran"))
                dve.transpose(c_vt, c_v).then_inc(sig["c_in"], 1)
                dve.wait_ge(sig["c_in"], seen.up("c_in"))

            layernorm(X, XN, LN_EPS)
            dve.wait_ge(sig["w_l1"], 16)
            heads()
            core("causal")
            residual()

            layernorm(X, XN, LN_EPS)
            dve.wait_ge(sig["gate_mm"], seen.up("gate_mm", 2))
            ps = PS[:, 7, 0:NT]
            small = row("small")
            z = lambda j: g_z[:, j, :]
            dve.tensor_scalar(z(0), ps, small[:, SMALL_DPB2:SMALL_DPB2 + 1], None, ALU.add).then_inc(sig["dve_ran"], 1)
            dve.wait_ge(sig["dve_ran"], seen.up("dve_ran"))
            dve.tensor_scalar(z(1), z(0), -1.0, None, ALU.mult).then_inc(sig["dve_ran"], 1)
            dve.wait_ge(sig["dve_ran"], seen.up("dve_ran"))
            tt(z(1), z(0), z(1), ALU.max).then_inc(sig["gate_entropy"], 1)
            dve.wait_ge(sig["gate_entropy"], seen.up("gate_entropy"))
            dve.tensor_scalar(z(0), z(0), 0.0, None, ALU.max).then_inc(sig["dve_ran"], 1)
            dve.wait_ge(sig["dve_ran"], seen.up("dve_ran"))
            dve.wait_ge(sig["gate_act"], seen.up("gate_act", 2))
            tt(z(0), z(0), z(3), ALU.add).then_inc(sig["dve_ran"], 1)
            dve.wait_ge(sig["dve_ran"], seen.up("dve_ran"))
            dve.tensor_scalar(z(0), z(0), 0.5, 1.0 / 1.5, ALU.subtract, ALU.mult).then_inc(sig["dve_ran"], 1)
            dve.wait_ge(sig["dve_ran"], seen.up("dve_ran"))
            dve.tensor_scalar(z(0), z(0), 0.0, 1.0, ALU.max, ALU.min).then_inc(sig["dve_ran"], 1)
            dve.wait_ge(sig["dve_ran"], seen.up("dve_ran"))
            dve.tensor_scalar(z(0), z(0), 3.0, 1.0, ALU.mult, ALU.add).then_inc(sig["dve_ran"], 1)
            dve.wait_ge(sig["dve_ran"], seen.up("dve_ran"))
            dve.tensor_scalar(z(1), z(0), 1.5, 1.0, ALU.is_ge, ALU.add).then_inc(sig["dve_ran"], 1)
            dve.wait_ge(sig["dve_ran"], seen.up("dve_ran"))
            dve.tensor_scalar(z(4), z(0), 2.5, None, ALU.is_gt).then_inc(sig["dve_ran"], 1)
            dve.wait_ge(sig["dve_ran"], seen.up("dve_ran"))
            tt(z(1), z(1), z(4), ALU.add).then_inc(sig["dve_ran"], 1)
            dve.wait_ge(sig["dve_ran"], seen.up("dve_ran"))
            dve.tensor_scalar(z(4), z(0), 3.5, None, ALU.is_ge).then_inc(sig["dve_ran"], 1)
            dve.wait_ge(sig["dve_ran"], seen.up("dve_ran"))
            tt(z(1), z(1), z(4), ALU.add).then_inc(sig["dve_ran"], 1)
            dve.wait_ge(sig["dve_ran"], seen.up("dve_ran"))
            gb = small[:, SMALL_L1GATE:SMALL_L1GATE + 4].unsqueeze(1).broadcast_to([P, NT, 4])
            tt(g_l[:, 0:32].rearrange("p (t e) -> p t e", t=NT),
                   PS[:, 6, 0:32].rearrange("p (t e) -> p t e", t=NT), gb, ALU.add).then_inc(sig["dve_ran"], 1)
            dve.wait_ge(sig["dve_ran"], seen.up("dve_ran"))
            softmax_gates()
            rank_gates(4, w("rank_low4"))
            rk = g_rank[:, 0:32].rearrange("p (t e) -> p t e", t=NT)
            tt(rk, rk, z(1).unsqueeze(2).broadcast_to([P, NT, 4]), ALU.is_lt).then_inc(sig["dve_ran"], 1)
            dve.wait_ge(sig["dve_ran"], seen.up("dve_ran"))
            dve.wait_ge(sig["gate_act"], seen.up("gate_act"))
            share(4, g_e)
            dve.memset(flat(ACC), 0.0).then_inc(sig["dve_ran"], 1)
            dve.wait_ge(sig["dve_ran"], seen.up("dve_ran"))
            ff("l1f")
            tt(flat(X), flat(X), flat(ACC), ALU.add).then_inc(sig["dve_ran"], 1)
            dve.wait_ge(sig["dve_ran"], seen.up("dve_ran"))
            dve.wait_ge(sig["bias_ready"], seen.up("bias_ready"))
            tt(flat(X), flat(X), flat(ACCB), ALU.add).then_inc(sig["resid_done"], 1)
            dve.wait_ge(sig["resid_done"], seen.up("resid_done"))

            def take_queries(bq):
                dve.wait_ge(sig["xq_mm"], seen.up("xq_mm"))
                scale = float(DK) ** -0.5
                if bq:
                    ins = dve.tensor_scalar(x_q, PSF[:, 1024:2048], col(bq), scale, ALU.add, ALU.mult)
                else:
                    ins = dve.tensor_scalar(x_q, PSF[:, 1024:2048], scale, None, ALU.mult)
                ins.then_inc(sig["xq_ready"], 1)
                dve.wait_ge(sig["xq_ready"], seen.up("xq_ready"))

            def cross(biased, bv):
                def x_vl_take(k):
                    dve.wait_ge(sig["xv_taken"], seen.up("xv_taken"))
                    tt(x_vl[k][0:4, :], PS[0:4, 1, 256:384], w("mask_last")[0:4, :], ALU.mult)\
                        .then_inc(sig["xvl_taken"], 1)
                    dve.wait_ge(sig["xvl_taken"], seen.up("xvl_taken"))

                def x_add(k, first):
                    dve.wait_ge(sig[f"ctx_landed{k}"], seen.up(f"ctx_landed{k}", 32))
                    if not first:
                        dve.wait_ge(sig["xexp"], seen.up("xexp"))
                    tt(x_s, PS[:, 2:6, 0:KEYS], c_F[k], ALU.add).then_inc(sig["xs_added"], 1)
                    dve.wait_ge(sig["xs_added"], seen.up("xs_added"))

                def x_max(q):
                    src = x_s if biased else PS[:, 2:6, 0:KEYS]
                    dve.tensor_reduce(x_neg[q], src, AX, ALU.max, negate=True).then_inc(sig["xmax"], 1)
                    dve.wait_ge(sig["xmax"], seen.up("xmax"))

                def x_turned():
                    dve.wait_ge(sig["xpt_ready"], seen.up("xpt_ready"))
                    dve.tensor_copy(x_pt[:, 1, :], PS[:, 7, :]).then_inc(sig["xpt_d"], 1)
                    dve.wait_ge(sig["xpt_d"], seen.up("xpt_d"))

                def x_tail(b):
                    dve.wait_ge(sig["xu_ready"], seen.up("xu_ready"))
                    x4 = x_t.rearrange("p (h q) -> p h q", h=4)
                    m4 = w("mask4").unsqueeze(2).broadcast_to([P, 4, 32])
                    tt(x4, PS[:, 6, 0:128].rearrange("p (h q) -> p h q", h=4), m4, ALU.mult).then_inc(sig["dve_ran"], 1)
                    dve.wait_ge(sig["dve_ran"], seen.up("dve_ran"))
                    dve.reciprocal(x_rec, PS[:, 7, 0:32]).then_inc(sig["dve_ran"], 1)
                    dve.wait_ge(sig["dve_ran"], seen.up("dve_ran"))
                    tt(x4[:, 0:2, :], x4[:, 0:2, :], x4[:, 2:4, :], ALU.add).then_inc(sig["dve_ran"], 1)
                    dve.wait_ge(sig["dve_ran"], seen.up("dve_ran"))
                    tt(x4[:, 0, :], x4[:, 0, :], x4[:, 1, :], ALU.add).then_inc(sig["dve_ran"], 1)
                    dve.wait_ge(sig["dve_ran"], seen.up("dve_ran"))
                    tt(OT[:, bass.ds(b * 32, 32)], x4[:, 0, :], x_rec, ALU.mult).then_inc(sig["x_out"], 1)
                    dve.wait_ge(sig["x_out"], seen.up("x_out"))

                def x_four(c, first=False, last=False):
                    for k in range(4):
                        dve.wait_ge(sig["xs_ready"], seen.up("xs_ready"))
                        if biased:
                            x_add(k, first and k == 0)
                        else:
                            x_max(k % 2)
                        if not (first and k == 0):
                            x_turned()
                        if biased:
                            x_max(k % 2)
                        if not (last and k == 3):
                            x_vl_take((k + 1) % 4)
                        if not (first and k == 0):
                            x_tail(c * 4 + (k - 1))

                x_vl_take(0)
                x_four(0, first=True)
                per = {"dve_ran": 16} | {k: 4 for k in "xs_ready xmax xpt_ready xpt_d xv_taken xvl_taken xu_ready "
                                                       "x_out".split()}
                if biased:
                    per |= {"xexp": 4, "xs_added": 4} | {f"ctx_landed{k}": 32 for k in range(4)}
                seen.loop(B // 4 - 2, per, lambda i: x_four(i + 1))
                x_four(B // 4 - 1, last=True)
                x_turned()
                x_tail(B - 1)
                seen.up("xexp", 1 if biased else B)
                if bv:
                    dve.tensor_scalar(OT[:, :], OT[:, :], col(bv), None, ALU.add).then_inc(sig["x_out"], 1)
                    dve.wait_ge(sig["x_out"], seen.up("x_out"))

            layernorm(X, XN, LN_EPS)
            dve.wait_ge(sig["w_l2"], 16)
            take_queries(None)
            for k in range(4):
                seen.up(f"ctx_landed{k}", (64 * (L0X_STEPS // 2) if k < 2 else 0) + 48 * (B // 4))
            cross(True, None)
            dve.wait_ge(sig["proj_ready"], seen.up("proj_ready"))
            tt(flat(Y), PSF[:, 3072:4096], flat(XN), ALU.add).then_inc(sig["dve_ran"], 1)
            dve.wait_ge(sig["dve_ran"], seen.up("dve_ran"))
            layernorm(Y, Z, 1e-5, signal=False)
            affine(Z[:, :, :], "l2x_g1", "l2x_be1").then_inc(sig["stream_ready"], 1)
            dve.wait_ge(sig["stream_ready"], seen.up("stream_ready"))
            tt(ACC[:, :, :], Y[:, :, :], rows_t("l2x_b2"), ALU.add).then_inc(sig["dve_ran"], 1)
            dve.wait_ge(sig["dve_ran"], seen.up("dve_ran"))
            ff("l2x")
            layernorm(ACC, Z, 1e-5, signal=False)
            affine(Z[:, :, :], "l2x_g2", "l2x_be2").then_inc(sig["dve_ran"], 1)
            dve.wait_ge(sig["dve_ran"], seen.up("dve_ran"))
            tt(flat(X), flat(X), flat(Z), ALU.add).then_inc(sig["resid_done"], 1)
            dve.wait_ge(sig["resid_done"], seen.up("resid_done"))

            layernorm(X, XN, LN_EPS)
            dve.wait_ge(sig["relb_landed"], 64)
            for j in range(4):
                r = slice(32 * j, 32 * j + 32)
                dve.tensor_copy(c_rel2[r].rearrange("p k m -> p m k"),
                                    ACCB[r, 0:4, :].rearrange("p t n -> p (t n)")
                                    .rearrange("p (k m j) -> p j m k", k=32, m=4)[:, j]).then_inc(sig["dve_ran"], 1)
                dve.wait_ge(sig["dve_ran"], seen.up("dve_ran"))
            oh = w("onehot").rearrange("p (k u) -> p k u", k=32)
            for m4i in range(4):
                rb = c_rel2[:, :, m4i].unsqueeze(1).broadcast_to([P, 32, 32])
                tt(c_p[:, 0:1024].rearrange("p (k u) -> p k u", k=32), oh, rb, ALU.mult).then_inc(sig["dve_ran"], 1)
                dve.wait_ge(sig["dve_ran"], seen.up("dve_ran"))
                dve.tensor_reduce(c_relb[:, m4i, :], c_p[:, 0:1024].rearrange("p (k u) -> p k u", k=32),
                                      AX, ALU.add).then_inc(sig["dve_ran"], 1)
                dve.wait_ge(sig["dve_ran"], seen.up("dve_ran"))
            mp = w("mask_pair").rearrange("p (m r) -> p m r", r=2)
            for name, dst in (("l2a_bq", c_qb), ("l2a_bk", c_big), ("l2a_bv", c_big)):
                for cc in range(2):
                    dve.wait_ge(sig["pair_ready"], seen.up("pair_ready"))
                    for c in range(8):
                        o = dst.rearrange("p (m r c) -> p m r c", r=2, c=H)[:, :, :, 8 * cc + c]
                        i0 = PS[:, c // 2, 256 * (c % 2):256 * (c % 2) + 256].rearrange("p (m r) -> p m r", r=2)
                        ins = dve.scalar_tensor_tensor(out=o, in0=i0, scalar=col(name, 16)[:, 8 * cc + c:8 * cc + c + 1],
                                                       in1=mp, op0=ALU.add, op1=ALU.mult)
                        if c == 7 and (cc == 0 or name == "l2a_bq"):
                            ins.then_inc(sig["pair_taken"], 1)
                            dve.wait_ge(sig["pair_taken"], seen.up("pair_taken"))
                        else:
                            ins.then_inc(sig["dve_ran"], 1)
                            dve.wait_ge(sig["dve_ran"], seen.up("dve_ran"))
                    if cc == 1 and name != "l2a_bq":
                        o = c_k if name == "l2a_bk" else c_v
                        dve.tensor_reduce(o.rearrange("p (m i) -> p m i", m=32),
                                                 c_big.rearrange("p (m j i) -> p m i j", m=32, j=4), AX, ALU.add).then_inc(sig["pair_taken"], 1)
                        dve.wait_ge(sig["pair_taken"], seen.up("pair_taken"))
            dve.transpose(c_vt, c_v).then_inc(sig["c_in"], 1)
            dve.wait_ge(sig["c_in"], seen.up("c_in"))
            core("pairs")
            dve.wait_ge(sig["proj_ready"], seen.up("proj_ready"))
            tt(flat(Y), PSF[:, 1024:2048], flat(XN), ALU.add).then_inc(sig["dve_ran"], 1)
            dve.wait_ge(sig["dve_ran"], seen.up("dve_ran"))
            tt(Y[:, :, :], Y[:, :, :], rows_t("l2a_bo"), ALU.add).then_inc(sig["dve_ran"], 1)
            dve.wait_ge(sig["dve_ran"], seen.up("dve_ran"))
            layernorm(Y, Z, 0.0)
            dve.wait_ge(sig["proj_ready"], seen.up("proj_ready"))
            tt(flat(Z), PSF[:, 3072:4096], flat(Z), ALU.add).then_inc(sig["dve_ran"], 1)
            dve.wait_ge(sig["dve_ran"], seen.up("dve_ran"))
            tt(Z[:, :, :], Z[:, :, :], rows_t("l2a_b2"), ALU.add).then_inc(sig["dve_ran"], 1)
            dve.wait_ge(sig["dve_ran"], seen.up("dve_ran"))
            layernorm(Z, Y, 0.0, signal=False)
            tt(flat(X), flat(X), flat(Y), ALU.add).then_inc(sig["resid_done"], 1)
            dve.wait_ge(sig["resid_done"], seen.up("resid_done"))

            layernorm(X, XN, LN_EPS)
            dve.tensor_copy(flat(Y), flat(XN)).then_inc(sig["dve_ran"], 1)
            dve.wait_ge(sig["dve_ran"], seen.up("dve_ran"))
            for r in range(4):
                dve.wait_ge(sig["gate_mm"], seen.up("gate_mm"))
                gb = small[:, SMALL_L2GATE + 4 * r:SMALL_L2GATE + 4 * r + 4].unsqueeze(1).broadcast_to([P, NT, 4])
                tt(g_l[:, 0:32].rearrange("p (t e) -> p t e", t=NT),
                       PS[:, 6, 0:32].rearrange("p (t e) -> p t e", t=NT), gb, ALU.add).then_inc(sig["dve_ran"], 1)
                dve.wait_ge(sig["dve_ran"], seen.up("dve_ran"))
                softmax_gates()
                rank_gates(4, w("rank_low4"))
                dve.tensor_scalar(g_rank[:, 0:32], g_rank[:, 0:32], 2.0, None, ALU.is_lt).then_inc(sig["dve_ran"], 1)
                dve.wait_ge(sig["dve_ran"], seen.up("dve_ran"))
                dve.wait_ge(sig["gate_act"], seen.up("gate_act"))
                share(4, g_e)
                dve.tensor_copy(flat(ACC), flat(Y)).then_inc(sig["dve_ran"], 1)
                dve.wait_ge(sig["dve_ran"], seen.up("dve_ran"))
                ff("l2f")
                dve.wait_ge(sig["bias_ready"], seen.up("bias_ready"))
                ins = tt(flat(Y), flat(ACC), flat(ACCB), ALU.add)
                name = "stream_ready" if r < 3 else "dve_ran"
                ins.then_inc(sig[name], 1)
                dve.wait_ge(sig[name], seen.up(name))
            tt(flat(X), flat(X), flat(Y), ALU.add).then_inc(sig["resid_done"], 1)
            dve.wait_ge(sig["resid_done"], seen.up("resid_done"))

            layernorm(X, XN, LN_EPS)
            dve.wait_ge(sig["w_l3"], 16)
            take_queries("l3x_bq")
            cross(False, "l3x_bv")
            dve.wait_ge(sig["bias_ready"], seen.up("bias_ready"))
            residual()

            layernorm(X, XN, LN_EPS)
            layernorm(XN, Z, 1e-5, signal=False)
            affine(Z[:, :, :], "l3a_lng", "l3a_lnb").then_inc(sig["dve_ran"], 1)
            dve.wait_ge(sig["dve_ran"], seen.up("dve_ran"))
            heads()
            core("plain")
            dve.wait_ge(sig["bias_ready"], seen.up("bias_ready"))
            tt(flat(X), flat(X), flat(Z), ALU.add).then_inc(sig["dve_ran"], 1)
            dve.wait_ge(sig["dve_ran"], seen.up("dve_ran"))
            residual()

            layernorm(X, XN, LN_EPS)
            dve.memset(flat(ACC), 0.0).then_inc(sig["dve_ran"], 1)
            dve.wait_ge(sig["dve_ran"], seen.up("dve_ran"))
            ff("l3f")
            dve.wait_ge(sig["bias_ready"], seen.up("bias_ready"))
            residual()

        @block.gpsimd
        def _(pool):
            seen = Tally(pool)
            for q in range(2):
                pool.memset(y_P[q][:, 2, :], 0.0).then_inc(sig["pool_ran"], 1)
            pool.memset(ar(17408, 4 * FQ), 0.0).then_inc(sig["pool_ran"], 1)
            pool.wait_ge(sig["pool_ran"], seen.up("pool_ran", 3))
            pool.sem_inc(sig["y_padded"], 1)
            for g in ("l0", "l1", "l2", "l3"):
                a, cols = SPANS["group_" + g]
                if g == "l1":
                    pool.dma_start(RB[:, :, :], wrows.rearrange("a r n -> (a) r n").broadcast_to([P, len(ROWS), P])
                                   ).then_inc(sig["rows_landed"], 16)
                    pool.dma_start(MK[:, 0:2, :], mask[0:2 * P, :].rearrange("(c p) b -> p c b", c=2))\
                        .then_inc(sig["mask_landed"], 16)
                    pool.dma_start(MK[0:1, 2, :], mask[2 * P:KEYS, :]).then_inc(sig["mask_landed"], 16)
                pool.dma_start(W[:, a:a + cols], wpack[:, a:a + cols]).then_inc(sig["w_" + g], 16)
            pool.wait_ge(sig["w_l0"], 16)
            pool.wait_ge(sig["rows_landed"], 16)
            ready = sig["rows_landed"]

            def bias(name):
                pool.tensor_tensor(X[:, :, :], X[:, :, :], rows_t(name), ALU.add).then_inc(sig["bias_ready"], 1)
                pool.wait_ge(sig["bias_ready"], seen.up("bias_ready"))

            pool.wait_ge(sig["norm_ready"], seen.up("norm_ready", NT))
            pool.wait_ge(sig["l0s_q_ready"], seen.up("l0s_q_ready"))

            def stage(s, q, first):
                if not (first and isinstance(s, int) and s < 2):
                    pool.wait_ge(sig["l0s_scores"], seen.up("l0s_scores"))
                pool.wait_ge(ready, 16)
                pool.tensor_copy(l0_qs[q], l0_qp[:, bass.ds(s * P, P)]).then_inc(sig["l0s_staged"], 1)
                pool.wait_ge(sig["l0s_staged"], seen.up("l0s_staged"))
            stage(0, 0, True)
            stage(1, 1, True)
            seen.loop(L0X_STEPS // 2 - 1, {"l0s_scores": 2, "l0s_staged": 2},
                   lambda i: (stage(i * 2 + 2, 0, False), stage(i * 2 + 3, 1, False)))
            bias("l0x_bo")
            pool.wait_ge(sig["norm_ready"], seen.up("norm_ready", 2 * NT))
            pool.dma_start(ar(8192, 4096), l1x_w).then_inc(sig["l1x_w_landed"], 16)
            seen.up("expert_weights")

            pool.wait_ge(sig["norm_ready"], seen.up("norm_ready", NT))
            bias("l1x_bo")
            seen.up("norm_ready", NT)

            def expert_bias(names):
                pool.wait_ge(sig["expert_weights"], seen.up("expert_weights"))
                for e, name in enumerate(names):
                    we = f_w[:, :, e:e + 1].broadcast_to([P, NT, P])
                    dst = ACCB if e == 0 else Z
                    pool.tensor_tensor(dst[:, :, :], rows_t(name), we, ALU.mult).then_inc(sig["pool_ran"], 1)
                    pool.wait_ge(sig["pool_ran"], seen.up("pool_ran"))
                    if e:
                        ins = pool.tensor_tensor(ACCB[:, :, :], ACCB[:, :, :], Z[:, :, :], ALU.add)
                        name = "bias_ready" if e == 3 else "pool_ran"
                        ins.then_inc(sig[name], 1)
                        pool.wait_ge(sig[name], seen.up(name))

            pool.wait_ge(sig["norm_ready"], seen.up("norm_ready", NT))
            expert_bias([f"l1f_b2_{e}" for e in range(4)])

            def spread():
                pool.wait_ge(sig["xq_ready"], seen.up("xq_ready"))
                m16 = w("mask16").unsqueeze(2).broadcast_to([P, H, 32])

                def x_queries(b, q, first):
                    if not first:
                        pool.wait_ge(sig["xs_ready"], seen.up("xs_ready"))
                    qv = x_q[:, bass.ds(b * 32, 32)].unsqueeze(1).broadcast_to([P, H, 32])
                    pool.tensor_tensor(x_qb[q].rearrange("p (h q) -> p h q", h=H), qv, m16, ALU.mult).then_inc(sig["xqb"], 1)
                    pool.wait_ge(sig["xqb"], seen.up("xqb"))

                def x_sums(q):
                    pool.wait_ge(sig["xexp"], seen.up("xexp"))
                    pool.tensor_tensor(x_r[q].rearrange("p (g f) -> p g f", g=HG),
                                       w("head_mask").rearrange("p (g f) -> p g f", g=HG),
                                       x_sum[q].unsqueeze(2).broadcast_to([P, HG, 32]), ALU.mult)\
                        .then_inc(sig["xsum_spread"], 1)
                    pool.wait_ge(sig["xsum_spread"], seen.up("xsum_spread"))
                x_queries(0, 0, True)
                x_queries(1, 1, True)
                x_sums(0)

                def body(i):
                    for k in range(2):
                        x_queries(i * 2 + (2 + k), k, False)
                        x_sums(1 - k)
                seen.loop(B // 2 - 1, {k: 2 for k in "xs_ready xqb xexp xsum_spread".split()}, body)
                x_sums(1)
                seen.up("xs_ready", 2)

            pool.wait_ge(sig["norm_ready"], seen.up("norm_ready", NT))
            pool.wait_ge(sig["resid_done"], seen.up("resid_done", 6))
            for j in range(4):
                pool.dma_start(ACCB[32 * j:32 * j + 32, 0:4, :].rearrange("p t n -> p (t n)"),
                               relb.broadcast_to([32, 512])).then_inc(sig["relb_landed"], 16)
            spread()
            seen.up("norm_ready", 2 * NT)

            pool.wait_ge(sig["norm_ready"], seen.up("norm_ready", NT))
            for r in range(4):
                expert_bias([f"l2f_b2_{e}" for e in range(4)])

            pool.wait_ge(sig["norm_ready"], seen.up("norm_ready", NT))
            bias("l3x_bo")
            spread()
            pool.wait_ge(sig["norm_ready"], seen.up("norm_ready", NT))
            bias("l3a_bp")
            pool.wait_ge(sig["norm_ready"], seen.up("norm_ready", NT))
            bias("l3f_b2")

    return nc



def kernel(**inputs):
    import numpy as np
    import concourse.bacc as bacc
    from concourse import mybir as mb
    from concourse.bass_utils import run_bass_kernel_spmd

    a = {k: np.asarray(v) for k, v in inputs.items()}
    f = np.float32
    wp = np.zeros((P, WTOTAL), f)

    def put(name, m):
        at, n = SPANS[name]
        m = np.asarray(m)
        wp[:m.shape[0], at:at + m.shape[1]] = m

    put("ident", np.eye(P, dtype=f))
    put("l0x_q", a["L0_xattn_Wq"].T)
    put("l0x_k", a["L0_xattn_Wk"])
    put("l0x_v", a["L0_xattn_Wv"].T)
    put("l0x_o", a["L0_xattn_Wo"].T)
    p = np.arange(P)
    put("blockones", (p[:, None] // 32 == p[None, :] // 32).astype(f))
    put("l0a_qkvg", np.concatenate([a["L0_attn_W" + c] for c in "qkvg"], 1))
    put("l0a_o", a["L0_attn_Wo"])
    put("l0f_gate", a["L0_ffn_Wg"])
    for E in (8, 4):
        e = np.arange(E)
        put(f"rank_low{E}", np.broadcast_to((e[None, :] < e[:, None]).astype(f).reshape(1, -1), (P, E * E)))
    put("mask4", ((p[:, None] % 32) // 8 == np.arange(4)[None, :]).astype(f))
    put("mask16", (p[:, None] // 8 == np.arange(16)[None, :]).astype(f))
    put("mask_last", (np.arange(4)[:, None] == p[None, :] // 32).astype(f))
    put("l1a_q", a["L1_attn_wq"].T)
    rep4 = np.array([8 * g + d for g in range(4) for m in range(4) for d in range(8)])
    put("l1a_k", a["L1_attn_wk"][rep4].T)
    put("l1a_v", a["L1_attn_wv"][rep4].T)
    put("l1a_o", a["L1_attn_wo"].T)
    put("causal", np.where(np.arange(32)[None, :] > (p[:, None] % 32), f(-1e30), f(0)))
    put("l1f_gate", a["L1_ffn_gate_w"])
    put("l1f_dp1", a["L1_ffn_dp_w1"])
    put("l1f_dp2", a["L1_ffn_dp_w2"])
    for c in "qkvo":
        put("l2x_" + c, a["L2_xattn_W" + c].T)
        put("l3x_" + c, a["L3_xattn_W" + c].T)
    jd = p % 32 % 8
    for c in "qkv":
        wt = a["L2_attn_W" + c].T
        put("l2a_" + c, np.concatenate([wt[:, 8 * k + jd[:32]] for k in range(16)], 1))
    wt = a["L2_attn_Wo"].T
    put("l2a_o", np.concatenate([wt[8 * k + jd] for k in range(16)], 1))
    put("l2a_w1", a["L2_attn_W1"].T)
    put("l2a_w2", a["L2_attn_W2"].T)
    put("mask_pair", np.repeat(np.tile(((p[:, None] % 32) // 8 == np.arange(4)[None, :]).astype(f), (1, 32)), 2, 1))
    put("head_mask", (p[:, None] // 32 == (p[None, :] % 32) // 8).astype(f))
    put("fold", (p[:, None] % 32 == np.arange(32)[None, :]).astype(f))
    put("onehot", np.tile(one_hot_buckets().reshape(32, 1024), (4, 1)))
    put("l2f_gate", np.concatenate(list(a["L2_ffn_Wg"]), 1))
    for i, c in enumerate("qkv"):
        put("l3a_" + c, a["L3_attn_W_qkv"][128 * i:128 * i + 128].T)
    put("l3a_o", a["L3_attn_W_proj"].T)
    put("l3f_u1", a["L3_ffn_U1"])
    put("l3f_v2", a["L3_ffn_V2"])

    def put_col(name, v):
        at = SPANS["cols"][0] + COLS[name]
        v = np.asarray(v)
        wp[:v.shape[0], at:at + v.shape[1]] = v
    put_col("l0x_bq", a["L0_xattn_bq"][:, None])
    put_col("l0x_bv", a["L0_xattn_bv"][:, None])
    put_col("l3x_bq", a["L3_xattn_bq"][:, None])
    put_col("l3x_bk", a["L3_xattn_bk"][:, None])
    put_col("l3x_bv", a["L3_xattn_bv"][:, None])
    put_col("l2a_b1", a["L2_attn_b1"][:, None])
    put_col("l1f_dpb1", a["L1_ffn_dp_b1"][:, None])
    for c in "qkv":
        put_col("l2a_b" + c, a["L2_attn_b" + c].reshape(16, 8)[:, jd].T)

    rows = np.zeros((1, len(ROWS), P), f)
    src = {"l0x_bo": "L0_xattn_bo", "l0a_gamma": "L0_attn_gamma", "l0a_beta": "L0_attn_beta",
           "l1x_bo": "L1_xattn_bo", "l2x_b2": "L2_xattn_b2", "l2x_g1": "L2_xattn_g1", "l2x_be1": "L2_xattn_be1",
           "l2x_g2": "L2_xattn_g2", "l2x_be2": "L2_xattn_be2", "l2a_bo": "L2_attn_bo", "l2a_b2": "L2_attn_b2",
           "l3x_bo": "L3_xattn_bo", "l3a_bp": "L3_attn_b_proj",
           "l3a_lng": "L3_attn_ln_gamma", "l3a_lnb": "L3_attn_ln_beta", "l3f_b2": "L3_ffn_b2"}
    for k, v in src.items():
        rows[0, ROWS.index(k)] = a[v]
    for e in range(4):
        rows[0, ROWS.index(f"l1f_b2_{e}")] = a["L1_ffn_eb2"][e]
        rows[0, ROWS.index(f"l2f_b2_{e}")] = a["L2_ffn_b2"][e]
    small = rows[0, ROWS.index("small")]
    small[SMALL_L1GATE:SMALL_L1GATE + 4] = a["L1_ffn_gate_b"]
    small[SMALL_DPB2:SMALL_DPB2 + 1] = a["L1_ffn_dp_b2"]
    small[SMALL_L2GATE:SMALL_L2GATE + 16] = a["L2_ffn_bg"].reshape(-1)

    def two(m):
        return m.reshape(8, 2, 64, P).transpose(1, 2, 0, 3).reshape(P, 1, 8, P)
    wkv = a["L1_xattn_Wkv"]
    l1x_w = np.concatenate([two(a["L1_xattn_Wq"].T), two(wkv[:, :1024].T), two(wkv[:, 1024:].T),
                            two(a["L1_xattn_Wo"])], 1).reshape(P, 4096)

    units = np.zeros((N_UNITS, P, WCOLS), f)

    def unit(i, w1, w3, b1, w2):
        units[i, :w1.shape[0], 0:UNIT] = w1
        if w3 is not None:
            units[i, :, UNIT:2 * UNIT] = w3
        if b1 is not None:
            units[i, :, 3 * UNIT:] = b1.reshape(2, P).T
        for c in range(2):
            units[i, :, 2 * UNIT + P * c:2 * UNIT + P * c + w2.shape[1]] = w2[P * c:P * c + P]
    u0 = FF_UNITS["l0f"][0]
    unit(u0, a["L0_ffn_Ws1"], a["L0_ffn_Ws3"], None, a["L0_ffn_Ws2"])
    for e in range(8):
        unit(u0 + 1 + e, a["L0_ffn_We1"][e], a["L0_ffn_We3"][e], None, a["L0_ffn_We2"][e])
    for e in range(4):
        unit(FF_UNITS["l1f"][0] + e, a["L1_ffn_ew1"][e], None, a["L1_ffn_eb1"][e], a["L1_ffn_ew2"][e])
    for k in range(2):
        s = slice(UNIT * k, UNIT * k + UNIT)
        unit(FF_UNITS["l2x"][0] + k, a["L2_xattn_W1"].T[:, s], None, a["L2_xattn_b1"][s], a["L2_xattn_W2"].T[s])
        unit(FF_UNITS["l3f"][0] + k, a["L3_ffn_V1"][:, s], None, a["L3_ffn_b1"][s], a["L3_ffn_U2"][s])
        for e in range(4):
            unit(FF_UNITS["l2f"][0] + 2 * e + k, a["L2_ffn_W1"][e][:, s], None, a["L2_ffn_b1"][e][s],
                 a["L2_ffn_W2"][e][s])

    ctxv = a["ctx_1024"]
    ctxT = np.zeros((B, P, KPAD), f)
    ctxT[:, :, :KEYS] = ctxv.transpose(0, 2, 1)
    ctxT[:, :, KEYS:] = ctxv[:, 256, :, None]
    ctxN = np.ones((B, KEYS, FQ), f)
    ctxN[:, :, :P] = ctxv
    mask_words = np.zeros((KEYS, B, 4), np.uint8)
    mask_words[:, :, 0] = a["mask_BxS2_bk1"].T
    arrays = {
        "ctxT": ctxT, "ctxN": ctxN,
        "fside": np.ascontiguousarray(a["fside_Bx16xSxS2_0"]).reshape(B, H * S, KEYS),
        "mask": mask_words.view(np.int32).reshape(KEYS, B),
        "wpack": wp, "wrows": rows, "l1x_w": l1x_w, "units": units,
        "relb": np.ascontiguousarray(a["L2_attn_rel_bias"]).reshape(1, 512),
        "x": np.ascontiguousarray(a["x"]).reshape(TOK, P),
    }
    nc = bacc.Bacc("TRN2", target_bir_lowering=False, num_devices=1)
    ap = {n: nc.dram_tensor("in_" + n, v.shape, mb.dt.from_np(v.dtype), kind="ExternalInput").ap()
          for n, v in arrays.items()}
    out = nc.dram_tensor("out_x", (TOK, P), F32, kind="ExternalOutput").ap()
    tiles = lambda t: t.rearrange("(t p) d -> p t d", p=P)
    perceiver(nc, ap["ctxT"], ap["ctxN"], ap["fside"], ap["mask"], ap["wpack"], ap["wrows"], ap["l1x_w"],
              ap["units"], ap["relb"], tiles(ap["x"]), tiles(out))
    r = run_bass_kernel_spmd(nc, [{"in_" + n: v for n, v in arrays.items()}], core_ids=[0])
    return r.results[0]["out_x"].reshape(B, S, P)


def one_hot_buckets():
    import math

    import numpy as np
    rel = np.arange(32)[:, None] - np.arange(32)[None, :]
    n = -rel
    ret = (n < 0).astype(np.int32) * 16
    n = np.abs(n)
    large = 8 + (np.log(np.maximum(n, 1).astype(np.float32) / 8) / math.log(128 / 8) * 8).astype(np.int32)
    bucket = ret + np.where(n < 8, n, np.minimum(large, 15))
    return (bucket[:, :, None] == np.arange(32)).astype(np.float32)
```

```python
from contextlib import ExitStack

import concourse.bass as bass
from concourse import mybir

F32 = mybir.dt.float32
I32 = mybir.dt.int32
ALU = mybir.AluOpType
ACT = mybir.ActivationFunctionType
AX = mybir.AxisListType.X

P = 128
B = 32
S = 32
NT = B * S // P
TOK = B * S
KEYS = 257
KPAD = 260
H = 16
HG = 4
DK = 8
FQ = P + 1
DH1 = 64
UNIT = 256
WCOLS = 3 * UNIT + 2
LN_EPS = 1e-5
L0X_STEPS = B // 4


def weight_plan():
    groups = {
        "first": [("ident", 128), ("l0x_q", 128), ("l0x_k", 128), ("l0x_v", 128), ("l0x_o", 128),
                  ("cols", 64)],
        "l0": [("blockones", 128), ("l0a_qkvg", 512), ("l0a_o", 128), ("l0f_gate", 8), ("rank_low8", 64),
               ("rank_low4", 16), ("mask4", 4), ("mask16", 16), ("mask_last", 128),
               ("head_mask", 128), ("fold", 32)],
        "l1": [("l1a_q", 128), ("l1a_k", 128), ("l1a_v", 128), ("l1a_o", 128), ("causal", 32),
               ("l1f_gate", 4), ("l1f_dp1", 64), ("l1f_dp2", 1)],
        "l2": [("l2x_q", 128), ("l2x_k", 128), ("l2x_v", 128), ("l2x_o", 128), ("l2a_q", 128),
               ("l2a_k", 128), ("l2a_v", 128), ("l2a_o", 128), ("l2a_w1", 128), ("l2a_w2", 128),
               ("onehot", 1024), ("l2f_gate", 16)],
        "l3": [("l3x_q", 128), ("l3x_k", 128), ("l3x_v", 128), ("l3x_o", 128), ("l3a_q", 128),
               ("l3a_k", 128), ("l3a_v", 128), ("l3a_o", 128), ("l3f_u1", 128), ("l3f_v2", 128)],
    }
    at, spans = 0, {}
    for g, items in groups.items():
        a0 = at
        for name, n in items:
            spans[name] = (at, n)
            at += n
        spans["group_" + g] = (a0, at - a0)
    return spans, at


SPANS, WTOTAL = weight_plan()

ROWS = ["l0x_bo", "l0a_gamma", "l0a_beta", "l1x_bo", "l1f_b2_0", "l1f_b2_1", "l1f_b2_2", "l1f_b2_3",
        "l2x_b2", "l2x_g1", "l2x_be1", "l2x_g2", "l2x_be2", "l2a_bo", "l2a_b2",
        "l2f_b2_0", "l2f_b2_1", "l2f_b2_2", "l2f_b2_3", "l3x_bo", "l3a_bp", "l3a_lng",
        "l3a_lnb", "l3f_b2", "small"]
SMALL_L1GATE, SMALL_DPB2, SMALL_L2GATE = 0, 4, 8

COLS = {"l0x_bq": 0, "l0x_bv": 1, "l3x_bq": 2, "l3x_bk": 3, "l2a_b1": 4, "l1f_dpb1": 5, "l3x_bv": 6,
        "l2a_bq": 7, "l2a_bk": 8, "l2a_bv": 9}

FF_UNITS = {"l0f": (0, 9), "l1f": (9, 4), "l2x": (13, 2), "l2f": (15, 8), "l3f": (23, 2)}
N_UNITS = 25


class Tally:

    def __init__(self, eng):
        self.eng, self.n = eng, {}
        self.i, self.per, self.start = None, {}, {}

    def value(self, name):
        v = self.n[name]
        return v + self.i * self.per[name] if self.i is not None and self.per.get(name) else v

    def up(self, name, k=1):
        self.n[name] = self.n.get(name, 0) + k
        return self.value(name)

    def loop(self, trips, per, body):
        self.start = dict(self.n)
        with self.eng.Fori(0, trips, 1) as i:
            self.i, self.per = i, per
            body(i)
            self.i, self.per = None, {}
        rise = {k: v - self.start.get(k, 0) for k, v in self.n.items() if v != self.start.get(k, 0)}
        assert rise == per, f"{self.eng.engine}: {rise}"
        for k, v in rise.items():
            self.n[k] = self.start.get(k, 0) + trips * v

    def paired(self, steps, per, step):
        step(0, 0)
        step(1, 1)
        self.loop(steps // 2 - 1, per, lambda i: (step(i * 2 + 2, 0), step(i * 2 + 3, 1)))


def perceiver(nc, ctxT, ctxN, fside, mask, wpack, wrows, l1x_w, units, relb, x_in, out):
    ctx = ExitStack()
    with ctx:
        def sb(name, shape, dt=F32):
            return ctx.enter_context(nc.sbuf_tensor(name, shape, dt))

        W = sb("W", [P, WTOTAL])
        RB = sb("RB", [P, len(ROWS), P])
        X = sb("X", [P, NT, P])
        XN = sb("XN", [P, NT, P])
        XNT = sb("XNT", [P, TOK])
        Y = sb("Y", [P, NT, P])
        Z = sb("Z", [P, NT, P])
        ZT = sb("ZT", [P, TOK])
        OT = sb("OT", [P, TOK])
        ACC = sb("ACC", [P, NT, P])
        ACCB = sb("ACCB", [P, NT, P])
        CTX = sb("CTX", [P, 2, 2592])
        WB = sb("WB", [P, 2, WCOLS])
        ST = sb("ST", [P, NT, 6])
        MV = sb("MV", [P, NT, 2])
        SD = sb("SD", [P, 2, NT])
        SM = sb("SM", [P, 1200])
        AR = sb("AR", [P, 18432])
        MK = sb("MK", [P, 3, B], I32)
        PS = ctx.enter_context(nc.psum_tensor("PS", [P, 8, 512], F32))
        PSF = PS[:, :, :].rearrange("p b n -> p (b n)")

        def w(name):
            a, n = SPANS[name]
            return W[:, a:a + n]

        def row(name):
            return RB[:, ROWS.index(name), :]

        def rows_t(name, nt=NT):
            return row(name).unsqueeze(1).broadcast_to([P, nt, P])

        def col(name, n=1):
            a = SPANS["cols"][0] + COLS[name]
            return W[:, a:a + n]

        def ar(a, n):
            return AR[:, a:a + n]

        ident = w("ident")

        names = """act_ran dve_ran pool_ran
            x_landed w_first w_l0 w_l1 w_l2 w_l3 rows_landed l1x_w_landed mask_landed relb_landed
            ctx_landed0 ctx_landed1 ctx_landed2 ctx_landed3
            ctx_rows_landed0 ctx_rows_landed1 unit_landed0 unit_landed1 out_landed
            var_ready std_ready norm_ready stream_ready turned turned_taken
            lin_ready lin_taken proj_ready bias_ready bias_taken resid_done
            l0s_q_ready l0s_staged l0s_scores l0s_max l0s_exp l0s_pt l0s_pt_taken l0s_u l0s_u_taken
            l0a_mm l0a_act l0a_gate l0a_qk l0a_ksum
            gate_mm gate_hidden gate_entropy gate_shift gate_act expert_weights
            up_ready act_half h_ready down_ready down_used
            y_w_ready y_w_taken yq_ready yq_taken ys_ready yclip yexp yu_ready yu_taken yt_ready yt_taken
            yo_ready yo_taken y_padded
            xq_mm xq_ready xk_ready xk_taken xv_ready xv_taken xvl_taken xqb xs_ready xs_added xmax xexp
            xsum_spread xpl_ready xpl_taken xpt_ready xpt_a xpt_d
            xu_ready x_out
            qkv_taken c_in c_scores c_shift c_exp c_rec c_divided c_probs c_pv c_first_head c_heads c_out
            pair_staged pair_landed pair_out_landed pair_out_pool pair_ready pair_turned""".split()
        sig = {n: ctx.enter_context(nc.semaphore(n)) for n in names}
        block = ctx.enter_context(nc.Block())

        l0_cT = [CTX[:, q, 0:4 * KPAD].rearrange("p (j k) -> p j k", j=4) for q in range(2)]
        l0_cn = [CTX[:, q, 1040:1040 + 8 * FQ].rearrange("p (j c f) -> p j c f", j=4, c=2) for q in range(2)]
        l0_cl = [CTX[0:1, q, 2072:2072 + 4 * FQ].rearrange("p (j f) -> p j f", j=4) for q in range(2)]
        l0_qp = ar(0, TOK)
        l0_qt = ar(TOK, TOK)
        l0_qs = [ar(2048 + 128 * q, 128) for q in range(2)]
        l0_p = [ar(2304 + KEYS * q, KEYS) for q in range(2)]
        l0_pt = [ar(2820 + 384 * q, 384).rearrange("p (c n) -> p c n", c=3) for q in range(2)]
        l0_ut = ar(3588, TOK)
        l0_ct = ar(4612, TOK)
        l0_u = ar(5636, TOK)
        l0_neg = [SM[:, 0 + q:1 + q] for q in range(2)]
        l0_sum = [SM[:, 2 + q:3 + q] for q in range(2)]
        c_buf = lambda k, a, n: CTX[:, k // 2, 1296 * (k % 2) + a:1296 * (k % 2) + a + n]
        c_T = [c_buf(k, 0, KPAD) for k in range(4)]
        c_N = [c_buf(k, KPAD, 2 * FQ).rearrange("p (c f) -> p c f", c=2) for k in range(4)]
        c_F = [c_buf(k, KPAD, HG * KEYS).rearrange("p (g k) -> p g k", g=HG) for k in range(4)]
        y_w = ar(8192, 4096).rearrange("p (m h n) -> p m h n", m=4, h=8)
        y_A = ar(14336, 2048).rearrange("p (h n) -> p h n", h=H)
        y_M = ar(12288, 2048).rearrange("p (h n) -> p h n", h=H)
        y_P = [ar(1024 * q, 1024).rearrange("p (c n) -> p c n", c=2) for q in range(2)]
        y_Q = ar(3072, 2048).rearrange("p (b h n) -> p b h n", b=4, h=H)
        y_V = ar(5120, 2048).rearrange("p (h b n) -> p h b n", h=H, b=4)
        y_C = ar(8192, 1536).rearrange("p (c n) -> p c n", c=3)
        y_U = ar(9728, 512).rearrange("p (g n) -> p g n", g=4)
        y_P_last = [ar(16384 + 512 * q, 512) for q in range(2)]
        y_last = [ar(17408 + FQ * k, FQ) for k in range(4)]
        y_hi = ar(17924, 3 * B).rearrange("p (c b) -> p c b", c=3)
        y_r = SM[:, 8:12]
        y_at = lambda h: 8 * (h % 2) + h // 2
        x_q = ar(0, TOK)
        x_qb = [ar(1024 + 512 * q, 512) for q in range(2)]
        x_k = [ar(2048 + 257 * q, 257) for q in range(2)]
        x_v = [ar(2564 + 256 * k, 256).rearrange("p (c n) -> p c n", c=2) for k in range(4)]
        x_vl = [ar(3588 + 128 * k, 128) for k in range(4)]
        x_p = [ar(4100 + 1028 * q, 1028).rearrange("p (g k) -> p g k", g=HG) for q in range(2)]
        x_s = ar(6156, 1028).rearrange("p (g k) -> p g k", g=HG)
        x_pt = ar(7184, 1024).rearrange("p (c n) -> p c n", c=2)
        x_pl = ar(8208, 128)
        x_r = [ar(8336 + 128 * q, 128) for q in range(2)]
        x_t = ar(8592, 128)
        x_neg = [SM[:, 16 + 4 * q:20 + 4 * q] for q in range(2)]
        x_sum = [SM[:, 24 + 4 * q:28 + 4 * q] for q in range(2)]
        x_rec = SM[:, 32:64]
        c_qb = ar(0, 4096)
        c_k = ar(4096, 1024)
        c_v = ar(5120, 1024)
        c_q = ar(6144, 1024)
        c_vt = ar(7168, 1024)
        c_p = [ar(8192 + 2048 * half, 2048) for half in range(2)]
        c_pt = [ar(12288 + 2048 * half, 2048) for half in range(2)]
        c_sum = [ar(16384 + 512 * half, 512) for half in range(2)]
        c_red = [SM[:, 64:128], SM[:, 520:584]]
        c_tokens = ar(8192, 3072)
        c_pairs = ar(11264, 3072)
        c_onehot = ar(14336, 1024)

        def to_pairs(u):
            return (c_pairs[DK * u:DK * u + DK, :].rearrange("i (c y) -> i c y", c=H),
                    c_tokens[:, 192 * u:192 * u + 192])

        def to_tokens(u):
            return ZT[:, 64 * u:64 * u + 64], OT[DK * u:DK * u + DK, :].rearrange("i (c x) -> i c x", c=H)
        c_relb = ar(17408, 128).rearrange("p (m k) -> p m k", m=4)
        c_rel2 = ar(17536, 128).rearrange("p (k m) -> p k m", k=32)
        flat = lambda a: a[:, :, :].rearrange("p t n -> p (t n)")
        f_h = [ar(1024 * q, 1024).rearrange("p (c n) -> p c n", c=2) for q in range(2)]
        f_s = [ar(2048 + 512 * c, 512) for c in range(2)]
        f_pt = ar(3072, TOK)
        f_w = SM[:, 128:200].rearrange("p (t e) -> p t e", t=NT)

        g_l = SM[:, 200:264]
        g_e = SM[:, 264:328]
        g_m = SM[:, 328:336]
        g_k = SM[:, 336:344]
        g_rank = SM[:, 344:408]
        g_a = ar(4096, 512)
        g_b = ar(4608, 512)
        g_h = ar(5120, TOK)
        g_z = SM[:, 408:480].rearrange("p (j t) -> p j t", j=9)

        LAYERS_FF = {
            "l0f": (True, ACT.Silu, True), "l1f": (False, ACT.Relu, True),
            "l2x": (False, ACT.Gelu, False), "l2f": (False, ACT.Gelu_apprx_tanh, True),
            "l3f": (False, ACT.Gelu_apprx_tanh, False)}

        @block.sync
        def _(sp):
            seen = Tally(sp)
            sp.dma_start(X[:, :, :], x_in).then_inc(sig["x_landed"], 16)
            a, cols = SPANS["group_first"]
            sp.dma_start(W[:, a:a + cols], wpack[:, a:a + cols]).then_inc(sig["w_first"], 16)

            def load_units(layer, trips=1):
                u0, nu = FF_UNITS[layer]

                if seen.n.get("down_ready"):
                    sp.wait_ge(sig["down_ready"], seen.up("down_ready", 0))

                def load(u, q, free):
                    if free:
                        sp.wait_ge(sig["down_ready"], seen.up("down_ready", 2))
                    sp.dma_start(WB[:, q, :], units[bass.ds(u, 1), :, :].rearrange("u p n -> (u p) n"))\
                        .then_inc(sig[f"unit_landed{q}"], 16)
                if layer == "l0f":
                    load(0, 0, False)
                    load(1, 1, False)
                    seen.loop(3, {"down_ready": 4}, lambda i: (load(i * 2 + 2, 0, True), load(i * 2 + 3, 1, True)))
                    load(8, 0, True)
                    seen.up("down_ready", 4)
                elif layer == "l2f":
                    load(u0, 0, False)
                    load(u0 + 1, 1, False)
                    for r in range(4):
                        seen.loop(3, {"down_ready": 4}, lambda i: (load(i * 2 + (u0 + 2), 0, True),
                                                                load(i * 2 + (u0 + 3), 1, True)))
                        if r < 3:
                            load(u0, 0, True)
                            load(u0 + 1, 1, True)
                    seen.up("down_ready", 4)
                else:
                    load(u0, 0, False)
                    load(u0 + 1, 1, False)
                    if nu == 4:
                        load(u0 + 2, 0, True)
                        load(u0 + 3, 1, True)
                    seen.up("down_ready", 4)

            def l0_load(s, q):
                first = isinstance(s, int) and s < 2
                if not first:
                    sp.wait_ge(sig["l0s_scores"], seen.up("l0s_scores"))
                src = ctxT[bass.ds(s * 4, 4), :, :].rearrange("j p k -> p j k")
                sp.dma_start(l0_cT[q], src).then_inc(sig[f"ctx_landed{q}"], 16)
                if not first:
                    sp.wait_ge(sig["l0s_u"], seen.up("l0s_u"))
                d = sig[f"ctx_rows_landed{q}"]
                for c in range(2):
                    src = ctxN[bass.ds(s * 4, 4), c * P:(c + 1) * P, :].rearrange("j p f -> p j f")
                    sp.dma_start(l0_cn[q][:, :, c, :], src).then_inc(d, 16)
                src = ctxN[bass.ds(s * 4, 4), 2 * P:KEYS, :].rearrange("j p f -> p j f")
                sp.dma_start(l0_cl[q], src).then_inc(d, 16)
            seen.paired(L0X_STEPS, {"l0s_scores": 2, "l0s_u": 2}, l0_load)
            seen.up("l0s_u", 2)
            load_units("l0f")

            def l1_load(b, k, free):
                if free:
                    sp.wait_ge(sig["yu_ready"], seen.up("yu_ready"))
                d = sig[f"ctx_landed{k}"]
                sp.dma_start(c_T[k], ctxT[bass.ds(b, 1), :, :].rearrange("j p k -> (j p) k")).then_inc(d, 16)
                src = ctxN[bass.ds(b, 1), 0:2 * P, :].rearrange("j (c p) f -> (j p) c f", c=2)
                sp.dma_start(c_N[k], src).then_inc(d, 16)
                sp.dma_start(y_last[k][0:1, :], ctxN[bass.ds(b, 1), 2 * P:KEYS, :].rearrange("j p f -> (j p) f"))\
                    .then_inc(d, 16)

            def l1_loads(c, free):
                for k in range(4):
                    l1_load(c * 4 + k, k, free)
            sp.wait_ge(sig["l0s_u"], seen.up("l0s_u", 0))
            sp.wait_ge(sig["y_padded"], 1)
            l1_loads(0, False)
            seen.loop(B // 4 - 1, {"yu_ready": 4}, lambda i: l1_loads(i + 1, True))
            seen.up("yu_ready", 4)
            load_units("l1f")

            def x_load(b, k, free, with_bias):
                if free:
                    sp.wait_ge(sig["xmax"], seen.up("xmax"))
                    sp.wait_ge(sig["xs_ready"], seen.up("xs_ready"))
                d = sig[f"ctx_landed{k}"]
                sp.dma_start(c_T[k], ctxT[bass.ds(b, 1), :, :].rearrange("j p k -> (j p) k")).then_inc(d, 16)
                if with_bias:
                    src = fside[bass.ds(b, 1), :, :].rearrange("j (g p) k -> (j p) g k", g=HG)
                    sp.dma_start(c_F[k], src).then_inc(d, 16)

            def x_loads(with_bias):
                for k in range(4):
                    x_load(k, k, False, with_bias)
                seen.loop(B // 4 - 1, {"xmax": 4, "xs_ready": 4},
                          lambda i: [x_load(i * 4 + (4 + k), k, True, with_bias) for k in range(4)])
                seen.up("xmax", 4)
                seen.up("xs_ready", 4)
            sp.wait_ge(sig["yu_ready"], seen.up("yu_ready", 0))
            x_loads(True)
            load_units("l2x")
            sp.wait_ge(sig["pair_staged"], 3)
            for u in range(1, H, 2):
                sp.dma_start(*to_pairs(u)).then_inc(sig["pair_landed"], 16)
            sp.wait_ge(sig["c_out"], seen.up("c_out", 4))
            for u in range(6, 11):
                sp.dma_start(*to_tokens(u)).then_inc(sig["pair_out_landed"], 16)
            load_units("l2f")
            sp.wait_ge(sig["xmax"], seen.up("xmax", 0))
            sp.wait_ge(sig["xs_ready"], seen.up("xs_ready", 0))
            x_loads(False)
            load_units("l3f")
            sp.wait_ge(sig["resid_done"], seen.up("resid_done", 10))
            sp.dma_start(out, X[:, :, :]).then_inc(sig["out_landed"], 16)
            sp.wait_ge(sig["out_landed"], 16)

        @block.tensor
        def _(pe):
            seen = Tally(pe)
            bank = lambda k: PS[:, k, :]

            def turn(src, ready="norm_ready"):
                if ready == "stream_ready":
                    pe.wait_ge(sig[ready], seen.up(ready))
                for t in range(NT):
                    if ready == "norm_ready":
                        pe.wait_ge(sig[ready], seen.up(ready))
                    m = pe.transpose(PS[:, t // 4, 128 * (t % 4):128 * (t % 4) + 128], src[:, t, :], ident)
                    if t % 4 == 3:
                        m.then_inc(sig["turned"], 1)
                pe.wait_ge(sig["turned_taken"], seen.up("turned_taken", 2))

            def wide(k, weight, src):
                for hh in range(2):
                    m = pe.matmul(bank(k + hh), weight, src[:, 512 * hh:512 * hh + 512], start=True, stop=True)
                return m

            def project(src, weight):
                for t in range(NT):
                    m = pe.matmul(PS[:, 6 + t // 4, 128 * (t % 4):128 * (t % 4) + 128],
                                  src[:, P * t:P * t + P], weight, start=True, stop=True)
                    if t % 4 == 3:
                        m.then_inc(sig["proj_ready"], 1)

            def ff(layer, src, gates=None):
                gated = LAYERS_FF[layer][0]
                u0, nu = FF_UNITS[layer]
                def up(q, hh, first=False):
                    if hh == 0:
                        pe.wait_ge(sig[f"unit_landed{q}"], seen.up(f"unit_landed{q}", 16))
                    for c in range(2):
                        if not first:
                            pe.wait_ge(sig["h_ready"], seen.up("h_ready"))
                        m = pe.matmul(bank(2 * c), WB[:, q, 128 * c:128 * c + 128],
                                      src[:, 512 * hh:512 * hh + 512], start=True, stop=True)
                        if gated:
                            m = pe.matmul(bank(2 * c + 1), WB[:, q, UNIT + 128 * c:UNIT + 128 * c + 128],
                                          src[:, 512 * hh:512 * hh + 512], start=True, stop=True)
                        m.then_inc(sig["up_ready"], 1)

                def down(q, hh, first=False):
                    if not first:
                        pe.wait_ge(sig["down_used"], seen.up("down_used"))
                    for t in range(4):
                        for c in range(2):
                            m = pe.matmul(PS[:, 4 + hh, 128 * t:128 * t + 128],
                                          f_h[hh][:, c, 128 * t:128 * t + 128],
                                          WB[:, q, 2 * UNIT + 128 * c:2 * UNIT + 128 * c + 128],
                                          start=(c == 0), stop=(c == 1))
                    m.then_inc(sig["down_ready"], 1)

                up(0, 0, first=True)
                if gates:
                    gates()
                up(0, 1)
                down(0, 0, first=True)
                up(1, 0)
                down(0, 1, first=True)

                def body(i):
                    up(1, 1)
                    down(1, 0)
                    up(0, 0)
                    down(1, 1)
                    up(0, 1)
                    down(0, 0)
                    up(1, 0)
                    down(0, 1)
                trips = (nu - 2) // 2
                if trips > 0:
                    seen.loop(trips, {"unit_landed0": 16, "unit_landed1": 16, "h_ready": 8, "down_used": 4}, body)
                up(1, 1)
                down(1, 0)
                if nu % 2:
                    up(0, 0)
                    down(1, 1)
                    up(0, 1)
                    down(0, 0)
                    pe.wait_ge(sig["h_ready"], seen.up("h_ready", 2))
                    down(0, 1)
                else:
                    pe.wait_ge(sig["h_ready"], seen.up("h_ready", 2))
                    down(1, 1)
                pe.wait_ge(sig["down_used"], seen.up("down_used", 2))

            pe.wait_ge(sig["w_first"], 16)
            turn(XN)
            wide(2, w("l0x_q"), XNT).then_inc(sig["lin_ready"], 1)
            pe.wait_ge(sig["lin_taken"], seen.up("lin_taken"))
            wide(4, w("l0x_k"), l0_qt).then_inc(sig["lin_ready"], 1)

            def l0_front(s, q):
                pe.wait_ge(sig[f"ctx_landed{q}"], seen.up(f"ctx_landed{q}", 16))
                pe.wait_ge(sig["l0s_staged"], seen.up("l0s_staged"))
                for j in range(4):
                    m = pe.matmul(PS[32 * j:32 * j + 32, 0, 0:KEYS], l0_qs[q][:, 32 * j:32 * j + 32],
                                  l0_cT[q][:, j, 0:KEYS], start=True, stop=True)
                m.then_inc(sig["l0s_scores"], 1)

            def l0_turn(q):
                pe.wait_ge(sig["l0s_exp"], seen.up("l0s_exp"))
                for c in range(2):
                    m = pe.transpose(PS[:, 1, 128 * c:128 * c + 128], l0_p[q][:, 128 * c:128 * c + 128], ident)
                m = pe.transpose(PS[0:1, 1, 256:384], l0_p[q][:, 256:257], ident)
                m.then_inc(sig["l0s_pt"], 1)

            def l0_values(s, q):
                pe.wait_ge(sig["l0s_pt_taken"], seen.up("l0s_pt_taken"))
                if not (isinstance(s, int) and s == 0):
                    pe.wait_ge(sig["l0s_u_taken"], seen.up("l0s_u_taken"))
                pe.wait_ge(sig[f"ctx_rows_landed{q}"], seen.up(f"ctx_rows_landed{q}", 48))
                for c in range(3):
                    for j in range(4):
                        k = slice(0, P) if c < 2 else slice(0, 1)
                        rows = l0_cn[q][:, j, c, 0:P] if c < 2 else l0_cl[q][0:1, j, 0:P]
                        m = pe.matmul(PS[32 * j:32 * j + 32, 2, 0:P], l0_pt[q][k, c, 32 * j:32 * j + 32], rows,
                                      start=(c == 0), stop=(c == 2), skip_group_check=True)
                m.then_inc(sig["l0s_u"], 1)

            def l0_step(s, q):
                l0_turn(q)
                l0_front(s + 1, 1 - q)
                l0_values(s, q)
            l0_front(0, 0)
            l0_step(0, 0)
            seen.loop(L0X_STEPS // 2 - 1, {"ctx_landed0": 16, "ctx_landed1": 16, "ctx_rows_landed0": 48,
                                           "ctx_rows_landed1": 48} | {k: 2 for k in (
                "l0s_staged", "l0s_exp", "l0s_pt_taken", "l0s_u_taken")},
                      lambda i: (l0_step(i * 2 + 1, 1), l0_step(i * 2 + 2, 0)))
            l0_turn(1)
            l0_values(L0X_STEPS - 1, 1)
            pe.wait_ge(sig["l0s_u_taken"], seen.up("l0s_u_taken"))
            turn(l0_u.rearrange("p (t n) -> p t n", t=NT), None)
            wide(4, w("l0x_v"), l0_ut).then_inc(sig["lin_ready"], 1)
            pe.wait_ge(sig["lin_taken"], seen.up("lin_taken"))
            project(l0_ct, w("l0x_o"))

            pe.wait_ge(sig["w_l0"], 16)
            turn(XN)
            for t in range(NT):
                m = pe.matmul(bank(t), XNT[:, P * t:P * t + P], w("l0a_qkvg"), start=True, stop=True)
                m.then_inc(sig["l0a_mm"], 1)
            pe.wait_ge(sig["l0a_qk"], seen.up("l0a_qk", 2))
            lk = ar(0, 2048).rearrange("p (t n) -> p t n", t=NT)
            for hh in range(2):
                m = pe.matmul(bank(hh), w("blockones"), lk[:, 4 * hh:4 * hh + 4, 128:256], start=True, stop=True)
            m.then_inc(sig["l0a_ksum"], 1)

            def weight_products(m_out):
                for odd in range(2):
                    r = slice(64 * odd, 64 * odd + 64)
                    for k in range(2):
                        for e in range(4):
                            m = pe.matmul(PS[:, 2 + 2 * odd + k, 128 * e:128 * e + 128],
                                          y_w[r, 2 * m_out, 4 * k + e, :], y_w[r, 2 * m_out + 1, 4 * k + e, :],
                                          start=True, stop=True)
                        m.then_inc(sig["y_w_ready"], 1)
            pe.wait_ge(sig["l1x_w_landed"], 16)
            pe.wait_ge(sig["l0a_act"], 2)
            weight_products(0)
            turn(Z, "stream_ready")
            project(ZT, w("l0a_o"))
            pe.wait_ge(sig["y_w_taken"], seen.up("y_w_taken", 4))
            weight_products(1)
            pe.wait_ge(sig["y_w_taken"], seen.up("y_w_taken", 4))

            turn(XN)
            for t in range(NT):
                m = pe.matmul(PS[:, 6, 8 * t:8 * t + 8], XNT[:, P * t:P * t + P], w("l0f_gate"),
                              start=True, stop=True)
            m.then_inc(sig["gate_mm"], 1)
            ff("l0f", XNT)

            turn(XN)

            def y_q(c, j):
                if j >= 2:
                    pe.wait_ge(sig["yq_taken"], seen.up("yq_taken"))
                elif j == 1 and not (isinstance(c, int) and c < 2):
                    pe.wait_ge(sig["yo_taken"], seen.up("yo_taken"))
                for e in range(4):
                    m = pe.matmul(PS[:, 7 * (j % 2), P * e:P * e + P], y_A[:, y_at(4 * j + e), :],
                                  XNT[:, bass.ds(c * P, P)], start=True, stop=True)
                m.then_inc(sig["yq_ready"], 1)

            def y_s(k, first):
                pe.wait_ge(sig[f"ctx_landed{k}"], seen.up(f"ctx_landed{k}", 48))
                if k == 0:
                    pe.wait_ge(sig["yq_taken"], seen.up("yq_taken", 2))
                if not (first and k == 0):
                    pe.wait_ge(sig["yclip"], seen.up("yclip"))
                rhs = y_Q[:, k, :, :].rearrange("p h n -> p (h n)")
                for c in range(2):
                    pe.matmul(bank(1 + c), c_T[k][:, P * c:P * c + P], rhs, start=True, stop=True)
                m = pe.matmul(PS[0:1, 3, :], c_T[k][:, 256:257], rhs, start=True, stop=True)
                m.then_inc(sig["ys_ready"], 1)

            def y_t(k):
                pe.wait_ge(sig["yu_taken"], seen.up("yu_taken"))
                if k > 0:
                    pe.wait_ge(sig["yt_taken"], seen.up("yt_taken"))
                for g in range(HG):
                    m = pe.transpose(PS[:, 6, P * g:P * g + P], y_U[:, g, :], ident)
                m.then_inc(sig["yt_ready"], 1)

            def y_u(k):
                q = k % 2
                pe.wait_ge(sig["yexp"], seen.up("yexp"))
                for g in range(HG):
                    o = PS[:, 4 + g // 2, FQ * (g % 2):FQ * (g % 2) + FQ]
                    for c in range(3):
                        probs = y_P[q][:, c, P * g:P * g + P] if c < 2 else y_P_last[q][:, P * g:P * g + P]
                        m = pe.matmul(o, probs, c_N[k][:, c, :] if c < 2 else y_last[k],
                                      start=(c == 0), stop=(c == 2))
                m.then_inc(sig["yu_ready"], 1)

            def y_o():
                pe.wait_ge(sig["yt_taken"], seen.up("yt_taken"))
                for h in range(H):
                    m = pe.matmul(PS[:, 7, 0:P], y_M[:, y_at(h), :], y_V[:, h, :, :].rearrange("p b n -> p (b n)"),
                                  start=(h == 0), stop=(h == H - 1))
                m.then_inc(sig["yo_ready"], 1)

            def y_chunk(c, first=False, last=False):
                for k in range(4):
                    y_s(k, first)
                    if k == 3 and not last:
                        y_q(c + 1, 0)
                        y_q(c + 1, 1)
                    if not first or k >= 2:
                        y_t((k - 2) % 4)
                    if k == 3 and not last:
                        y_q(c + 1, 2)
                        y_q(c + 1, 3)
                    if not first or k >= 1:
                        y_u((k - 1) % 4)
                    if k == 1 and not first:
                        y_o()

            for j in range(4):
                y_q(0, j)
            y_chunk(0, first=True)
            y_chunk(1)
            seen.loop(B // 4 - 3, {f"ctx_landed{k}": 48 for k in range(4)} | {k: 4 for k in (
                "yq_taken", "yclip", "yexp", "yu_taken", "yt_taken")} | {"yo_taken": 1}, lambda i: y_chunk(i + 2))
            y_chunk(B // 4 - 1, last=True)
            y_t(2)
            y_u(3)
            y_t(3)
            pe.wait_ge(sig["yo_taken"], seen.up("yo_taken"))
            y_o()
            seen.up("yclip")
            pe.wait_ge(sig["yo_taken"], seen.up("yo_taken"))
            for t in range(NT):
                m = pe.transpose(PS[:, 6 + t // 4, 128 * (t % 4):128 * (t % 4) + 128], OT[:, P * t:P * t + P], ident)
                if t % 4 == 3:
                    m.then_inc(sig["proj_ready"], 1)

            def core(pairs=False):
                pe.wait_ge(sig["qkv_taken"], seen.up("qkv_taken", 2))
                for half in range(2):
                    if half:
                        if pairs:
                            pe.wait_ge(sig["pair_ready"], seen.up("pair_ready"))
                            for t in range(NT):
                                m = pe.transpose(PS[:, 4 + t // 4, P * (t % 4):P * (t % 4) + P],
                                                 c_v[:, P * t:P * t + P], ident)
                            m.then_inc(sig["pair_turned"], 1)
                        pe.wait_ge(sig["qkv_taken"], seen.up("qkv_taken"))
                    pe.wait_ge(sig["c_in"], seen.up("c_in"))
                    for g in range(HG):
                        r = slice(32 * g, 32 * g + 32)
                        for tt in range(4):
                            for b in range(4):
                                n = 16 * half + 4 * tt + b
                                m = pe.matmul(PS[32 * b:32 * b + 32, 4 * half + g, P * tt:P * tt + P],
                                              c_k[r, 32 * n:32 * n + 32], c_qb[r, P * n:P * n + P],
                                              start=True, stop=True)
                        m.then_inc(sig["c_scores"], 1)
                for half in range(2):
                    pt = c_pt[half].rearrange("p (g t n) -> p g t n", g=HG, t=4)
                    for g in range(HG):
                        pe.wait_ge(sig["c_probs"], seen.up("c_probs"))
                        for tt in range(4):
                            for b in range(4):
                                at = P * (4 * half + tt) + 32 * g
                                m = pe.matmul(PS[32 * g:32 * g + 32, 4 * half + b, P * tt:P * tt + P],
                                              c_vt[32 * b:32 * b + 32, at:at + 32], pt[32 * b:32 * b + 32, g, tt, :],
                                              start=True, stop=True)
                    m.then_inc(sig["c_pv"], 1)
                pe.wait_ge(sig["c_out"], seen.up("c_out", 2))

            def self_attention(q, k, v, o):
                turn(XN)
                wide(2, w(q), XNT)
                wide(4, w(k), XNT)
                for t in range(NT):
                    m = pe.matmul(PS[:, 6 + t // 4, P * (t % 4):P * (t % 4) + P], XNT[:, P * t:P * t + P], w(v),
                                  start=True, stop=True)
                m.then_inc(sig["lin_ready"], 1)
                core()
                project(OT, w(o))

            pe.wait_ge(sig["w_l1"], 16)
            self_attention("l1a_q", "l1a_k", "l1a_v", "l1a_o")

            turn(XN)
            for t in range(NT):
                m = pe.matmul(PS[:, 6, 4 * t:4 * t + 4], XNT[:, P * t:P * t + P], w("l1f_gate"),
                              start=True, stop=True)
            for hh in range(2):
                m = pe.matmul(PS[0:64, 2 + hh, :], w("l1f_dp1"), XNT[:, 512 * hh:512 * hh + 512],
                              start=True, stop=True)
            m.then_inc(sig["gate_mm"], 1)
            pe.wait_ge(sig["gate_hidden"], seen.up("gate_hidden"))
            for t in range(NT):
                m = pe.matmul(PS[:, 7, t:t + 1], g_h[0:64, P * t:P * t + P], w("l1f_dp2")[0:64, :],
                              start=True, stop=True)
            m.then_inc(sig["gate_mm"], 1)
            ff("l1f", XNT)

            def cross(kname, vname, biased):
                def x_kv(k, first):
                    pe.wait_ge(sig[f"ctx_landed{k}"], seen.up(f"ctx_landed{k}", 32 if biased else 16))
                    m = pe.matmul(PS[:, 0, 0:KEYS], w(kname), c_T[k][:, 0:KEYS], start=True, stop=True)
                    m.then_inc(sig["xk_ready"], 1)
                    if not first:
                        pe.wait_ge(sig["xpl_taken"], seen.up("xpl_taken"))
                    for c in range(2):
                        pe.matmul(PS[:, 1, P * c:P * c + P], c_T[k][:, P * c:P * c + P], w(vname),
                                  start=True, stop=True)
                    m = pe.matmul(PS[0:4, 1, 256:384], c_T[k][:, 256:260], w(vname), start=True, stop=True)
                    m.then_inc(sig["xv_ready"], 1)

                def x_s(q, first):
                    pe.wait_ge(sig["xk_taken"], seen.up("xk_taken"))
                    pe.wait_ge(sig["xqb"], seen.up("xqb"))
                    if not first and biased:
                        pe.wait_ge(sig["xs_added"], seen.up("xs_added"))
                    for g in range(HG):
                        if not first and not biased:
                            pe.wait_ge(sig["xexp"], seen.up("xexp"))
                        m = pe.matmul(PS[:, 2 + g, 0:KEYS], x_qb[q][:, P * g:P * g + P], x_k[q],
                                      start=True, stop=True)
                    m.then_inc(sig["xs_ready"], 1)

                def x_turn(q, first, last=False):
                    if biased or last:
                        pe.wait_ge(sig["xexp"], seen.up("xexp", HG))
                    if not last:
                        pe.wait_ge(sig["xv_taken"], seen.up("xv_taken"))
                        pe.wait_ge(sig["xvl_taken"], seen.up("xvl_taken"))
                    if not first:
                        pe.wait_ge(sig["x_out"], seen.up("x_out"))
                    m = pe.transpose(PS[0:4, 1, 384:512], x_p[q][:, :, 256], ident)
                    m.then_inc(sig["xpl_ready"], 1)
                    for c in range(2):
                        for g in range(HG):
                            m = pe.transpose(PS[:, 6 + c, P * g:P * g + P], x_p[q][:, g, P * c:P * c + P], ident)
                    m.then_inc(sig["xpt_ready"], 1)

                def x_pv(k, last=False):
                    q = k % 2
                    if last:
                        pe.wait_ge(sig["xpl_taken"], seen.up("xpl_taken"))
                    pe.wait_ge(sig["xsum_spread"], seen.up("xsum_spread"))
                    pe.wait_ge(sig["xpt_a"], seen.up("xpt_a"))
                    if not biased:
                        pe.wait_ge(sig["xpt_d"], seen.up("xpt_d"))
                    pe.matmul(PS[:, 7, 0:32], x_r[q], w("fold"), start=True, stop=True)
                    for g in range(HG):
                        for c in range(2):
                            pe.matmul(PS[32 * g:32 * g + 32, 6, 0:128], x_v[k][:, c, 32 * g:32 * g + 32],
                                      x_pt[:, c, P * g:P * g + P], start=(c == 0), stop=False,
                                      skip_group_check=True)
                    m = pe.matmul(PS[:, 6, 0:128], x_vl[k][0:4, :], x_pl[0:4, :], start=False, stop=True,
                                  skip_group_check=True)
                    m.then_inc(sig["xu_ready"], 1)

                def x_four(first=False, last=False):
                    for k in range(4):
                        x_s(k % 2, first and k == 0)
                        if not (first and k == 0):
                            x_turn((k - 1) % 2, first and k == 1)
                        if first and k == 0:
                            pe.wait_ge(sig["xv_taken"], seen.up("xv_taken"))
                            pe.wait_ge(sig["xvl_taken"], seen.up("xvl_taken"))
                        end = last and k == 3
                        if not end:
                            x_kv((k + 1) % 4, first and k == 0)
                        if not (first and k == 0):
                            x_pv((k - 1) % 4, last=end)

                x_kv(0, True)
                x_four(first=True)
                seen.loop(B // 4 - 2, {f"ctx_landed{k}": 32 if biased else 16 for k in range(4)} |
                          {"xs_added" if biased else "xpt_d": 4} |
                          {"xexp": 16} | {k: 4 for k in "xk_taken xv_taken xvl_taken xqb xpl_taken xpt_a xsum_spread "
                                         "x_out".split()}, lambda i: x_four())
                x_four(last=True)
                x_turn(1, False, last=True)
                x_pv(3, last=True)
                if biased:
                    seen.up("xs_added")
                pe.wait_ge(sig["x_out"], seen.up("x_out", 1 if biased else 2))

            pe.wait_ge(sig["w_l2"], 16)
            turn(XN)
            wide(2, w("l2x_q"), XNT).then_inc(sig["xq_mm"], 1)
            cross("l2x_k", "l2x_v", True)
            project(OT, w("l2x_o"))
            turn(Z, "stream_ready")
            ff("l2x", ZT)

            turn(XN)
            wide(2, w("l2a_q"), XNT)
            wide(4, w("l2a_k"), XNT)
            wide(6, w("l2a_v"), XNT).then_inc(sig["lin_ready"], 1)
            core(pairs=True)
            pe.wait_ge(sig["pair_out_landed"], 16 * 11)
            pe.wait_ge(sig["pair_out_pool"], 16 * (H - 11))
            project(ZT, w("l2a_o"))
            turn(Z)
            wide(2, w("l2a_w1"), ZT).then_inc(sig["lin_ready"], 1)
            pe.wait_ge(sig["lin_taken"], seen.up("lin_taken"))
            project(OT, w("l2a_w2"))

            def moe_round(r):
                turn(XN) if r == 0 else turn(ACC, None)
                src = XNT if r == 0 else ZT

                def gates():
                    for t in range(NT):
                        m = pe.matmul(PS[:, 6, 4 * t:4 * t + 4], src[:, P * t:P * t + P],
                                      w("l2f_gate")[:, 4 * r:4 * r + 4], start=True, stop=True)
                    m.then_inc(sig["gate_mm"], 1)
                ff("l2f", src, gates)
            for r in range(4):
                moe_round(r)

            pe.wait_ge(sig["w_l3"], 16)
            turn(XN)
            wide(2, w("l3x_q"), XNT).then_inc(sig["xq_mm"], 1)
            cross("l3x_k", "l3x_v", False)
            project(OT, w("l3x_o"))
            self_attention("l3a_q", "l3a_k", "l3a_v", "l3a_o")
            turn(XN)
            wide(6, w("l3f_u1"), XNT).then_inc(sig["lin_ready"], 1)
            pe.wait_ge(sig["lin_taken"], seen.up("lin_taken"))
            ff("l3f", f_pt)
            turn(ACC, None)
            project(ZT, w("l3f_v2"))

        @block.scalar
        def _(act):
            seen = Tally(act)

            def f(o, i, fn=ACT.Identity, **k):
                return act.activation(o, i, fn, **k)

            def prepare(fn):
                f(SM[:, 592:593], ident[:, 0:1], fn).then_inc(sig["act_ran"], 1)
                act.wait_ge(sig["act_ran"], seen.up("act_ran"))

            def norm_std(then=None):
                prepare(ACT.Sqrt)
                act.wait_ge(sig["var_ready"], seen.up("var_ready"))
                f(SD[:, 1, :], SD[:, 0, :], ACT.Sqrt).then_inc(sig["std_ready"], 1)
                act.wait_ge(sig["std_ready"], seen.up("std_ready"))
                if then:
                    prepare(then)

            def turned(dst):
                for hh in range(2):
                    act.wait_ge(sig["turned"], seen.up("turned"))
                    act.copy(dst[:, 512 * hh:512 * hh + 512], PS[:, hh, :]).then_inc(sig["turned_taken"], 1)
                    act.wait_ge(sig["turned_taken"], seen.up("turned_taken"))

            def ff(layer, gates=None):
                gated, fn, _ = LAYERS_FF[layer]
                nu = FF_UNITS[layer][1]

                def half(q, hh, landed=False):
                    if gated:
                        for c in range(2):
                            act.wait_ge(sig["up_ready"], seen.up("up_ready"))
                            if not landed:
                                act.wait_ge(sig["h_ready"], seen.up("h_ready"))
                            f(f_s[c], PS[:, 2 * c, :], fn).then_inc(sig["act_half"], 1)
                            act.wait_ge(sig["act_half"], seen.up("act_half"))
                        return
                    for c in range(2):
                        act.wait_ge(sig["up_ready"], seen.up("up_ready"))
                        if c == 0 and not landed:
                            act.wait_ge(sig["down_ready"], seen.up("down_ready"))
                        f(f_h[hh][:, c, :], PS[:, 2 * c, :], fn,
                                 bias=WB[:, q, 3 * UNIT + c:3 * UNIT + c + 1]).then_inc(sig["h_ready"], 1)
                        act.wait_ge(sig["h_ready"], seen.up("h_ready"))
                half(0, 0, True)
                half(0, 1, not gated)
                if gates:
                    gates()
                trips = (nu - 2) // 2
                if trips > 0:
                    def body(i):
                        for q in (1, 0):
                            for hh in range(2):
                                half(q, hh)
                    per = {"up_ready": 8, "act_half": 8, "h_ready": 8} if gated else \
                        {"up_ready": 8, "h_ready": 8, "down_ready": 4}
                    seen.loop(trips, per, body)
                half(1, 0)
                half(1, 1)
                if nu % 2:
                    half(0, 0)
                    half(0, 1)
                if gated:
                    seen.up("h_ready", 2)
                    seen.up("down_ready", 2 * nu)
                else:
                    seen.up("down_ready", 2)

            act.wait_ge(sig["w_first"], 16)
            norm_std(ACT.Exp)
            turned(XNT[:, :])
            act.wait_ge(sig["lin_ready"], seen.up("lin_ready"))
            f(l0_qt, PSF[:, 1024:2048], bias=col("l0x_bq")).then_inc(sig["lin_taken"], 1)
            act.wait_ge(sig["lin_taken"], seen.up("lin_taken"))
            act.wait_ge(sig["lin_ready"], seen.up("lin_ready"))
            f(l0_qp, PSF[:, 2048:3072], scale=float(P) ** -0.5).then_inc(sig["l0s_q_ready"], 1)
            act.wait_ge(sig["l0s_q_ready"], seen.up("l0s_q_ready"))

            def l0_exp(s, q):
                act.wait_ge(sig["l0s_max"], seen.up("l0s_max"))
                if not (isinstance(s, int) and s < 2):
                    act.wait_ge(sig["l0s_pt"], seen.up("l0s_pt"))
                f(l0_p[q], PS[:, 0, 0:KEYS], ACT.Exp, bias=l0_neg[q], accum_out=l0_sum[q]).then_inc(sig["l0s_exp"], 1)
                act.wait_ge(sig["l0s_exp"], seen.up("l0s_exp"))
            l0_exp(0, 0)
            l0_exp(1, 1)
            seen.loop(L0X_STEPS // 2 - 1, {"l0s_max": 2, "l0s_pt": 2, "l0s_exp": 2},
                   lambda i: (l0_exp(None, 0), l0_exp(None, 1)))
            seen.up("l0s_pt", 2)
            turned(l0_ut)
            act.wait_ge(sig["lin_ready"], seen.up("lin_ready"))
            f(l0_ct, PSF[:, 2048:3072], bias=col("l0x_bv")).then_inc(sig["lin_taken"], 1)
            act.wait_ge(sig["lin_taken"], seen.up("lin_taken"))

            norm_std(ACT.Exp)
            turned(XNT[:, :])
            le = ar(2048, 2048).rearrange("p (t n) -> p t n", t=NT)
            lvg = ar(4096, 2048).rearrange("p (c t n) -> p t c n", c=2, t=NT)
            for hh in range(2):
                t4 = slice(4 * hh, 4 * hh + 4)
                act.wait_ge(sig["l0a_mm"], seen.up("l0a_mm", 4))
                f(le[:, t4, :], PS[:, t4, 0:256], ACT.Exp).then_inc(sig["act_ran"], 1)
                act.wait_ge(sig["act_ran"], seen.up("act_ran"))
                act.copy(lvg[:, t4], PS[:, t4, 256:512].rearrange("p t (c n) -> p t c n", c=2))\
                    .then_inc(sig["l0a_act"], 1)
                act.wait_ge(sig["l0a_act"], seen.up("l0a_act"))
            f(ar(5120, 1024), ar(5120, 1024), ACT.Silu).then_inc(sig["l0a_gate"], 1)
            act.wait_ge(sig["l0a_gate"], seen.up("l0a_gate"))

            def weight_products(m_out):
                dst, scale = ((y_A, float(DH1) ** -0.5), (y_M, 1.0))[m_out]
                for k in range(4):
                    act.wait_ge(sig["y_w_ready"], seen.up("y_w_ready"))
                    f(dst[:, 4 * k:4 * k + 4, :], PS[:, 2 + k, :].rearrange("p (h n) -> p h n", h=4),
                      scale=scale).then_inc(sig["y_w_taken"], 1)
                    act.wait_ge(sig["y_w_taken"], seen.up("y_w_taken"))
            weight_products(0)
            norm_std()
            turned(ZT[:, :])

            weight_products(1)
            norm_std(ACT.Sigmoid)
            turned(XNT[:, :])
            act.wait_ge(sig["gate_mm"], seen.up("gate_mm"))
            f(g_e, PS[:, 6, 0:64], ACT.Sigmoid).then_inc(sig["gate_act"], 1)
            act.wait_ge(sig["gate_act"], seen.up("gate_act"))
            ff("l0f")

            norm_std(ACT.Exp)
            turned(XNT[:, :])

            def y_q(j, first):
                act.wait_ge(sig["yq_ready"], seen.up("yq_ready"))
                if j == 0 and not first:
                    act.wait_ge(sig["ys_ready"], seen.up("ys_ready", 4))
                act.copy(y_Q[:, :, 4 * j:4 * j + 4, :],
                         PS[:, 7 * (j % 2), :].rearrange("p (h b n) -> p b h n", h=4, b=4))\
                             .then_inc(sig["yq_taken"], 1)
                act.wait_ge(sig["yq_taken"], seen.up("yq_taken"))

            def y_exp(k, first):
                q = k % 2
                act.wait_ge(sig["yclip"], seen.up("yclip"))
                if not (first and k < 2):
                    act.wait_ge(sig["yu_ready"], seen.up("yu_ready"))
                f(y_P[q], y_C[:, 0:2, :], ACT.Exp).then_inc(sig["act_ran"], 1)
                act.wait_ge(sig["act_ran"], seen.up("act_ran"))
                f(y_P_last[q][0:1, :], y_C[0:1, 2, :], ACT.Exp).then_inc(sig["yexp"], 1)
                act.wait_ge(sig["yexp"], seen.up("yexp"))

            def y_t(k, first):
                act.wait_ge(sig["yt_ready"], seen.up("yt_ready"))
                if k == 0 and not first:
                    act.wait_ge(sig["yo_ready"], seen.up("yo_ready"))
                act.copy(y_V[:, :, k, :], PS[:, 6, :].rearrange("p (h n) -> p h n", h=H)).then_inc(sig["yt_taken"], 1)
                act.wait_ge(sig["yt_taken"], seen.up("yt_taken"))

            def y_chunk(first=False, last=False):
                for k in range(4):
                    if k == 3 and not last:
                        y_q(0, False)
                        y_q(1, False)
                    if not first or k >= 2:
                        y_t((k - 2) % 4, first)
                    if k == 3 and not last:
                        y_q(2, False)
                        y_q(3, False)
                    y_exp(k, first)
            act.wait_ge(sig["y_padded"], 1)
            for j in range(4):
                y_q(j, True)
            y_chunk(first=True)
            seen.loop(B // 4 - 2, {k: 4 for k in ("yq_ready", "ys_ready", "yq_taken", "yclip", "yu_ready", "act_ran",
                                                  "yexp", "yt_ready", "yt_taken")} | {"yo_ready": 1},
                      lambda i: y_chunk())
            y_chunk(last=True)
            y_t(2, False)
            y_t(3, False)
            seen.up("ys_ready", 4)
            seen.up("yu_ready", 2)
            seen.up("yo_ready")

            def core(pairs=False):
                for half in range(2):
                    act.wait_ge(sig["c_shift"], seen.up("c_shift"))
                    f(c_p[half], c_p[half], ACT.Exp).then_inc(sig["c_exp"], 1)
                    act.wait_ge(sig["c_exp"], seen.up("c_exp"))
                heads = lambda half: PSF[:, 2048 * half:2048 * half + 2048]\
                    .rearrange("p (n h q) -> p n h q", n=16, h=4)
                for half in range(2):
                    act.wait_ge(sig["c_pv"], seen.up("c_pv"))
                    f(c_sum[half].rearrange("p (n q) -> p n q", n=16), heads(half)[:, :, 0, :],
                      scale=w("mask4")[:, 0:1]).then_inc(sig["c_first_head"], 1)
                    act.wait_ge(sig["c_first_head"], seen.up("c_first_head"))
                for half in range(2):
                    act.wait_ge(sig["c_heads"], seen.up("c_heads"))
                    if not pairs:
                        act.copy(OT[:, 512 * half:512 * half + 512].rearrange("p (t b q) -> p b t q", t=4, b=4),
                                 c_sum[half].rearrange("p (b t q) -> p b t q", b=4, t=4)).then_inc(sig["c_out"], 1)
                        act.wait_ge(sig["c_out"], seen.up("c_out"))
                    else:
                        for b in range(4):
                            dst = OT[:, :].rearrange("p (c m b r) -> p b m r c", c=H, m=8, b=4)
                            src = c_sum[half].rearrange("p (b t r c) -> p b t r c", b=4, t=4, r=2)
                            ins = act.copy(dst[:, b, 4 * half:4 * half + 4], src[:, b])
                            name = "c_out" if b == 3 else "act_ran"
                            ins.then_inc(sig[name], 1)
                            act.wait_ge(sig[name], seen.up(name))

            def self_attention(scale, second_norm=False):
                norm_std(None if second_norm else ACT.Exp)
                turned(XNT[:, :])
                act.wait_ge(sig["lin_ready"], seen.up("lin_ready"))
                f(c_q, PSF[:, 1024:2048], scale=scale).then_inc(sig["qkv_taken"], 1)
                act.wait_ge(sig["qkv_taken"], seen.up("qkv_taken"))
                act.copy(c_k, PSF[:, 2048:3072]).then_inc(sig["qkv_taken"], 1)
                act.wait_ge(sig["qkv_taken"], seen.up("qkv_taken"))
                act.copy(c_vt, PSF[:, 3072:4096]).then_inc(sig["qkv_taken"], 1)
                act.wait_ge(sig["qkv_taken"], seen.up("qkv_taken"))
                if second_norm:
                    norm_std(ACT.Exp)
                core()

            self_attention(float(DK) ** -0.5)

            norm_std(ACT.Exp)
            turned(XNT[:, :])
            act.wait_ge(sig["gate_mm"], seen.up("gate_mm"))
            f(g_h[0:64, :], PSF[0:64, 1024:2048], ACT.Relu, bias=col("l1f_dpb1")[0:64, :])\
                .then_inc(sig["gate_hidden"], 1)
            act.wait_ge(sig["gate_hidden"], seen.up("gate_hidden"))
            act.wait_ge(sig["gate_entropy"], seen.up("gate_entropy"))
            f(g_z[:, 2, :], g_z[:, 1, :], ACT.Exp, scale=-1.0).then_inc(sig["gate_act"], 1)
            act.wait_ge(sig["gate_act"], seen.up("gate_act"))
            f(g_z[:, 3, :], g_z[:, 2, :], ACT.Ln, bias=SM[:, 500:501]).then_inc(sig["gate_act"], 1)
            act.wait_ge(sig["gate_act"], seen.up("gate_act"))
            act.wait_ge(sig["gate_shift"], seen.up("gate_shift"))
            f(g_e[:, 0:32], g_e[:, 0:32], ACT.Exp).then_inc(sig["gate_act"], 1)
            act.wait_ge(sig["gate_act"], seen.up("gate_act"))
            ff("l1f")

            def cross(bk):
                def x_kv(k):
                    act.wait_ge(sig["xk_ready"], seen.up("xk_ready"))
                    f(x_k[k % 2], PS[:, 0, 0:KEYS], bias=col(bk) if bk else 0.0).then_inc(sig["xk_taken"], 1)
                    act.wait_ge(sig["xk_taken"], seen.up("xk_taken"))
                    act.wait_ge(sig["xv_ready"], seen.up("xv_ready"))
                    act.copy(x_v[k], PS[:, 1, 0:256].rearrange("p (c n) -> p c n", c=2)).then_inc(sig["xv_taken"], 1)
                    act.wait_ge(sig["xv_taken"], seen.up("xv_taken"))

                def x_turned():
                    act.wait_ge(sig["xpl_ready"], seen.up("xpl_ready"))
                    act.copy(x_pl[0:4, :], PS[0:4, 1, 384:512]).then_inc(sig["xpl_taken"], 1)
                    act.wait_ge(sig["xpl_taken"], seen.up("xpl_taken"))
                    act.wait_ge(sig["xpt_ready"], seen.up("xpt_ready"))
                    if bk:
                        act.copy(x_pt[:, 0, :], PS[:, 6, :]).then_inc(sig["xpt_a"], 1)
                    else:
                        act.copy(x_pt, PS[:, 6:8, :]).then_inc(sig["xpt_a"], 1)
                    act.wait_ge(sig["xpt_a"], seen.up("xpt_a"))

                def x_exp(q):
                    act.wait_ge(sig["xmax"], seen.up("xmax"))
                    for g in range(HG):
                        src = x_s[:, g, :] if not bk else PS[:, 2 + g, 0:KEYS]
                        ins = f(x_p[q][:, g, :], src, ACT.Exp, bias=x_neg[q][:, g:g + 1],
                                accum_out=x_sum[q][:, g:g + 1])
                        ins.then_inc(sig["xexp"], 1)
                        act.wait_ge(sig["xexp"], seen.up("xexp"))

                def x_four(first=False, last=False):
                    for k in range(4):
                        if not (first and k == 0):
                            x_turned()
                        if not (last and k == 3):
                            x_kv((k + 1) % 4)
                        x_exp(k % 2)
                x_kv(0)
                x_four(first=True)
                seen.loop(B // 4 - 2, {"xexp": 16} | {k: 4 for k in "xk_ready xk_taken xv_ready xv_taken xpl_ready "
                          "xpl_taken xpt_ready xpt_a xmax".split()}, lambda i: x_four())
                x_four(last=True)
                x_turned()

            norm_std(ACT.Exp)
            turned(XNT[:, :])
            cross(None)
            norm_std(LAYERS_FF["l2x"][1])
            turned(ZT[:, :])
            ff("l2x")
            norm_std()

            norm_std(ACT.Exp)
            turned(XNT[:, :])
            act.wait_ge(sig["lin_ready"], seen.up("lin_ready"))
            for k, c in enumerate("qkv"):
                f(c_tokens.rearrange("p (u k x) -> p k u x", u=H, k=3)[:, k],
                  PSF[:, TOK + TOK * k:2 * TOK + TOK * k].rearrange("p (u x) -> p u x", u=H), bias=col("l2a_b" + c))\
                    .then_inc(sig["pair_staged"], 1)
                act.wait_ge(sig["pair_staged"], seen.up("pair_staged"))
            for u in range(0, H, 2):
                act.dma_start(*to_pairs(u)).then_inc(sig["pair_landed"], 16)
            act.wait_ge(sig["pair_landed"], 16 * H)
            for k, dst in enumerate((c_q, c_k, c_v)):
                ins = act.copy(dst.rearrange("p (m c) -> p m c", c=H),
                               c_pairs.rearrange("p (c k m) -> p k m c", c=H, k=3)[:, k])
                name = "pair_ready" if k == 2 else "qkv_taken"
                ins.then_inc(sig[name], 1)
                act.wait_ge(sig[name], seen.up(name))
            act.wait_ge(sig["pair_turned"], seen.up("pair_turned"))
            act.copy(c_vt, PSF[:, 2048:3072]).then_inc(sig["qkv_taken"], 1)
            act.wait_ge(sig["qkv_taken"], seen.up("qkv_taken"))
            core(pairs=True)
            for u in range(0, 6):
                act.dma_start(*to_tokens(u)).then_inc(sig["pair_out_landed"], 16)
            norm_std()
            turned(ZT[:, :])
            act.wait_ge(sig["lin_ready"], seen.up("lin_ready"))
            f(OT[:, :], PSF[:, 1024:2048], bias=col("l2a_b1")).then_inc(sig["lin_taken"], 1)
            act.wait_ge(sig["lin_taken"], seen.up("lin_taken"))
            norm_std()

            norm_std()

            def gate_exp():
                act.wait_ge(sig["gate_shift"], seen.up("gate_shift"))
                f(g_e[:, 0:32], g_e[:, 0:32], ACT.Exp).then_inc(sig["gate_act"], 1)
                act.wait_ge(sig["gate_act"], seen.up("gate_act"))
                prepare(LAYERS_FF["l2f"][1])
            for r in range(4):
                turned(XNT[:, :] if r == 0 else ZT[:, :])
                prepare(LAYERS_FF["l2f"][1])
                ff("l2f", gate_exp)

            norm_std(ACT.Exp)
            turned(XNT[:, :])
            cross("l3x_bk")
            self_attention(float(DK) ** -0.5, True)
            norm_std(LAYERS_FF["l3f"][1])
            turned(XNT[:, :])
            act.wait_ge(sig["lin_ready"], seen.up("lin_ready"))
            act.copy(f_pt, PSF[:, 3072:4096]).then_inc(sig["lin_taken"], 1)
            act.wait_ge(sig["lin_taken"], seen.up("lin_taken"))
            ff("l3f")
            turned(ZT[:, :])

        @block.vector
        def _(dve):
            seen = Tally(dve)

            def tt(o, a, b, op):
                return dve.tensor_tensor(o, a, b, op)

            def stats(src, tiles):
                for t in tiles:
                    dve.bn_stats(ST[:, t, :], src[:, t, :]).then_inc(sig["dve_ran"], 1)
                    seen.up("dve_ran")
                dve.wait_ge(sig["dve_ran"], seen.up("dve_ran", 0))

            def layernorm(src, dst, eps, signal=True, stats_done=False):
                if not stats_done:
                    stats(src, range(NT))
                for t in range(NT):
                    dve.bn_aggr(MV[:, t, :], ST[:, t, :]).then_inc(sig["dve_ran"], 1)
                    seen.up("dve_ran")
                    if t == NT - 1:
                        dve.wait_ge(sig["dve_ran"], seen.up("dve_ran", 0))
                dve.tensor_scalar(SD[:, 0, :], MV[:, :, 1], eps, None, ALU.add).then_inc(sig["var_ready"], 1)
                dve.wait_ge(sig["var_ready"], seen.up("var_ready"))
                dve.wait_ge(sig["std_ready"], seen.up("std_ready"))
                dve.reciprocal(SD[:, 1, :], SD[:, 1, :]).then_inc(sig["dve_ran"], 1)
                dve.wait_ge(sig["dve_ran"], seen.up("dve_ran"))
                for t in range(NT):
                    ins = dve.tensor_scalar(dst[:, t, :], src[:, t, :], MV[:, t, 0:1], SD[:, 1, t:t + 1],
                                            ALU.subtract, ALU.mult)
                    name = "norm_ready" if signal else "dve_ran"
                    ins.then_inc(sig[name], 1)
                    seen.up(name)
                    if t == NT - 1:
                        dve.wait_ge(sig[name], seen.up(name, 0))

            def affine(dst, g, b):
                tt(dst, dst, rows_t(g), ALU.mult).then_inc(sig["dve_ran"], 1)
                dve.wait_ge(sig["dve_ran"], seen.up("dve_ran"))
                return tt(dst, dst, rows_t(b), ALU.add)

            def residual(dst=X, to=X, last=False):
                for hh in range(2):
                    dve.wait_ge(sig["proj_ready"], seen.up("proj_ready"))
                    ins = tt(flat(dst)[:, 512 * hh:512 * hh + 512], PS[:, 6 + hh, :],
                             flat(to)[:, 512 * hh:512 * hh + 512], ALU.add)
                    name = "resid_done" if dst is X and hh else "dve_ran"
                    ins.then_inc(sig[name], 1)
                    dve.wait_ge(sig[name], seen.up(name))
                    if not last:
                        stats(dst, range(4 * hh, 4 * hh + 4))

            def rank_gates(E, low):
                pairs = NT * E * E
                v = lambda a: a[:, 0:pairs].rearrange("p (t e j) -> p t e j", t=NT, e=E)
                gl = g_l[:, 0:NT * E].rearrange("p (t e) -> p t e", t=NT)
                other = gl.unsqueeze(2).broadcast_to([P, NT, E, E])
                own = gl.unsqueeze(3).broadcast_to([P, NT, E, E])
                lw = low.rearrange("p (e j) -> p e j", e=E).unsqueeze(1).broadcast_to([P, NT, E, E])
                tt(v(g_a), other, own, ALU.is_equal).then_inc(sig["dve_ran"], 1)
                dve.wait_ge(sig["dve_ran"], seen.up("dve_ran"))
                tt(v(g_a), v(g_a), lw, ALU.mult).then_inc(sig["dve_ran"], 1)
                dve.wait_ge(sig["dve_ran"], seen.up("dve_ran"))
                tt(v(g_b), other, own, ALU.is_gt).then_inc(sig["dve_ran"], 1)
                dve.wait_ge(sig["dve_ran"], seen.up("dve_ran"))
                tt(v(g_a), v(g_a), v(g_b), ALU.add).then_inc(sig["dve_ran"], 1)
                dve.wait_ge(sig["dve_ran"], seen.up("dve_ran"))
                rk = g_rank[:, 0:NT * E]
                dve.tensor_reduce(rk, g_a[:, 0:pairs].rearrange("p (m j) -> p m j", j=E), AX, ALU.add)\
                    .then_inc(sig["dve_ran"], 1)
                dve.wait_ge(sig["dve_ran"], seen.up("dve_ran"))

            def share(E, weights):
                rk = g_rank[:, 0:NT * E].rearrange("p (t e) -> p t e", t=NT)
                we = weights[:, 0:NT * E].rearrange("p (t e) -> p t e", t=NT)
                tt(rk, rk, we, ALU.mult).then_inc(sig["dve_ran"], 1)
                dve.wait_ge(sig["dve_ran"], seen.up("dve_ran"))
                dve.tensor_reduce(g_m, rk, AX, ALU.add).then_inc(sig["dve_ran"], 1)
                dve.wait_ge(sig["dve_ran"], seen.up("dve_ran"))
                dve.reciprocal(g_m, g_m).then_inc(sig["dve_ran"], 1)
                dve.wait_ge(sig["dve_ran"], seen.up("dve_ran"))
                tt(f_w[:, :, 0:E], rk, g_m.unsqueeze(2).broadcast_to([P, NT, E]), ALU.mult)\
                    .then_inc(sig["expert_weights"], 1)
                dve.wait_ge(sig["expert_weights"], seen.up("expert_weights"))

            def softmax_gates():
                gl = g_l[:, 0:32].rearrange("p (t e) -> p t e", t=NT)
                ge = g_e[:, 0:32].rearrange("p (t e) -> p t e", t=NT)
                dve.tensor_reduce(g_m, gl, AX, ALU.max).then_inc(sig["dve_ran"], 1)
                dve.wait_ge(sig["dve_ran"], seen.up("dve_ran"))
                tt(ge, gl, g_m.unsqueeze(2).broadcast_to([P, NT, 4]), ALU.subtract).then_inc(sig["gate_shift"], 1)
                dve.wait_ge(sig["gate_shift"], seen.up("gate_shift"))

            def ff(layer, into=ACC, middle=None):
                gated, _, weighed = LAYERS_FF[layer]
                u0, nu = FF_UNITS[layer]

                def hidden(hh):
                    for c in range(2):
                        dve.wait_ge(sig["act_half"], seen.up("act_half"))
                        tt(f_h[hh][:, c, :], PS[:, 2 * c + 1, :], f_s[c], ALU.mult).then_inc(sig["h_ready"], 1)
                        dve.wait_ge(sig["h_ready"], seen.up("h_ready"))

                def add(e, hh):
                    dve.wait_ge(sig["down_ready"], seen.up("down_ready"))
                    for t in range(4):
                        y = PS[:, 4 + hh, 128 * t:128 * t + 128]
                        a = into[:, 4 * hh + t, :]
                        if weighed:
                            ins = dve.scalar_tensor_tensor(out=a, in0=y, scalar=f_w[:, 4 * hh + t, bass.ds(e, 1)],
                                                           in1=a, op0=ALU.mult, op1=ALU.add)
                        else:
                            ins = tt(a, y, a, ALU.add)
                        name = "down_used" if t == 3 else "dve_ran"
                        ins.then_inc(sig[name], 1)
                        seen.up(name)
                        if t == 3:
                            dve.wait_ge(sig[name], seen.up(name, 0))

                def last_unit(e):
                    for hh in range(2):
                        add(e, hh)
                        stats(into, range(4 * hh, 4 * hh + 4))

                def unit(e):
                    for hh in range(2):
                        hidden(1 - hh)
                        add(e, hh)
                if gated:
                    hidden(0)
                    unit(8)
                    seen.loop(3, {"act_half": 8, "h_ready": 8, "down_ready": 4, "down_used": 4, "dve_ran": 12},
                           lambda i: (unit(i * 2), unit(i * 2 + 1)))
                    unit(6)
                    hidden(1)
                    last_unit(7)
                else:
                    per = {"down_ready": 4, "down_used": 4, "dve_ran": 12}
                    if layer == "l2f":
                        seen.loop(nu // 2 - 1, per, lambda i: [add(i, hh) for q in range(2) for hh in range(2)])
                        middle()
                        for q in range(2):
                            for hh in range(2):
                                add(nu // 2 - 1, hh)
                    elif layer == "l1f":
                        seen.loop(nu // 2 - 1, per, lambda i: [add(i * 2 + q, hh) for q in range(2)
                                                               for hh in range(2)])
                        middle()
                        add(nu - 2, 0)
                        add(nu - 2, 1)
                        last_unit(nu - 1)
                    elif layer == "l2x":
                        add(None, 0)
                        add(None, 1)
                        last_unit(None)
                    else:
                        for q in range(2):
                            for hh in range(2):
                                add(None, hh)

            def expert_biases(into):
                dve.wait_ge(sig["bias_ready"], seen.up("bias_ready"))
                tt(flat(into), flat(into), flat(ACCB), ALU.add).then_inc(sig["bias_taken"], 1)
                dve.wait_ge(sig["bias_taken"], seen.up("bias_taken"))

            dve.memset(SM[:, 500:501], 1.0).then_inc(sig["dve_ran"], 1)
            dve.wait_ge(sig["dve_ran"], seen.up("dve_ran"))

            dve.wait_ge(sig["x_landed"], 16)
            dve.wait_ge(sig["w_first"], 16)
            layernorm(X, XN, LN_EPS)

            def l0_front(s, q):
                dve.wait_ge(sig["l0s_scores"], seen.up("l0s_scores"))
                dve.tensor_reduce(l0_neg[q], PS[:, 0, 0:KEYS], AX, ALU.max, negate=True).then_inc(sig["l0s_max"], 1)
                dve.wait_ge(sig["l0s_max"], seen.up("l0s_max"))

            def l0_turned(q):
                dve.wait_ge(sig["l0s_pt"], seen.up("l0s_pt"))
                dve.tensor_copy(l0_pt[q][:, 0:2, :], PS[:, 1, 0:256].rearrange("p (c n) -> p c n", c=2))\
                    .then_inc(sig["dve_ran"], 1)
                dve.wait_ge(sig["dve_ran"], seen.up("dve_ran"))
                dve.tensor_copy(l0_pt[q][0:1, 2, :], PS[0:1, 1, 256:384]).then_inc(sig["l0s_pt_taken"], 1)
                dve.wait_ge(sig["l0s_pt_taken"], seen.up("l0s_pt_taken"))

            def l0_values(s, q):
                dve.wait_ge(sig["l0s_exp"], seen.up("l0s_exp"))
                dve.reciprocal(l0_sum[q], l0_sum[q]).then_inc(sig["dve_ran"], 1)
                dve.wait_ge(sig["dve_ran"], seen.up("dve_ran"))
                dve.wait_ge(sig["l0s_u"], seen.up("l0s_u"))
                dve.tensor_scalar(l0_u[:, bass.ds(s * P, P)], PS[:, 2, 0:P], l0_sum[q], None, ALU.mult)\
                    .then_inc(sig["l0s_u_taken"], 1)
                dve.wait_ge(sig["l0s_u_taken"], seen.up("l0s_u_taken"))

            def l0_step(s, q):
                l0_turned(q)
                l0_front(s + 1, 1 - q)
                l0_values(s, q)
            l0_front(0, 0)
            l0_step(0, 0)
            seen.loop(L0X_STEPS // 2 - 1, {"dve_ran": 4} | {k: 2 for k in "l0s_exp l0s_scores l0s_max "
                      "l0s_pt l0s_pt_taken l0s_u l0s_u_taken".split()},
                      lambda i: (l0_step(i * 2 + 1, 1), l0_step(i * 2 + 2, 0)))
            l0_turned(1)
            l0_values(L0X_STEPS - 1, 1)
            dve.wait_ge(sig["bias_ready"], seen.up("bias_ready"))
            residual()

            layernorm(X, XN, LN_EPS, stats_done=True)
            dve.wait_ge(sig["w_l0"], 16)
            dve.wait_ge(sig["rows_landed"], 16)
            lq = ar(0, 2048).rearrange("p (t n) -> p t n", t=NT)
            le = ar(2048, 2048).rearrange("p (t n) -> p t n", t=NT)
            lv = ar(4096, 1024)
            lg = ar(5120, 1024)
            for hh in range(2):
                t4 = slice(4 * hh, 4 * hh + 4)
                dve.wait_ge(sig["l0a_mm"], seen.up("l0a_mm", 4))
                dve.wait_ge(sig["l0a_act"], seen.up("l0a_act"))
                dve.tensor_scalar(lq[:, t4, :], PS[:, t4, 0:256], 0.0, None, ALU.max).then_inc(sig["dve_ran"], 1)
                dve.wait_ge(sig["dve_ran"], seen.up("dve_ran"))
                s = slice(1024 * hh, 1024 * hh + 1024)
                dve.scalar_tensor_tensor(out=ar(0, 2048)[:, s], in0=ar(2048, 2048)[:, s], scalar=1.0,
                                         in1=ar(0, 2048)[:, s], op0=ALU.min, op1=ALU.add).then_inc(sig["l0a_qk"], 1)
                dve.wait_ge(sig["l0a_qk"], seen.up("l0a_qk"))
            qk = ar(2048, 1024)
            qs = ar(3072, 1024)
            v3 = lambda a: a.rearrange("p (t n) -> p t n", t=NT)
            tt(v3(qk), lq[:, :, 0:128], lq[:, :, 128:256], ALU.mult).then_inc(sig["dve_ran"], 1)
            dve.wait_ge(sig["dve_ran"], seen.up("dve_ran"))
            r1, r2 = SM[:, 600:728], SM[:, 728:856]
            dve.tensor_reduce(r1, qk.rearrange("p (m d) -> p m d", d=DK), AX, ALU.add).then_inc(sig["dve_ran"], 1)
            dve.wait_ge(sig["dve_ran"], seen.up("dve_ran"))
            dve.wait_ge(sig["l0a_ksum"], seen.up("l0a_ksum"))
            tt(v3(qs), PSF[:, 0:1024].rearrange("p (t n) -> p t n", t=NT), lq[:, :, 0:128], ALU.mult)\
                .then_inc(sig["dve_ran"], 1)
            dve.wait_ge(sig["dve_ran"], seen.up("dve_ran"))
            dve.tensor_reduce(r2, qs.rearrange("p (m d) -> p m d", d=DK), AX, ALU.add).then_inc(sig["dve_ran"], 1)
            dve.wait_ge(sig["dve_ran"], seen.up("dve_ran"))
            dve.tensor_scalar(r2, r2, 1e-6, None, ALU.add).then_inc(sig["dve_ran"], 1)
            dve.wait_ge(sig["dve_ran"], seen.up("dve_ran"))
            dve.reciprocal(r2, r2).then_inc(sig["dve_ran"], 1)
            dve.wait_ge(sig["dve_ran"], seen.up("dve_ran"))
            tt(r1, r1, r2, ALU.mult).then_inc(sig["dve_ran"], 1)
            dve.wait_ge(sig["dve_ran"], seen.up("dve_ran"))
            tt(lv.rearrange("p (m d) -> p m d", d=DK), lv.rearrange("p (m d) -> p m d", d=DK),
                   r1.unsqueeze(2).broadcast_to([P, 128, DK]), ALU.mult).then_inc(sig["dve_ran"], 1)
            dve.wait_ge(sig["dve_ran"], seen.up("dve_ran"))
            layernorm(v3(lv), Z, 1e-5, signal=False)
            affine(Z[:, :, :], "l0a_gamma", "l0a_beta").then_inc(sig["dve_ran"], 1)
            dve.wait_ge(sig["dve_ran"], seen.up("dve_ran"))
            dve.wait_ge(sig["l0a_gate"], seen.up("l0a_gate"))
            tt(flat(Z), flat(Z), lg, ALU.mult).then_inc(sig["stream_ready"], 1)
            dve.wait_ge(sig["stream_ready"], seen.up("stream_ready"))
            residual()

            layernorm(X, XN, LN_EPS, stats_done=True)
            seen.up("gate_mm")
            dve.wait_ge(sig["gate_act"], seen.up("gate_act"))
            dve.tensor_copy(g_l, g_e).then_inc(sig["dve_ran"], 1)
            dve.wait_ge(sig["dve_ran"], seen.up("dve_ran"))
            rank_gates(8, w("rank_low8"))
            dve.tensor_scalar(g_rank, g_rank, 2.0, None, ALU.is_lt).then_inc(sig["dve_ran"], 1)
            dve.wait_ge(sig["dve_ran"], seen.up("dve_ran"))
            share(8, g_e)
            dve.tensor_scalar(f_w[:, :, 0:8], f_w[:, :, 0:8], 1.0 / 3.0, None, ALU.mult).then_inc(sig["dve_ran"], 1)
            dve.wait_ge(sig["dve_ran"], seen.up("dve_ran"))
            dve.memset(f_w[:, :, 8:9], 1.0 / 3.0).then_inc(sig["dve_ran"], 1)
            dve.wait_ge(sig["dve_ran"], seen.up("dve_ran"))
            ff("l0f", into=X)

            layernorm(X, XN, LN_EPS, stats_done=True)
            dve.wait_ge(sig["mask_landed"], seen.up("mask_landed", 32))
            dve.tensor_scalar(y_hi[:, 0:2, :], MK[:, 0:2, :], 10.0, -5.0, ALU.mult, ALU.add)\
                .then_inc(sig["dve_ran"], 1)
            dve.wait_ge(sig["dve_ran"], seen.up("dve_ran"))
            dve.tensor_scalar(y_hi[0:1, 2, :], MK[0:1, 2, :], 10.0, -5.0, ALU.mult, ALU.add)\
                .then_inc(sig["dve_ran"], 1)
            dve.wait_ge(sig["dve_ran"], seen.up("dve_ran"))

            def y_clip(b, first):
                dve.wait_ge(sig["ys_ready"], seen.up("ys_ready"))
                if not first:
                    dve.wait_ge(sig["yexp"], seen.up("yexp"))
                for c in range(3):
                    r = slice(0, P) if c < 2 else slice(0, 1)
                    ins = dve.tensor_scalar(y_C[r, c, :], PS[r, 1 + c, :], -5.0, y_hi[r, c, bass.ds(b, 1)],
                                            ALU.max, ALU.min)
                    name = "yclip" if c == 2 else "dve_ran"
                    ins.then_inc(sig[name], 1)
                    dve.wait_ge(sig[name], seen.up(name))

            def y_norm(first):
                dve.wait_ge(sig["yu_ready"], seen.up("yu_ready"))
                if not first:
                    dve.wait_ge(sig["yt_ready"], seen.up("yt_ready"))
                u = PS[:, 4:6, 0:2 * FQ].rearrange("p a (g f) -> p a g f", g=2)
                dve.reciprocal(y_r.rearrange("p (a g) -> p a g", a=2), u[:, :, :, P]).then_inc(sig["dve_ran"], 1)
                dve.wait_ge(sig["dve_ran"], seen.up("dve_ran"))
                for a in range(2):
                    ins = tt(y_U[:, 2 * a:2 * a + 2, :], u[:, a, :, 0:P],
                             y_r[:, 2 * a:2 * a + 2].unsqueeze(2).broadcast_to([P, 2, P]), ALU.mult)
                    name = "yu_taken" if a else "dve_ran"
                    ins.then_inc(sig[name], 1)
                    dve.wait_ge(sig[name], seen.up(name))

            def y_out(c):
                dve.wait_ge(sig["yo_ready"], seen.up("yo_ready"))
                dve.tensor_copy(OT[:, bass.ds(c * P, P)], PS[:, 7, 0:P]).then_inc(sig["yo_taken"], 1)
                dve.wait_ge(sig["yo_taken"], seen.up("yo_taken"))

            def y_chunk(c, first=False):
                for k in range(4):
                    y_clip(c * 4 + k, first and k == 0)
                    if not first or k >= 1:
                        y_norm(first and k == 1)
                    if k == 1 and not first:
                        y_out(c - 1)
            y_chunk(0, first=True)
            seen.loop(B // 4 - 1, {"dve_ran": 16, "yo_ready": 1, "yo_taken": 1} | {k: 4 for k in (
                "ys_ready", "yexp", "yclip", "yu_ready", "yt_ready", "yu_taken")}, lambda i: y_chunk(i + 1))
            y_norm(False)
            y_out(B // 4 - 1)
            seen.up("yexp")
            seen.up("yt_ready")
            dve.wait_ge(sig["bias_ready"], seen.up("bias_ready"))
            residual()

            def core(kind):
                rows = lambda a: a.rearrange("p (m k) -> p m k", k=32)
                for half, g0, n in [(0, g, 1) for g in range(HG)] + [(1, 0, HG)]:
                    part = c_p[half][:, 512 * g0:512 * (g0 + n)]
                    p3 = rows(part)
                    red = c_red[half][:, 16 * g0:16 * (g0 + n)]
                    dve.wait_ge(sig["c_scores"], seen.up("c_scores", n))
                    src = PSF[:, 2048 * half + 512 * g0:2048 * half + 512 * (g0 + n)]
                    dve.transpose(part, src).then_inc(sig["dve_ran"], 1)
                    dve.wait_ge(sig["dve_ran"], seen.up("dve_ran"))
                    if kind == "causal":
                        cz = w("causal").unsqueeze(1).broadcast_to([P, 16 * n, 32])
                        tt(p3, p3, cz, ALU.add).then_inc(sig["dve_ran"], 1)
                        dve.wait_ge(sig["dve_ran"], seen.up("dve_ran"))
                    dve.tensor_reduce(red, p3, AX, ALU.max).then_inc(sig["dve_ran"], 1)
                    dve.wait_ge(sig["dve_ran"], seen.up("dve_ran"))
                    ins = tt(p3, p3, red.unsqueeze(2).broadcast_to([P, 16 * n, 32]), ALU.subtract)
                    name = "c_shift" if g0 + n == HG else "dve_ran"
                    ins.then_inc(sig[name], 1)
                    dve.wait_ge(sig[name], seen.up(name))
                for half in range(2):
                    red = c_red[half]
                    dve.wait_ge(sig["c_exp"], seen.up("c_exp"))
                    dve.tensor_reduce(red, rows(c_p[half]), AX, ALU.add).then_inc(sig["dve_ran"], 1)
                    dve.wait_ge(sig["dve_ran"], seen.up("dve_ran"))
                    dve.reciprocal(red, red).then_inc(sig["c_rec"], 1)
                    dve.wait_ge(sig["c_rec"], seen.up("c_rec"))
                    for g in range(HG):
                        part = c_p[half][:, 512 * g:512 * g + 512]
                        if g >= 2:
                            dve.wait_ge(sig["c_divided"], seen.up("c_divided"))
                            if kind == "pairs":
                                o = part.rearrange("p (t h k) -> p t h k", t=4, h=4)
                                tt(o, o, c_relb.unsqueeze(2).broadcast_to([P, 4, 4, 32]), ALU.add)\
                                    .then_inc(sig["dve_ran"], 1)
                                dve.wait_ge(sig["dve_ran"], seen.up("dve_ran"))
                            dve.transpose(c_pt[half][:, 512 * g:512 * g + 512], part).then_inc(sig["c_probs"], 1)
                            dve.wait_ge(sig["c_probs"], seen.up("c_probs"))
                            continue
                        rg = red[:, 16 * g:16 * g + 16].unsqueeze(2).broadcast_to([P, 16, 32])
                        tt(rows(part), rows(part), rg, ALU.mult).then_inc(sig["dve_ran"], 1)
                        dve.wait_ge(sig["dve_ran"], seen.up("dve_ran"))
                        if kind == "pairs":
                            o = part.rearrange("p (t h k) -> p t h k", t=4, h=4)
                            tt(o, o, c_relb.unsqueeze(2).broadcast_to([P, 4, 4, 32]), ALU.add)\
                                .then_inc(sig["dve_ran"], 1)
                            dve.wait_ge(sig["dve_ran"], seen.up("dve_ran"))
                        dve.transpose(c_pt[half][:, 512 * g:512 * g + 512], part).then_inc(sig["c_probs"], 1)
                        dve.wait_ge(sig["c_probs"], seen.up("c_probs"))
                for half in range(2):
                    dve.wait_ge(sig["c_first_head"], seen.up("c_first_head"))
                    o = c_sum[half].rearrange("p (n q) -> p n q", n=16)
                    src = PSF[:, 2048 * half:2048 * half + 2048].rearrange("p (n h q) -> p n h q", n=16, h=4)
                    for h in range(1, 4):
                        ins = dve.scalar_tensor_tensor(out=o, in0=src[:, :, h, :], scalar=w("mask4")[:, h:h + 1],
                                                       in1=o, op0=ALU.mult, op1=ALU.add)
                        name = "c_heads" if h == 3 else "dve_ran"
                        ins.then_inc(sig[name], 1)
                        dve.wait_ge(sig[name], seen.up(name))

            def heads():
                dve.wait_ge(sig["qkv_taken"], seen.up("qkv_taken"))
                seen.up("qkv_taken", 2)
                m4 = w("mask4").unsqueeze(1).unsqueeze(3).broadcast_to([P, 16, 4, 32])
                for half in range(2):
                    q4 = c_q[:, 512 * half:512 * half + 512].rearrange("p (n q) -> p n q", n=16)\
                        .unsqueeze(2).broadcast_to([P, 16, 4, 32])
                    tt(c_qb[:, 2048 * half:2048 * half + 2048].rearrange("p (n h q) -> p n h q", n=16, h=4),
                       q4, m4, ALU.mult).then_inc(sig["c_in"], 1)
                    dve.wait_ge(sig["c_in"], seen.up("c_in"))

            layernorm(X, XN, LN_EPS, stats_done=True)
            dve.wait_ge(sig["w_l1"], 16)
            heads()
            core("causal")
            residual()

            layernorm(X, XN, LN_EPS, stats_done=True)
            dve.wait_ge(sig["gate_mm"], seen.up("gate_mm", 2))
            ps = PS[:, 7, 0:NT]
            small = row("small")
            z = lambda j: g_z[:, j, :]
            dve.tensor_scalar(z(0), ps, small[:, SMALL_DPB2:SMALL_DPB2 + 1], None, ALU.add)\
                .then_inc(sig["dve_ran"], 1)
            dve.wait_ge(sig["dve_ran"], seen.up("dve_ran"))
            dve.tensor_scalar(z(1), z(0), -1.0, None, ALU.mult).then_inc(sig["dve_ran"], 1)
            dve.wait_ge(sig["dve_ran"], seen.up("dve_ran"))
            tt(z(1), z(0), z(1), ALU.max).then_inc(sig["gate_entropy"], 1)
            dve.wait_ge(sig["gate_entropy"], seen.up("gate_entropy"))
            dve.tensor_scalar(z(0), z(0), 0.0, None, ALU.max).then_inc(sig["dve_ran"], 1)
            dve.wait_ge(sig["dve_ran"], seen.up("dve_ran"))
            dve.wait_ge(sig["gate_act"], seen.up("gate_act", 2))
            tt(z(0), z(0), z(3), ALU.add).then_inc(sig["dve_ran"], 1)
            dve.wait_ge(sig["dve_ran"], seen.up("dve_ran"))
            dve.tensor_scalar(z(0), z(0), 0.5, 1.0 / 1.5, ALU.subtract, ALU.mult).then_inc(sig["dve_ran"], 1)
            dve.wait_ge(sig["dve_ran"], seen.up("dve_ran"))
            dve.tensor_scalar(z(0), z(0), 0.0, 1.0, ALU.max, ALU.min).then_inc(sig["dve_ran"], 1)
            dve.wait_ge(sig["dve_ran"], seen.up("dve_ran"))
            dve.tensor_scalar(z(0), z(0), 3.0, 1.0, ALU.mult, ALU.add).then_inc(sig["dve_ran"], 1)
            dve.wait_ge(sig["dve_ran"], seen.up("dve_ran"))
            dve.tensor_scalar(z(1), z(0), 1.5, 1.0, ALU.is_ge, ALU.add).then_inc(sig["dve_ran"], 1)
            dve.wait_ge(sig["dve_ran"], seen.up("dve_ran"))
            dve.tensor_scalar(z(4), z(0), 2.5, None, ALU.is_gt).then_inc(sig["dve_ran"], 1)
            dve.wait_ge(sig["dve_ran"], seen.up("dve_ran"))
            tt(z(1), z(1), z(4), ALU.add).then_inc(sig["dve_ran"], 1)
            dve.wait_ge(sig["dve_ran"], seen.up("dve_ran"))
            dve.tensor_scalar(z(4), z(0), 3.5, None, ALU.is_ge).then_inc(sig["dve_ran"], 1)
            dve.wait_ge(sig["dve_ran"], seen.up("dve_ran"))
            tt(z(1), z(1), z(4), ALU.add).then_inc(sig["dve_ran"], 1)
            dve.wait_ge(sig["dve_ran"], seen.up("dve_ran"))
            gb = small[:, SMALL_L1GATE:SMALL_L1GATE + 4].unsqueeze(1).broadcast_to([P, NT, 4])
            tt(g_l[:, 0:32].rearrange("p (t e) -> p t e", t=NT),
                   PS[:, 6, 0:32].rearrange("p (t e) -> p t e", t=NT), gb, ALU.add).then_inc(sig["dve_ran"], 1)
            dve.wait_ge(sig["dve_ran"], seen.up("dve_ran"))
            softmax_gates()
            rank_gates(4, w("rank_low4"))
            rk = g_rank[:, 0:32].rearrange("p (t e) -> p t e", t=NT)
            tt(rk, rk, z(1).unsqueeze(2).broadcast_to([P, NT, 4]), ALU.is_lt).then_inc(sig["dve_ran"], 1)
            dve.wait_ge(sig["dve_ran"], seen.up("dve_ran"))
            dve.wait_ge(sig["gate_act"], seen.up("gate_act"))
            share(4, g_e)
            ff("l1f", into=X, middle=lambda: expert_biases(X))

            def take_queries(bq):
                dve.wait_ge(sig["xq_mm"], seen.up("xq_mm"))
                scale = float(DK) ** -0.5
                if bq:
                    ins = dve.tensor_scalar(x_q, PSF[:, 1024:2048], col(bq), scale, ALU.add, ALU.mult)
                else:
                    ins = dve.tensor_scalar(x_q, PSF[:, 1024:2048], scale, None, ALU.mult)
                ins.then_inc(sig["xq_ready"], 1)
                dve.wait_ge(sig["xq_ready"], seen.up("xq_ready"))

            def cross(biased, bv):
                def x_vl_take(k):
                    dve.wait_ge(sig["xv_taken"], seen.up("xv_taken"))
                    tt(x_vl[k][0:4, :], PS[0:4, 1, 256:384], w("mask_last")[0:4, :], ALU.mult)\
                        .then_inc(sig["xvl_taken"], 1)
                    dve.wait_ge(sig["xvl_taken"], seen.up("xvl_taken"))

                def x_add(k, first):
                    dve.wait_ge(sig[f"ctx_landed{k}"], seen.up(f"ctx_landed{k}", 32))
                    if not first:
                        dve.wait_ge(sig["xexp"], seen.up("xexp", HG))
                    tt(x_s, PS[:, 2:6, 0:KEYS], c_F[k], ALU.add).then_inc(sig["xs_added"], 1)
                    dve.wait_ge(sig["xs_added"], seen.up("xs_added"))

                def x_max(q):
                    src = x_s if biased else PS[:, 2:6, 0:KEYS]
                    dve.tensor_reduce(x_neg[q], src, AX, ALU.max, negate=True).then_inc(sig["xmax"], 1)
                    dve.wait_ge(sig["xmax"], seen.up("xmax"))

                def x_turned():
                    dve.wait_ge(sig["xpt_ready"], seen.up("xpt_ready"))
                    dve.tensor_copy(x_pt[:, 1, :], PS[:, 7, :]).then_inc(sig["xpt_d"], 1)
                    dve.wait_ge(sig["xpt_d"], seen.up("xpt_d"))

                def x_tail(b):
                    dve.wait_ge(sig["xu_ready"], seen.up("xu_ready"))
                    x4 = x_t.rearrange("p (h q) -> p h q", h=4)
                    m4 = w("mask4").unsqueeze(2).broadcast_to([P, 4, 32])
                    tt(x4, PS[:, 6, 0:128].rearrange("p (h q) -> p h q", h=4), m4, ALU.mult)\
                        .then_inc(sig["dve_ran"], 1)
                    dve.wait_ge(sig["dve_ran"], seen.up("dve_ran"))
                    dve.reciprocal(x_rec, PS[:, 7, 0:32]).then_inc(sig["dve_ran"], 1)
                    dve.wait_ge(sig["dve_ran"], seen.up("dve_ran"))
                    tt(x4[:, 0:2, :], x4[:, 0:2, :], x4[:, 2:4, :], ALU.add).then_inc(sig["dve_ran"], 1)
                    dve.wait_ge(sig["dve_ran"], seen.up("dve_ran"))
                    tt(x4[:, 0, :], x4[:, 0, :], x4[:, 1, :], ALU.add).then_inc(sig["dve_ran"], 1)
                    dve.wait_ge(sig["dve_ran"], seen.up("dve_ran"))
                    tt(OT[:, bass.ds(b * 32, 32)], x4[:, 0, :], x_rec, ALU.mult).then_inc(sig["x_out"], 1)
                    dve.wait_ge(sig["x_out"], seen.up("x_out"))

                def x_four(c, first=False, last=False):
                    for k in range(4):
                        dve.wait_ge(sig["xs_ready"], seen.up("xs_ready"))
                        if biased:
                            x_add(k, first and k == 0)
                        else:
                            x_max(k % 2)
                        if not (first and k == 0) and not biased:
                            x_turned()
                        if biased:
                            x_max(k % 2)
                        if not (last and k == 3):
                            x_vl_take((k + 1) % 4)
                        if not (first and k == 0):
                            x_tail(c * 4 + (k - 1))

                x_vl_take(0)
                x_four(0, first=True)
                per = {"dve_ran": 16} | {k: 4 for k in "xs_ready xmax xv_taken xvl_taken xu_ready "
                                                       "x_out".split()}
                if biased:
                    per |= {"xexp": 16, "xs_added": 4} | {f"ctx_landed{k}": 32 for k in range(4)}
                else:
                    per |= {"xpt_ready": 4, "xpt_d": 4}
                seen.loop(B // 4 - 2, per, lambda i: x_four(i + 1))
                x_four(B // 4 - 1, last=True)
                if biased:
                    seen.up("xpt_ready", B)
                else:
                    x_turned()
                x_tail(B - 1)
                seen.up("xexp", HG if biased else HG * B)
                if bv:
                    dve.tensor_scalar(OT[:, :], OT[:, :], col(bv), None, ALU.add).then_inc(sig["x_out"], 1)
                    dve.wait_ge(sig["x_out"], seen.up("x_out"))

            layernorm(X, XN, LN_EPS, stats_done=True)
            dve.wait_ge(sig["w_l2"], 16)
            take_queries(None)
            for k in range(4):
                seen.up(f"ctx_landed{k}", (16 * (L0X_STEPS // 2) if k < 2 else 0) + 48 * (B // 4))
            cross(True, None)
            residual(Y, XN)
            layernorm(Y, Z, 1e-5, signal=False, stats_done=True)
            affine(Z[:, :, :], "l2x_g1", "l2x_be1").then_inc(sig["stream_ready"], 1)
            dve.wait_ge(sig["stream_ready"], seen.up("stream_ready"))
            tt(ACC[:, :, :], Y[:, :, :], rows_t("l2x_b2"), ALU.add).then_inc(sig["dve_ran"], 1)
            dve.wait_ge(sig["dve_ran"], seen.up("dve_ran"))
            ff("l2x")
            layernorm(ACC, Z, 1e-5, signal=False, stats_done=True)
            tt(Z[:, :, :], Z[:, :, :], rows_t("l2x_g2"), ALU.mult).then_inc(sig["dve_ran"], 1)
            dve.wait_ge(sig["dve_ran"], seen.up("dve_ran"))
            dve.wait_ge(sig["bias_ready"], seen.up("bias_ready"))
            tt(flat(X), flat(X), flat(Z), ALU.add).then_inc(sig["resid_done"], 1)
            dve.wait_ge(sig["resid_done"], seen.up("resid_done"))

            layernorm(X, XN, LN_EPS)
            dve.wait_ge(sig["relb_landed"], 64)
            for j in range(4):
                r = slice(32 * j, 32 * j + 32)
                dve.tensor_copy(c_rel2[r].rearrange("p k m -> p m k"),
                                    ACCB[r, 0:4, :].rearrange("p t n -> p (t n)")
                                    .rearrange("p (k m j) -> p j m k", k=32, m=4)[:, j]).then_inc(sig["dve_ran"], 1)
                dve.wait_ge(sig["dve_ran"], seen.up("dve_ran"))
            oh = w("onehot").rearrange("p (k u) -> p k u", k=32)
            for m4i in range(4):
                rb = c_rel2[:, :, m4i].unsqueeze(1).broadcast_to([P, 32, 32])
                tt(c_onehot.rearrange("p (k u) -> p k u", k=32), oh, rb, ALU.mult).then_inc(sig["dve_ran"], 1)
                dve.wait_ge(sig["dve_ran"], seen.up("dve_ran"))
                dve.tensor_reduce(c_relb[:, m4i, :], c_onehot.rearrange("p (k u) -> p k u", k=32),
                                      AX, ALU.add).then_inc(sig["dve_ran"], 1)
                dve.wait_ge(sig["dve_ran"], seen.up("dve_ran"))
            heads()
            core("pairs")
            tt(Y[:, :, :], XN[:, :, :], rows_t("l2a_bo"), ALU.add).then_inc(sig["dve_ran"], 1)
            dve.wait_ge(sig["dve_ran"], seen.up("dve_ran"))
            residual(Y, Y)
            layernorm(Y, Z, 0.0, stats_done=True)
            tt(ACC[:, :, :], Z[:, :, :], rows_t("l2a_b2"), ALU.add).then_inc(sig["dve_ran"], 1)
            dve.wait_ge(sig["dve_ran"], seen.up("dve_ran"))
            residual(ACC, ACC)
            layernorm(ACC, Y, 0.0, signal=False, stats_done=True)
            tt(flat(X), flat(X), flat(Y), ALU.add).then_inc(sig["resid_done"], 1)
            dve.wait_ge(sig["resid_done"], seen.up("resid_done"))

            layernorm(X, XN, LN_EPS)
            dve.tensor_copy(flat(ACC), flat(XN)).then_inc(sig["dve_ran"], 1)
            dve.wait_ge(sig["dve_ran"], seen.up("dve_ran"))
            for r in range(4):
                dve.wait_ge(sig["gate_mm"], seen.up("gate_mm"))
                gb = small[:, SMALL_L2GATE + 4 * r:SMALL_L2GATE + 4 * r + 4].unsqueeze(1).broadcast_to([P, NT, 4])
                tt(g_l[:, 0:32].rearrange("p (t e) -> p t e", t=NT),
                       PS[:, 6, 0:32].rearrange("p (t e) -> p t e", t=NT), gb, ALU.add).then_inc(sig["dve_ran"], 1)
                dve.wait_ge(sig["dve_ran"], seen.up("dve_ran"))
                softmax_gates()
                rank_gates(4, w("rank_low4"))
                dve.tensor_scalar(g_rank[:, 0:32], g_rank[:, 0:32], 2.0, None, ALU.is_lt).then_inc(sig["dve_ran"], 1)
                dve.wait_ge(sig["dve_ran"], seen.up("dve_ran"))
                dve.wait_ge(sig["gate_act"], seen.up("gate_act"))
                share(4, g_e)
                ff("l2f", middle=lambda: expert_biases(ACC))
            tt(flat(X), flat(X), flat(ACC), ALU.add).then_inc(sig["resid_done"], 1)
            dve.wait_ge(sig["resid_done"], seen.up("resid_done"))

            layernorm(X, XN, LN_EPS)
            dve.wait_ge(sig["w_l3"], 16)
            take_queries("l3x_bq")
            cross(False, "l3x_bv")
            dve.wait_ge(sig["bias_ready"], seen.up("bias_ready"))
            residual()

            layernorm(X, XN, LN_EPS, stats_done=True)
            layernorm(XN, Z, 1e-5, signal=False)
            affine(Z[:, :, :], "l3a_lng", "l3a_lnb").then_inc(sig["dve_ran"], 1)
            dve.wait_ge(sig["dve_ran"], seen.up("dve_ran"))
            heads()
            core("plain")
            dve.wait_ge(sig["bias_ready"], seen.up("bias_ready"))
            tt(flat(X), flat(X), flat(Z), ALU.add).then_inc(sig["dve_ran"], 1)
            dve.wait_ge(sig["dve_ran"], seen.up("dve_ran"))
            residual()

            layernorm(X, XN, LN_EPS, stats_done=True)
            dve.memset(flat(ACC), 0.0).then_inc(sig["dve_ran"], 1)
            dve.wait_ge(sig["dve_ran"], seen.up("dve_ran"))
            ff("l3f")
            dve.wait_ge(sig["bias_ready"], seen.up("bias_ready"))
            residual(last=True)

        @block.gpsimd
        def _(pool):
            seen = Tally(pool)
            for q in range(2):
                pool.memset(y_P_last[q], 0.0).then_inc(sig["pool_ran"], 1)
            pool.memset(ar(17408, 4 * FQ), 0.0).then_inc(sig["pool_ran"], 1)
            pool.wait_ge(sig["pool_ran"], seen.up("pool_ran", 3))
            pool.sem_inc(sig["y_padded"], 1)
            for g in ("l0", "l1", "l2", "l3"):
                a, cols = SPANS["group_" + g]
                if g == "l1":
                    pool.dma_start(RB[:, :, :], wrows.rearrange("a r n -> (a) r n").broadcast_to([P, len(ROWS), P])
                                   ).then_inc(sig["rows_landed"], 16)
                    pool.dma_start(MK[:, 0:2, :], mask[0:2 * P, :].rearrange("(c p) b -> p c b", c=2))\
                        .then_inc(sig["mask_landed"], 16)
                    pool.dma_start(MK[0:1, 2, :], mask[2 * P:KEYS, :]).then_inc(sig["mask_landed"], 16)
                pool.dma_start(W[:, a:a + cols], wpack[:, a:a + cols]).then_inc(sig["w_" + g], 16)
            pool.wait_ge(sig["w_l0"], 16)
            pool.wait_ge(sig["rows_landed"], 16)
            ready = sig["rows_landed"]

            def bias(name):
                pool.tensor_tensor(X[:, :, :], X[:, :, :], rows_t(name), ALU.add).then_inc(sig["bias_ready"], 1)
                pool.wait_ge(sig["bias_ready"], seen.up("bias_ready"))

            pool.wait_ge(sig["norm_ready"], seen.up("norm_ready", NT))
            pool.wait_ge(sig["l0s_q_ready"], seen.up("l0s_q_ready"))

            def stage(s, q):
                if not (isinstance(s, int) and s < 2):
                    pool.wait_ge(sig["l0s_scores"], seen.up("l0s_scores"))
                pool.wait_ge(ready, 16)
                pool.tensor_copy(l0_qs[q], l0_qp[:, bass.ds(s * P, P)]).then_inc(sig["l0s_staged"], 1)
                pool.wait_ge(sig["l0s_staged"], seen.up("l0s_staged"))
            seen.paired(L0X_STEPS, {"l0s_scores": 2, "l0s_staged": 2}, stage)
            bias("l0x_bo")
            pool.wait_ge(sig["norm_ready"], seen.up("norm_ready", NT))
            pool.dma_start(ar(8192, 4096), l1x_w).then_inc(sig["l1x_w_landed"], 16)
            seen.up("norm_ready", NT)
            seen.up("expert_weights")

            pool.wait_ge(sig["norm_ready"], seen.up("norm_ready", NT))
            bias("l1x_bo")
            seen.up("norm_ready", NT)

            def divide():
                for half in range(2):
                    pool.wait_ge(sig["c_rec"], seen.up("c_rec"))
                    for g in (2, 3):
                        part = c_p[half][:, 512 * g:512 * g + 512].rearrange("p (m k) -> p m k", k=32)
                        rg = c_red[half][:, 16 * g:16 * g + 16].unsqueeze(2).broadcast_to([P, 16, 32])
                        pool.tensor_tensor(part, part, rg, ALU.mult).then_inc(sig["c_divided"], 1)
                        pool.wait_ge(sig["c_divided"], seen.up("c_divided"))
            divide()

            def expert_bias(names):
                pool.wait_ge(sig["expert_weights"], seen.up("expert_weights"))
                for e, name in enumerate(names):
                    we = f_w[:, :, e:e + 1].broadcast_to([P, NT, P])
                    dst = ACCB if e == 0 else Z
                    pool.tensor_tensor(dst[:, :, :], rows_t(name), we, ALU.mult).then_inc(sig["pool_ran"], 1)
                    pool.wait_ge(sig["pool_ran"], seen.up("pool_ran"))
                    if e:
                        ins = pool.tensor_tensor(ACCB[:, :, :], ACCB[:, :, :], Z[:, :, :], ALU.add)
                        name = "bias_ready" if e == 3 else "pool_ran"
                        ins.then_inc(sig[name], 1)
                        pool.wait_ge(sig[name], seen.up(name))

            pool.wait_ge(sig["norm_ready"], seen.up("norm_ready", NT))
            expert_bias([f"l1f_b2_{e}" for e in range(4)])

            def spread():
                pool.wait_ge(sig["xq_ready"], seen.up("xq_ready"))
                m16 = w("mask16").unsqueeze(2).broadcast_to([P, H, 32])

                def x_queries(b, q, first):
                    if not first:
                        pool.wait_ge(sig["xs_ready"], seen.up("xs_ready"))
                    qv = x_q[:, bass.ds(b * 32, 32)].unsqueeze(1).broadcast_to([P, H, 32])
                    pool.tensor_tensor(x_qb[q].rearrange("p (h q) -> p h q", h=H), qv, m16, ALU.mult)\
                        .then_inc(sig["xqb"], 1)
                    pool.wait_ge(sig["xqb"], seen.up("xqb"))

                def x_sums(q):
                    pool.wait_ge(sig["xexp"], seen.up("xexp", HG))
                    pool.tensor_tensor(x_r[q].rearrange("p (g f) -> p g f", g=HG),
                                       w("head_mask").rearrange("p (g f) -> p g f", g=HG),
                                       x_sum[q].unsqueeze(2).broadcast_to([P, HG, 32]), ALU.mult)\
                        .then_inc(sig["xsum_spread"], 1)
                    pool.wait_ge(sig["xsum_spread"], seen.up("xsum_spread"))
                x_queries(0, 0, True)
                x_queries(1, 1, True)
                x_sums(0)

                def body(i):
                    for k in range(2):
                        x_queries(i * 2 + (2 + k), k, False)
                        x_sums(1 - k)
                seen.loop(B // 2 - 1, {"xexp": 2 * HG} | {k: 2 for k in "xs_ready xqb xsum_spread".split()}, body)
                x_sums(1)
                seen.up("xs_ready", 2)

            pool.wait_ge(sig["norm_ready"], seen.up("norm_ready", NT))
            bias("l2x_be2")
            pool.wait_ge(sig["bias_taken"], 1)
            for j in range(4):
                pool.dma_start(ACCB[32 * j:32 * j + 32, 0:4, :].rearrange("p t n -> p (t n)"),
                               relb.broadcast_to([32, 512])).then_inc(sig["relb_landed"], 16)
            spread()
            divide()
            pool.wait_ge(sig["c_out"], seen.up("c_out", 4))
            for u in range(11, H):
                pool.dma_start(*to_tokens(u)).then_inc(sig["pair_out_pool"], 16)
            seen.up("norm_ready", 2 * NT)

            pool.wait_ge(sig["norm_ready"], seen.up("norm_ready", NT))
            for r in range(4):
                expert_bias([f"l2f_b2_{e}" for e in range(4)])

            pool.wait_ge(sig["norm_ready"], seen.up("norm_ready", NT))
            bias("l3x_bo")
            spread()
            pool.wait_ge(sig["norm_ready"], seen.up("norm_ready", NT))
            bias("l3a_bp")
            divide()
            pool.wait_ge(sig["norm_ready"], seen.up("norm_ready", NT))
            bias("l3f_b2")

    return nc



def kernel(**inputs):
    import numpy as np
    import concourse.bacc as bacc
    from concourse import mybir as mb
    from concourse.bass_utils import run_bass_kernel_spmd

    a = {k: np.asarray(v) for k, v in inputs.items()}
    f = np.float32
    wp = np.zeros((P, WTOTAL), f)

    def put(name, m):
        at, n = SPANS[name]
        m = np.asarray(m)
        wp[:m.shape[0], at:at + m.shape[1]] = m

    put("ident", np.eye(P, dtype=f))
    put("l0x_q", a["L0_xattn_Wq"].T)
    put("l0x_k", a["L0_xattn_Wk"])
    put("l0x_v", a["L0_xattn_Wv"].T)
    put("l0x_o", a["L0_xattn_Wo"].T)
    p = np.arange(P)
    put("blockones", (p[:, None] // 32 == p[None, :] // 32).astype(f))
    put("l0a_qkvg", np.concatenate([a["L0_attn_W" + c] for c in "qkvg"], 1))
    put("l0a_o", a["L0_attn_Wo"])
    put("l0f_gate", a["L0_ffn_Wg"])
    for E in (8, 4):
        e = np.arange(E)
        put(f"rank_low{E}", np.broadcast_to((e[None, :] < e[:, None]).astype(f).reshape(1, -1), (P, E * E)))
    put("mask4", ((p[:, None] % 32) // 8 == np.arange(4)[None, :]).astype(f))
    put("mask16", (p[:, None] // 8 == np.arange(16)[None, :]).astype(f))
    put("mask_last", (np.arange(4)[:, None] == p[None, :] // 32).astype(f))
    put("l1a_q", a["L1_attn_wq"].T)
    rep4 = np.array([8 * g + d for g in range(4) for m in range(4) for d in range(8)])
    put("l1a_k", a["L1_attn_wk"][rep4].T)
    put("l1a_v", a["L1_attn_wv"][rep4].T)
    put("l1a_o", a["L1_attn_wo"].T)
    put("causal", np.where(np.arange(32)[None, :] > (p[:, None] % 32), f(-1e30), f(0)))
    put("l1f_gate", a["L1_ffn_gate_w"])
    put("l1f_dp1", a["L1_ffn_dp_w1"])
    put("l1f_dp2", a["L1_ffn_dp_w2"])
    for c in "qkvo":
        put("l2x_" + c, a["L2_xattn_W" + c].T)
        put("l3x_" + c, a["L3_xattn_W" + c].T)
    by_feature = np.arange(P).reshape(16, 8).T.reshape(-1)
    for c in "qkv":
        put("l2a_" + c, a["L2_attn_W" + c].T[:, by_feature])
    put("l2a_o", a["L2_attn_Wo"].T[by_feature])
    put("l2a_w1", a["L2_attn_W1"].T)
    put("l2a_w2", a["L2_attn_W2"].T)
    put("head_mask", (p[:, None] // 32 == (p[None, :] % 32) // 8).astype(f))
    put("fold", (p[:, None] % 32 == np.arange(32)[None, :]).astype(f))
    put("onehot", np.tile(one_hot_buckets().reshape(32, 1024), (4, 1)))
    put("l2f_gate", np.concatenate(list(a["L2_ffn_Wg"]), 1))
    for i, c in enumerate("qkv"):
        put("l3a_" + c, a["L3_attn_W_qkv"][128 * i:128 * i + 128].T)
    put("l3a_o", a["L3_attn_W_proj"].T)
    put("l3f_u1", a["L3_ffn_U1"])
    put("l3f_v2", a["L3_ffn_V2"])

    def put_col(name, v):
        at = SPANS["cols"][0] + COLS[name]
        v = np.asarray(v)
        wp[:v.shape[0], at:at + v.shape[1]] = v
    put_col("l0x_bq", a["L0_xattn_bq"][:, None])
    put_col("l0x_bv", a["L0_xattn_bv"][:, None])
    put_col("l3x_bq", a["L3_xattn_bq"][:, None])
    put_col("l3x_bk", a["L3_xattn_bk"][:, None])
    put_col("l3x_bv", a["L3_xattn_bv"][:, None])
    put_col("l2a_b1", a["L2_attn_b1"][:, None])
    put_col("l1f_dpb1", a["L1_ffn_dp_b1"][:, None])
    for c in "qkv":
        put_col("l2a_b" + c, a["L2_attn_b" + c][by_feature][:, None])

    rows = np.zeros((1, len(ROWS), P), f)
    src = {"l0x_bo": "L0_xattn_bo", "l0a_gamma": "L0_attn_gamma", "l0a_beta": "L0_attn_beta",
           "l1x_bo": "L1_xattn_bo", "l2x_b2": "L2_xattn_b2", "l2x_g1": "L2_xattn_g1", "l2x_be1": "L2_xattn_be1",
           "l2x_g2": "L2_xattn_g2", "l2x_be2": "L2_xattn_be2", "l2a_bo": "L2_attn_bo", "l2a_b2": "L2_attn_b2",
           "l3x_bo": "L3_xattn_bo", "l3a_bp": "L3_attn_b_proj",
           "l3a_lng": "L3_attn_ln_gamma", "l3a_lnb": "L3_attn_ln_beta", "l3f_b2": "L3_ffn_b2"}
    for k, v in src.items():
        rows[0, ROWS.index(k)] = a[v]
    for e in range(4):
        rows[0, ROWS.index(f"l1f_b2_{e}")] = a["L1_ffn_eb2"][e]
        rows[0, ROWS.index(f"l2f_b2_{e}")] = a["L2_ffn_b2"][e]
    small = rows[0, ROWS.index("small")]
    small[SMALL_L1GATE:SMALL_L1GATE + 4] = a["L1_ffn_gate_b"]
    small[SMALL_DPB2:SMALL_DPB2 + 1] = a["L1_ffn_dp_b2"]
    small[SMALL_L2GATE:SMALL_L2GATE + 16] = a["L2_ffn_bg"].reshape(-1)

    def two(m):
        return m.reshape(8, 2, 64, P).transpose(1, 2, 0, 3).reshape(P, 1, 8, P)
    wkv = a["L1_xattn_Wkv"]
    l1x_w = np.concatenate([two(a["L1_xattn_Wq"].T), two(wkv[:, :1024].T), two(wkv[:, 1024:].T),
                            two(a["L1_xattn_Wo"])], 1).reshape(P, 4096)

    units = np.zeros((N_UNITS, P, WCOLS), f)

    def unit(i, w1, w3, b1, w2):
        units[i, :w1.shape[0], 0:UNIT] = w1
        if w3 is not None:
            units[i, :, UNIT:2 * UNIT] = w3
        if b1 is not None:
            units[i, :, 3 * UNIT:] = b1.reshape(2, P).T
        for c in range(2):
            units[i, :, 2 * UNIT + P * c:2 * UNIT + P * c + w2.shape[1]] = w2[P * c:P * c + P]
    u0 = FF_UNITS["l0f"][0]
    unit(u0, a["L0_ffn_Ws1"], a["L0_ffn_Ws3"], None, a["L0_ffn_Ws2"])
    for e in range(8):
        unit(u0 + 1 + e, a["L0_ffn_We1"][e], a["L0_ffn_We3"][e], None, a["L0_ffn_We2"][e])
    for e in range(4):
        unit(FF_UNITS["l1f"][0] + e, a["L1_ffn_ew1"][e], None, a["L1_ffn_eb1"][e], a["L1_ffn_ew2"][e])
    for k in range(2):
        s = slice(UNIT * k, UNIT * k + UNIT)
        unit(FF_UNITS["l2x"][0] + k, a["L2_xattn_W1"].T[:, s], None, a["L2_xattn_b1"][s], a["L2_xattn_W2"].T[s])
        unit(FF_UNITS["l3f"][0] + k, a["L3_ffn_V1"][:, s], None, a["L3_ffn_b1"][s], a["L3_ffn_U2"][s])
        for e in range(4):
            unit(FF_UNITS["l2f"][0] + 2 * e + k, a["L2_ffn_W1"][e][:, s], None, a["L2_ffn_b1"][e][s],
                 a["L2_ffn_W2"][e][s])

    ctxv = a["ctx_1024"]
    ctxT = np.zeros((B, P, KPAD), f)
    ctxT[:, :, :KEYS] = ctxv.transpose(0, 2, 1)
    ctxT[:, :, KEYS:] = ctxv[:, 256, :, None]
    ctxN = np.ones((B, KEYS, FQ), f)
    ctxN[:, :, :P] = ctxv
    mask_words = np.zeros((KEYS, B, 4), np.uint8)
    mask_words[:, :, 0] = a["mask_BxS2_bk1"].T
    arrays = {
        "ctxT": ctxT, "ctxN": ctxN,
        "fside": np.ascontiguousarray(a["fside_Bx16xSxS2_0"]).reshape(B, H * S, KEYS),
        "mask": mask_words.view(np.int32).reshape(KEYS, B),
        "wpack": wp, "wrows": rows, "l1x_w": l1x_w, "units": units,
        "relb": np.ascontiguousarray(a["L2_attn_rel_bias"]).reshape(1, 512),
        "x": np.ascontiguousarray(a["x"]).reshape(TOK, P),
    }
    nc = bacc.Bacc("TRN2", target_bir_lowering=False, num_devices=1)
    ap = {n: nc.dram_tensor("in_" + n, v.shape, mb.dt.from_np(v.dtype), kind="ExternalInput").ap()
          for n, v in arrays.items()}
    out = nc.dram_tensor("out_x", (TOK, P), F32, kind="ExternalOutput").ap()
    tiles = lambda t: t.rearrange("(t p) d -> p t d", p=P)
    perceiver(nc, ap["ctxT"], ap["ctxN"], ap["fside"], ap["mask"], ap["wpack"], ap["wrows"], ap["l1x_w"],
              ap["units"], ap["relb"], tiles(ap["x"]), tiles(out))
    r = run_bass_kernel_spmd(nc, [{"in_" + n: v for n, v in arrays.items()}], core_ids=[0])
    return r.results[0]["out_x"].reshape(B, S, P)


def one_hot_buckets():
    import math

    import numpy as np
    rel = np.arange(32)[:, None] - np.arange(32)[None, :]
    n = -rel
    ret = (n < 0).astype(np.int32) * 16
    n = np.abs(n)
    large = 8 + (np.log(np.maximum(n, 1).astype(np.float32) / 8) / math.log(128 / 8) * 8).astype(np.int32)
    bucket = ret + np.where(n < 8, n, np.minimum(large, 15))
    return (bucket[:, :, None] == np.arange(32)).astype(np.float32)
```
